# Optimizing a Trainium2 kernel written in Bass

```python
import numpy as np
import jax
import jax.numpy as jnp

def _softmax(x, axis=-1):
    return jax.nn.softmax(x, axis=axis)

def _gelu(x):
    return jax.nn.gelu(x, approximate=True)

def _silu(x):
    return jax.nn.silu(x)

def _sigmoid(x):
    return jax.nn.sigmoid(x)

def _layernorm(x, axis=-1, eps=1e-05):
    m = jnp.mean(x, axis=axis, keepdims=True)
    v = jnp.var(x, axis=axis, keepdims=True)
    return (x - m) / jnp.sqrt(v + eps)

def _scatter_add(tgt, idx, src, axis=0):
    return tgt.at[idx].add(src)

def _segment_sum(src, seg, n):
    return jax.ops.segment_sum(src, seg, n)
kernel_name = 'mk_adaln_d1_jaxref_r4_47b42b'

def setup_inputs(seed: int=0):
    np.random.seed(seed)
    _w = jnp.asarray

    def _L0_attn_setup():
        import jax, jax.numpy as jnp
        import numpy as np
        D_MODEL = 512
        D_INNER = 1024
        D_STATE = 64
        N_QK_HEADS = 8
        N_V_HEADS = 64
        CHUNK = 128
        KSIZE = 4
        CONV_DIM = D_INNER + 2 * N_QK_HEADS * D_STATE
        PROJ_DIM = CONV_DIM + D_INNER + N_V_HEADS

        def segsum(x):
            T = x.shape[-1]
            xe = jnp.broadcast_to(x[..., None], x.shape + (T,))
            strict_lower = jnp.tril(jnp.ones((T, T), dtype=bool), -1)
            xe = jnp.where(strict_lower, xe, 0.0)
            s = jnp.cumsum(xe, axis=-2)
            lower = jnp.tril(jnp.ones((T, T), dtype=bool), 0)
            return jnp.where(lower, s, -jnp.inf)

        def ssd_chunk_scan(X, dA, Bm, Cm, chunk):
            b, l, h, p = X.shape
            g = Bm.shape[2]
            rep = h // g
            Bm = jnp.repeat(Bm, rep, axis=2)
            Cm = jnp.repeat(Cm, rep, axis=2)
            c = l // chunk
            X = X.reshape(b, c, chunk, h, p)
            Bm = Bm.reshape(b, c, chunk, h, -1)
            Cm = Cm.reshape(b, c, chunk, h, -1)
            A = jnp.transpose(dA.reshape(b, c, chunk, h), (0, 3, 1, 2))
            A_cum = jnp.cumsum(A, axis=-1)
            Lm = jnp.exp(segsum(A))
            Y_diag = jnp.einsum('bcshn,bczhn,bhcsz,bczhp->bcshp', Cm, Bm, Lm, X)
            decay_states = jnp.exp(A_cum[..., -1:] - A_cum)
            states = jnp.einsum('bcshn,bhcs,bcshp->bchpn', Bm, decay_states, X)
            states = jnp.concatenate([jnp.zeros_like(states[:, :1]), states], axis=1)
            chunk_sums = jnp.pad(A_cum[..., -1], ((0, 0), (0, 0), (1, 0)))
            decay_chunk = jnp.exp(segsum(chunk_sums))
            new_states = jnp.einsum('bhzc,bchpn->bzhpn', decay_chunk, states)
            states = new_states[:, :-1]
            state_decay_out = jnp.exp(A_cum)
            Y_off = jnp.einsum('bcshn,bchpn,bhcs->bcshp', Cm, states, state_decay_out)
            return (Y_diag + Y_off).reshape(b, l, h, p)
        key = jax.random.key(seed)
        ks = jax.random.split(key, 6)
        input_ = jax.random.normal(ks[0], (2, 1024, D_MODEL), dtype=jnp.float32)
        in_proj_w = jax.random.normal(ks[1], (PROJ_DIM, D_MODEL), dtype=jnp.float32) * (2.0 / D_MODEL) ** 0.5
        cb = (CONV_DIM * KSIZE) ** (-0.5)
        conv1d_weight = jax.random.uniform(ks[2], (CONV_DIM, 1, KSIZE), dtype=jnp.float32, minval=-cb, maxval=cb)
        conv1d_bias = jax.random.uniform(ks[3], (CONV_DIM,), dtype=jnp.float32, minval=-0.5, maxval=0.5)
        z_bias = jnp.zeros((D_INNER,), dtype=jnp.float32)
        D = jnp.ones((N_V_HEADS,), dtype=jnp.float32)
        out_proj_w = jax.random.normal(ks[4], (D_MODEL, D_INNER), dtype=jnp.float32) * (2.0 / D_INNER) ** 0.5
        return {'input_': input_, 'in_proj_w': in_proj_w, 'conv1d_weight': conv1d_weight, 'conv1d_bias': conv1d_bias, 'z_bias': z_bias, 'D': D, 'out_proj_w': out_proj_w}
    _L0_attn_in = _L0_attn_setup()

    def _L0_ffn_setup():
        import jax, jax.numpy as jnp
        import numpy as np

        def binarize_weight(w):
            alpha = jnp.mean(jnp.abs(w), axis=tuple(range(1, w.ndim)), keepdims=True)
            bw = jnp.where(w >= 0, 1.0, -1.0) * alpha
            return jax.lax.stop_gradient(bw - w) + w
        key = jax.random.key(seed)
        k1, k2, k3 = jax.random.split(key, 3)
        in_features, out_features = (512, 512)
        x = jax.random.normal(k1, (8, 512, in_features), dtype=jnp.float32)
        std = np.sqrt(2.0 / out_features).astype(np.float32)
        weight = jax.random.normal(k2, (out_features, in_features), dtype=jnp.float32) * std
        bias = jax.random.normal(k3, (out_features,), dtype=jnp.float32) * 0.01
        return {'x': x, 'weight': weight, 'bias': bias}
    _L0_ffn_in = _L0_ffn_setup()
    _L0_c = _w((lambda *s: np.random.randn(*s).astype(np.float32) * 0.05)(4, 512))
    _L0_wmod = _w((lambda *s: np.random.randn(*s).astype(np.float32) * 0.05)(512, 6 * 512) * 512 ** (-0.5))
    _d = {'L0_attn_input_': _L0_attn_in['input_'], 'L0_attn_in_proj_w': _L0_attn_in['in_proj_w'], 'L0_attn_conv1d_weight': _L0_attn_in['conv1d_weight'], 'L0_attn_conv1d_bias': _L0_attn_in['conv1d_bias'], 'L0_attn_z_bias': _L0_attn_in['z_bias'], 'L0_attn_D': _L0_attn_in['D'], 'L0_attn_out_proj_w': _L0_attn_in['out_proj_w'], 'L0_ffn_weight': _L0_ffn_in['weight'], 'L0_ffn_bias': _L0_ffn_in['bias'], 'L0_c': _L0_c, 'L0_wmod': _L0_wmod}
    _x0 = _d['L0_attn_input_']
    _d['L0_attn_input_'] = jax.random.normal(jax.random.fold_in(jax.random.key(seed), 1), (4, 512, 512), dtype=_x0.dtype)
    del _x0
    return _d

def reference(L0_attn_input_, L0_attn_in_proj_w, L0_attn_conv1d_weight, L0_attn_conv1d_bias, L0_attn_z_bias, L0_attn_D, L0_attn_out_proj_w, L0_ffn_weight, L0_ffn_bias, L0_c, L0_wmod):

    def _L0_attn_ref(input_, in_proj_w, conv1d_weight, conv1d_bias, z_bias, D, out_proj_w):
        import jax, jax.numpy as jnp
        import numpy as np
        D_MODEL = 512
        D_INNER = 1024
        D_STATE = 64
        N_QK_HEADS = 8
        N_V_HEADS = 64
        CHUNK = 128
        KSIZE = 4
        CONV_DIM = D_INNER + 2 * N_QK_HEADS * D_STATE
        PROJ_DIM = CONV_DIM + D_INNER + N_V_HEADS

        def segsum(x):
            T = x.shape[-1]
            xe = jnp.broadcast_to(x[..., None], x.shape + (T,))
            strict_lower = jnp.tril(jnp.ones((T, T), dtype=bool), -1)
            xe = jnp.where(strict_lower, xe, 0.0)
            s = jnp.cumsum(xe, axis=-2)
            lower = jnp.tril(jnp.ones((T, T), dtype=bool), 0)
            return jnp.where(lower, s, -jnp.inf)

        def ssd_chunk_scan(X, dA, Bm, Cm, chunk):
            b, l, h, p = X.shape
            g = Bm.shape[2]
            rep = h // g
            Bm = jnp.repeat(Bm, rep, axis=2)
            Cm = jnp.repeat(Cm, rep, axis=2)
            c = l // chunk
            X = X.reshape(b, c, chunk, h, p)
            Bm = Bm.reshape(b, c, chunk, h, -1)
            Cm = Cm.reshape(b, c, chunk, h, -1)
            A = jnp.transpose(dA.reshape(b, c, chunk, h), (0, 3, 1, 2))
            A_cum = jnp.cumsum(A, axis=-1)
            Lm = jnp.exp(segsum(A))
            Y_diag = jnp.einsum('bcshn,bczhn,bhcsz,bczhp->bcshp', Cm, Bm, Lm, X)
            decay_states = jnp.exp(A_cum[..., -1:] - A_cum)
            states = jnp.einsum('bcshn,bhcs,bcshp->bchpn', Bm, decay_states, X)
            states = jnp.concatenate([jnp.zeros_like(states[:, :1]), states], axis=1)
            chunk_sums = jnp.pad(A_cum[..., -1], ((0, 0), (0, 0), (1, 0)))
            decay_chunk = jnp.exp(segsum(chunk_sums))
            new_states = jnp.einsum('bhzc,bchpn->bzhpn', decay_chunk, states)
            states = new_states[:, :-1]
            state_decay_out = jnp.exp(A_cum)
            Y_off = jnp.einsum('bcshn,bchpn,bhcs->bcshp', Cm, states, state_decay_out)
            return (Y_diag + Y_off).reshape(b, l, h, p)
        b, L, _ = input_.shape
        xBCzA = jnp.einsum('bld,ed->ble', input_, in_proj_w)
        xBC = xBCzA[..., :CONV_DIM]
        z = xBCzA[..., CONV_DIM:CONV_DIM + D_INNER]
        A_log = xBCzA[..., CONV_DIM + D_INNER:]
        xt = jnp.transpose(xBC, (0, 2, 1))
        y = jax.lax.conv_general_dilated(xt, conv1d_weight, (1,), [(KSIZE - 1, 0)], feature_group_count=CONV_DIM, dimension_numbers=('NCH', 'OIH', 'NCH'))
        xBC = jax.nn.silu(jnp.transpose(y + conv1d_bias[None, :, None], (0, 2, 1)))
        x = xBC[..., :D_INNER].reshape(b, L, N_V_HEADS, D_INNER // N_V_HEADS)
        Bm = xBC[..., D_INNER:D_INNER + N_QK_HEADS * D_STATE].reshape(b, L, N_QK_HEADS, D_STATE)
        Cm = xBC[..., D_INNER + N_QK_HEADS * D_STATE:].reshape(b, L, N_QK_HEADS, D_STATE)
        dt = jax.nn.softplus(A_log)
        x_in = x / dt[..., None]
        y_ssm = ssd_chunk_scan(x_in * dt[..., None], -dt, Bm, Cm, CHUNK)
        Du = D[None, None, :, None] * x_in
        yf = (y_ssm + Du).reshape(b, L, D_INNER)
        out = jnp.einsum('bld,ed->ble', yf * jax.nn.silu(z + z_bias), out_proj_w)
        return out

    def _L0_ffn_ref(x, weight, bias):
        import jax, jax.numpy as jnp
        import numpy as np

        def binarize_weight(w):
            alpha = jnp.mean(jnp.abs(w), axis=tuple(range(1, w.ndim)), keepdims=True)
            bw = jnp.where(w >= 0, 1.0, -1.0) * alpha
            return jax.lax.stop_gradient(bw - w) + w
        bw = binarize_weight(weight)
        return jnp.einsum('bsi,oi->bso', x, bw) + bias
    x = L0_attn_input_
    mod = (_silu(L0_c) @ L0_wmod).reshape(L0_c.shape[0], 6, 1, -1)
    sa, ca, ga, sb, cb, gb = (mod[:, 0], mod[:, 1], mod[:, 2], mod[:, 3], mod[:, 4], mod[:, 5])
    ga = (2 * (ga >= 0) - 1) * jnp.maximum(jnp.abs(ga), 0.25)
    gb = (2 * (gb >= 0) - 1) * jnp.maximum(jnp.abs(gb), 0.25)
    h = _layernorm(x, axis=-1) * (1 + ca) + sa
    x = x + ga * _L0_attn_ref(h, L0_attn_in_proj_w, L0_attn_conv1d_weight, L0_attn_conv1d_bias, L0_attn_z_bias, L0_attn_D, L0_attn_out_proj_w)
    h = _layernorm(x, axis=-1) * (1 + cb) + sb
    x = x + gb * _L0_ffn_ref(h, L0_ffn_weight, L0_ffn_bias)
    return x

_drawn_inputs = setup_inputs


def setup_inputs(seed=0):
    import zlib

    import numpy as np

    out = dict(_drawn_inputs(seed))
    spreads = {'L0_attn_z_bias': (0.0, 0.328), 'L0_attn_D': (1.0, 0.2)}
    factors = {'L0_ffn_bias': 25.048}
    for name, (base, spread) in spreads.items():
        noise = np.random.default_rng([zlib.crc32(name.encode()), seed]).standard_normal(out[name].shape)
        drawn = base * np.exp(spread * noise) if base else spread * noise
        out[name] = jnp.asarray(drawn.astype(out[name].dtype))
    for name, factor in factors.items():
        out[name] = (out[name] * factor).astype(out[name].dtype)
    return out
```

```python
from contextlib import ExitStack

import concourse.bass as bass
from concourse import mybir

F32 = mybir.dt.float32
F32R = mybir.dt.float32r
ALU = mybir.AluOpType
ACT = mybir.ActivationFunctionType

P = 128
NB, L, D = 4, 512, 512
DI, NG, NS, NH = 1024, 8, 64, 64
HD = DI // NH
HG = NH // NG
KC = D // P
Q = 128
NC = L // Q
GP = NG // 2
NT = 6
KS = 4
BIG = 16384.0
DT_MAX = 87.0
EPS = 1e-5

R_MASK, R_NEG, R_POS, R_ALL = 0, 64, 80, 96

GROUPS = [[0, 1], [2, 3]] + [[m] for m in range(4, 18)]
FS = [1, 3, 6, 9, 12, 15]
W_SLOT = [6, 7, 10, 11, 14, 15, 18, 19, 22, 23, 26, 27]
PREP = 1


class Step:

    def __init__(self, gp, b):
        self.gp, self.b = gp, b

    def n(self, per_step, off):
        return self.gp * (4 * per_step) + (per_step * self.b + off)

    def next(self):
        return Step(self.gp, self.b + 1) if self.b < 3 else Step(self.gp + 1, 0)

    def prev(self):
        return Step(self.gp, self.b - 1) if self.b else Step(self.gp - 1, 3)

    @property
    def par(self):
        return self.b % 2


def wait(eng, sem, count):
    if not isinstance(count, int) or count > 0:
        eng.wait_ge(sem, count)


class Shared:
    pass


def adaln_kernel(nc, x, w_in, conv_w, conv_b, z_bias, d_skip, w_out, w_ffn, b_ffn, cond, w_mod, out):
    with ExitStack() as ctx:
        s = Shared()

        def sb(name, shape, dt=F32):
            return ctx.enter_context(nc.sbuf_tensor(name, shape, dt))

        s.bank = [ctx.enter_context(nc.psum_tensor(f"bank{i}", [P, 512], F32)) for i in range(8)]
        s.ident = sb("ident", [P, P])
        s.tri = sb("tri", [P, P])
        s.mod_t = sb("mod_t", [P, 4, KC, NB])
        s.y_d = nc.dram_tensor("y_scratch", (NG * P, NB * L), F32).ap()
        s.ea_d = nc.dram_tensor("ea_scratch", (NB * NH, L), F32).ap()
        s.dd_d = nc.dram_tensor("dd_scratch", (NB * NH, L), F32).ap()
        s.a_d = nc.dram_tensor("a_scratch", (2, NB * NH, L), F32).ap()
        s.na_d = nc.dram_tensor("na_scratch", (2, NB * NH, L), F32).ap()
        s.cd_d = nc.dram_tensor("cd_scratch", (NH, NB * NC), F32).ap()
        s.g_d = nc.dram_tensor("gate_scratch", (2, NB, D), F32).ap()
        with ExitStack() as main_ctx:
            def sbm(name, shape, dt=F32):
                return main_ctx.enter_context(nc.sbuf_tensor(name, shape, dt))

            s.h_hi = sbm("h_hi", [P, NB, KC, L], F32R)
            s.h_lo = sbm("h_lo", [P, NB, KC, L], F32R)
            s.w_hi = sbm("w_hi", [P, NT, KC, P], F32R)
            s.w_lo = sbm("w_lo", [P, NT, KC, P], F32R)
            s.R = sbm("R", [R_ALL, 2, 2, HG * Q], F32R)
            s.Lm = sbm("Lm", [R_ALL, 2, 2, Q], F32R)
            s.wend = sbm("wend", [P, GP, NB, NC, 2 * HG])
            s.gpc = sbm("gpc", [P, GP, 4 * (KS + 1) + 2])
            prologue(nc, s, x, w_in, conv_w, conv_b, z_bias, d_skip, cond, w_mod)
            main_part(nc, s, w_in)
        tail_part(nc, s, x, w_out, w_ffn, b_ffn, out)


def tile_rows(gp, t):
    if t < 2:
        return (2 * gp + t) * P
    if t < 4:
        return gp * P + (DI if t == 2 else DI + NG * NS)
    return (2 * gp + t - 4) * P + DI + 2 * NG * NS


def prologue(nc, s, x, w_in, conv_w, conv_b, z_bias, d_skip, cond, w_mod):
    with ExitStack() as ctx:
        def sb(name, shape, dt=F32):
            return ctx.enter_context(nc.sbuf_tensor("p_" + name, shape, dt))

        def sem(name):
            return ctx.enter_context(nc.semaphore("p_" + name))

        c4, th4, sc4 = sb("c4", [NB, D]), sb("th4", [NB, D]), sb("sc4", [NB, D])
        scT = sb("scT", [P, KC, NB])
        wm = sb("wm", [P, 2, KC, D])
        xt, xn = sb("xt", [P, 4, D]), sb("xn", [P, 2, D])
        st, mv, rstd = sb("st", [P, 2, 6]), sb("mv", [P, 2, 2]), sb("rstd", [P, 2, 2])
        half = sb("half", [P, 1])
        hf = sb("hf", [P, 2, L])
        stage = sb("stage", [R_ALL, HG * Q])
        lstage = sb("lstage", [R_ALL, Q])
        wa_raw = sb("wa_raw", [NH, D])
        wa_hi, wa_lo = sb("wa_hi", [P, KC, 192], F32R), sb("wa_lo", [P, KC, 192], F32R)
        wraw = sb("wraw", [P, 2, D])
        rows, rabs, rsg = sb("rows", [NB, 2, D]), sb("rabs", [NB, 2, D]), sb("rsg", [NB, 2, D])
        chunk_on = sb("chunk_on", [P, L])
        dcol = sb("dcol", [P, 1])
        r, e, den, sv, tt, pl, dt, tmp = [sb(f"a{i}", [P, L]) for i in range(8)]
        ahi = sb("ahi", [P, L], F32R)
        cde = sb("cde", [P, NC])

        d_c, d_wa, d_small, d_scr, d_gate = sem("d_c"), sem("d_wa"), sem("d_small"), sem("d_scr"), sem("d_gate")
        d_x, d_wm, d_w = [sem(f"d_x{i}") for i in range(4)], [sem(f"d_wm{i}") for i in range(2)], [sem(f"d_w{i}") for i in range(2)]
        konst, kcopy = sem("konst"), sem("kcopy")
        sc_ready, sct_pe, sct_ready = sem("sc_ready"), sem("sct_pe"), sem("sct_ready")
        th_ready, mod_pe, mod_ready = sem("th_ready"), sem("mod_pe"), sem("mod_ready")
        gate_abs, gate_v, gate_ready = sem("gate_abs"), sem("gate_v"), sem("gate_ready")
        ln_bn, ln_st, ln_eps, ln_rs, ln_n = sem("ln_bn"), sem("ln_st"), sem("ln_eps"), sem("ln_rs"), sem("ln_n")
        t_pe, h_act, h_hi, h_lo = sem("t_pe"), sem("h_act"), sem("h_hi"), sem("h_lo")
        wa_pe, wa_act, wa_dve = sem("wa_pe"), sem("wa_act"), sem("wa_dve")
        wt_pe, w_act, w_dve = sem("wt_pe"), sem("w_act"), sem("w_dve")
        a_pe, a_act, a_v, we_pe, we_ev = sem("a_pe"), sem("a_act"), sem("a_v"), sem("we_pe"), sem("we_ev")
        N_SMALL = 2 * 16 + GP + 2
        A_DD, A_SUM, A_PARTS, A_END, A_EA, A_ALL = 23, 25, 29, 30, 31, 31
        SEC = [1, 0, 4, 3, 2, 5]
        MOD_BANK = [6, 7, 0, 1]
        block = ctx.enter_context(nc.Block())

        @block.sync
        def _(sp):
            sp.dma_start(c4[:, :], cond).then_inc(d_c, 16)
            wmv = w_mod.rearrange("(k p) n -> p k n", p=P)
            xv = x.rearrange("b (t p) d -> (b t) p d", p=P)
            sp.dma_start(xt[:, 0, :], xv[0]).then_inc(d_x[0], 16)
            for n in range(2):
                sp.dma_start(wm[:, n, :, :], wmv[:, :, SEC[n] * D:(SEC[n] + 1) * D]).then_inc(d_wm[n], 16)
            for i in range(1, 4):
                sp.dma_start(xt[:, i, :], xv[i]).then_inc(d_x[i], 16)
            sp.dma_start(wa_raw[:, :], w_in[2 * DI + 2 * NG * NS:, :]).then_inc(d_wa, 16)
            for i in range(4, 16):
                sp.wait_ge(ln_n, i - 3)
                sp.dma_start(xt[:, i % 4, :], xv[i]).then_inc(d_x[i % 4], 16)
            for n in range(2, 4):
                sp.wait_ge(mod_pe, n - 1)
                sp.dma_start(wm[:, n % 2, :, :], wmv[:, :, SEC[n] * D:(SEC[n] + 1) * D]).then_inc(d_wm[n % 2], 16)
            for t in range(2):
                sp.dma_start(wraw[:, t, :], w_in[tile_rows(0, t):tile_rows(0, t) + P, :]).then_inc(d_w[t], 16)
            for pb in range(2):
                rows2 = slice(pb * P, pb * P + P)
                n0 = A_ALL * pb
                sp.wait_ge(a_v, n0 + A_DD)
                sp.dma_start(s.dd_d[rows2, :], den[:, :]).then_inc(d_scr, 16)
                sp.wait_ge(a_v, n0 + A_PARTS)
                sp.dma_start(s.a_d[0, rows2, :], ahi[:, :].bitcast(F32)).then_inc(d_scr, 16)
                sp.dma_start(s.a_d[1, rows2, :], sv[:, :]).then_inc(d_scr, 16)
                sp.dma_start(s.na_d[0, rows2, :], r[:, :]).then_inc(d_scr, 16)
                sp.dma_start(s.na_d[1, rows2, :], dt[:, :]).then_inc(d_scr, 16)
                sp.wait_ge(a_v, n0 + A_EA)
                sp.dma_start(s.ea_d[rows2, :], tt[:, :]).then_inc(d_scr, 16)
                sp.wait_ge(a_act, 5 * pb + 5)
                for q in range(2):
                    b = 2 * pb + q
                    with nc.allow_non_contiguous_dma(reason="a few decays per head"):
                        sp.dma_start(s.cd_d[:, b * NC:(b + 1) * NC], cde[64 * q:64 * q + 64, :]).then_inc(d_scr, 16)
            for n in range(4, 6):
                sp.wait_ge(mod_pe, n - 1)
                sp.dma_start(wm[:, n % 2, :, :], wmv[:, :, SEC[n] * D:(SEC[n] + 1) * D]).then_inc(d_wm[n % 2], 16)
            for t in range(2, NT):
                sp.wait_ge(wt_pe, 2 * (t - 2) + 2)
                sp.dma_start(wraw[:, t % 2, :], w_in[tile_rows(0, t):tile_rows(0, t) + P, :]).then_inc(d_w[t % 2], 16)
            sp.wait_ge(gate_ready, 2)
            sp.dma_start(s.g_d.rearrange("g b d -> b g d"), rows[:, :, :]).then_inc(d_gate, 16)
            sp.wait_ge(d_scr, 16 * 16)
            sp.wait_ge(d_gate, 16)

        @block.gpsimd
        def _(pool):
            pool.memset(s.ident[:, :], 0.0).then_inc(konst, 1)
            pool.wait_ge(konst, 1)
            pool.memset(s.tri[:, :], 0.125).then_inc(konst, 1)
            pool.wait_ge(konst, 2)
            pool.memset(stage[:, :], 0.0).then_inc(konst, 1)
            pool.wait_ge(konst, 3)
            pool.memset(lstage[0:64, :], 0.0).then_inc(konst, 1)
            pool.wait_ge(konst, 4)
            pool.memset(lstage[64:96, :], 1.0).then_inc(konst, 1)
            pool.wait_ge(konst, 5)
            pool.memset(half[:, :], -0.5).then_inc(konst, 1)
            pool.wait_ge(konst, 6)
            pool.memset(chunk_on[:, :], 1.0).then_inc(konst, 1)
            pool.wait_ge(konst, 7)
            pool.affine_select(out=s.ident[:, :], in_=s.ident[:, :], compare_op=ALU.not_equal, fill=1.0,
                               base=0, pattern=[[-1, P]], channel_multiplier=1).then_inc(konst, 1)
            pool.wait_ge(konst, 8)
            pool.affine_select(out=s.tri[:, :], in_=s.tri[:, :], compare_op=ALU.is_ge, fill=0.0,
                               base=0, pattern=[[1, P]], channel_multiplier=-1).then_inc(konst, 1)
            mrow = stage[0:64, :].rearrange("p (h s) -> p h s", h=HG)
            pool.wait_ge(konst, 9)
            pool.affine_select(out=mrow, in_=mrow, compare_op=ALU.is_ge, fill=-BIG,
                               base=0, pattern=[[0, HG], [1, Q]], channel_multiplier=-2).then_inc(konst, 1)
            lrow = lstage[0:64, :].rearrange("p (z r) -> p z r", r=2)
            pool.wait_ge(konst, 10)
            pool.affine_select(out=lrow, in_=lrow, compare_op=ALU.not_equal, fill=1.0,
                               base=0, pattern=[[-1, Q // 2], [0, 2]], channel_multiplier=1).then_inc(konst, 1)
            drow = stage[64:80, :].rearrange("p (h s) -> p h s", h=HG)
            pool.wait_ge(konst, 11)
            pool.affine_select(out=drow, in_=drow, compare_op=ALU.not_equal, fill=1.0,
                               base=0, pattern=[[-1, HG], [0, Q]], channel_multiplier=1).then_inc(konst, 1)
            pool.wait_ge(konst, 12)
            pool.affine_select(out=drow, in_=drow, compare_op=ALU.not_equal, fill=1.0,
                               base=-HG, pattern=[[-1, HG], [0, Q]], channel_multiplier=1).then_inc(konst, 1)
            cmv = chunk_on[:, :].rearrange("p (c q) -> p c q", q=Q)
            pool.wait_ge(konst, 13)
            pool.affine_select(out=cmv, in_=cmv, compare_op=ALU.not_equal, fill=0.0,
                               base=0, pattern=[[0, NC], [1, Q]], channel_multiplier=0).then_inc(konst, 1)
            pool.wait_ge(konst, 14)
            pool.memset(wa_hi[:, :, :].bitcast(F32), 0.0).then_inc(konst, 1)
            pool.wait_ge(konst, 15)
            pool.memset(wa_lo[:, :, :].bitcast(F32), 0.0).then_inc(konst, 1)
            for i in range(16):
                pool.wait_ge(ln_st, i + 1)
                if i >= 2:
                    pool.wait_ge(ln_n, i - 1)
                pool.tensor_scalar(rstd[:, i % 2, 0:1], mv[:, i % 2, 1:2], EPS, None, ALU.add).then_inc(ln_eps, 1)
                pool.wait_ge(ln_eps, i + 1)
                pool.tensor_tensor(rstd[:, i % 2, 1:2], rstd[:, i % 2, 0:1], half[:, :], ALU.pow).then_inc(ln_rs, 1)
            pool.wait_ge(d_small, 16 * N_SMALL)

        @block.vector
        def _(dve):
            dve.wait_ge(d_c, 16)
            dve.wait_ge(th_ready, 1)
            dve.scalar_tensor_tensor(out=sc4[:, :], in0=th4[:, :], scalar=1.0, in1=c4[:, :],
                                     op0=ALU.add, op1=ALU.mult).then_inc(sc_ready, 1)
            dve.wait_ge(sct_pe, 1)
            dve.tensor_scalar(scT[:, :, :], s.bank[4][:, 0:KC * NB].rearrange("p (k b) -> p k b", k=KC),
                              0.5, None, ALU.mult).then_inc(sct_ready, 1)
            dve.wait_ge(konst, 16)
            for i in range(4):
                dve.tensor_copy(s.R[:, i // 2, i % 2, :], stage[:, :]).then_inc(kcopy, 1)
                dve.tensor_copy(s.Lm[:, i // 2, i % 2, :], lstage[:, :]).then_inc(kcopy, 1)

            def modulation(n):
                dve.wait_ge(mod_pe, n + 1)
                dve.tensor_scalar(s.mod_t[:, n, :, :],
                                  s.bank[MOD_BANK[n]][:, 0:KC * NB].rearrange("p (k b) -> p k b", k=KC),
                                  1.0 - n % 2, None, ALU.add).then_inc(mod_ready, 1)

            def statistics(i):
                dve.wait_ge(d_x[i % 4], 16 * (i // 4 + 1))
                dve.bn_stats(st[:, i % 2, :], xt[:, i % 4, :]).then_inc(ln_bn, 1)
                dve.wait_ge(ln_bn, i + 1)
                if i >= 2:
                    dve.wait_ge(ln_rs, i - 1)
                    dve.wait_ge(ln_n, i - 1)
                dve.bn_aggr(mv[:, i % 2, :], st[:, i % 2, :]).then_inc(ln_st, 1)

            def normalize(i):
                dve.wait_ge(ln_rs, i + 1)
                if i >= 2:
                    dve.wait_ge(t_pe, i - 1)
                dve.tensor_scalar(xn[:, i % 2, :], xt[:, i % 4, :], mv[:, i % 2, 0:1], rstd[:, i % 2, 1:2],
                                  ALU.subtract, ALU.mult).then_inc(ln_n, 1)

            def split(b, k):
                n = b * KC + k
                dve.wait_ge(h_act, n + 1)
                dve.tensor_copy(s.h_hi[:, b, k, :], hf[:, n % 2, :]).then_inc(h_hi, 1)
                dve.wait_ge(h_hi, n + 1)
                dve.tensor_tensor(s.h_lo[:, b, k, :], hf[:, n % 2, :], s.h_hi[:, b, k, :].bitcast(F32),
                                  ALU.subtract).then_inc(h_lo, 1)

            statistics(0)
            modulation(0)
            modulation(1)
            for i in range(16):
                if i < 15:
                    statistics(i + 1)
                normalize(i)
                if i == 3:
                    dve.wait_ge(wa_act, 1)
                    dve.tensor_tensor(wa_lo[:, :, 64:128], s.bank[5][:, 0:KC * NH].rearrange("p (k h) -> p k h", k=KC),
                                      wa_hi[:, :, 64:128].bitcast(F32), ALU.subtract).then_inc(wa_dve, 1)
                if i % 4 == 3:
                    for k in range(KC):
                        split(i // 4, k)
            count = [0]

            def link(ins):
                count[0] += 1
                ins.then_inc(a_v, 1)
                dve.wait_ge(a_v, count[0])

            for pb in range(2):
                dve.wait_ge(a_pe, pb + 1)
                if pb:
                    dve.wait_ge(d_scr, 16 * 8)
                    dve.wait_ge(a_act, 5)
                link(dve.tensor_scalar(r[:, :], s.bank[4 + pb][:, :], 0.0, None, ALU.max))
                dve.wait_ge(a_act, 5 * pb + 2)
                link(dve.tensor_scalar(den[:, :], e[:, :], 2.0, None, ALU.add))
                link(dve.reciprocal(tmp[:, :], den[:, :]))
                link(dve.tensor_tensor(sv[:, :], e[:, :], tmp[:, :], ALU.mult))
                link(dve.tensor_tensor(tt[:, :], sv[:, :], sv[:, :], ALU.mult))
                link(dve.tensor_scalar(pl[:, :], tt[:, :], 1.0 / 17, 1.0 / 15, ALU.mult, ALU.add))
                for k in (13, 11, 9, 7, 5, 3):
                    link(dve.tensor_tensor(pl[:, :], pl[:, :], tt[:, :], ALU.mult))
                    link(dve.tensor_scalar(pl[:, :], pl[:, :], 1.0 / k, None, ALU.add))
                link(dve.tensor_tensor(pl[:, :], pl[:, :], tt[:, :], ALU.mult))
                link(dve.scalar_tensor_tensor(out=pl[:, :], in0=pl[:, :], scalar=1.0, in1=sv[:, :],
                                              op0=ALU.add, op1=ALU.mult))
                link(dve.scalar_tensor_tensor(out=dt[:, :], in0=pl[:, :], scalar=2.0, in1=r[:, :],
                                              op0=ALU.mult, op1=ALU.add))
                link(dve.reciprocal(den[:, :], dt[:, :]))
                dve.wait_ge(d_small, 16 * N_SMALL)
                link(dve.tensor_scalar(den[:, :], den[:, :], dcol[:, 0:1], 0.5, ALU.mult, ALU.mult))
                assert count[0] == A_ALL * pb + A_DD
                link(dve.tensor_scalar(tmp[:, :], dt[:, :], DT_MAX, -1.0, ALU.min, ALU.mult))
                link(dve.tensor_tensor_scan(out=pl[:, :], data0=chunk_on[:, :], data1=tmp[:, :], initial=0.0,
                                            op0=ALU.mult, op1=ALU.add))
                link(dve.tensor_copy(ahi[:, :], pl[:, :]))
                link(dve.tensor_tensor(sv[:, :], pl[:, :], ahi[:, :].bitcast(F32), ALU.subtract))
                link(dve.tensor_scalar(r[:, :], ahi[:, :].bitcast(F32), -1.0, None, ALU.mult))
                link(dve.tensor_scalar(dt[:, :], sv[:, :], -1.0, None, ALU.mult))
                assert count[0] == A_ALL * pb + A_PARTS
                plv = pl[:, :].rearrange("p (c q) -> p c q", q=Q)
                link(dve.tensor_tensor(tmp[:, :].rearrange("p (c q) -> p c q", q=Q),
                                       plv[:, :, Q - 1:Q].broadcast_to([P, NC, Q]), plv, ALU.subtract))
                dve.wait_ge(a_act, 5 * pb + 3)
                link(dve.tensor_scalar(tt[:, :], tt[:, :], 0.125, None, ALU.mult))
                assert count[0] == A_ALL * pb + A_EA
                dve.wait_ge(we_pe, pb + 1)
                for c in range(NC):
                    for q in range(2):
                        ins = dve.tensor_copy(
                            s.wend[:, :, 2 * pb + q, c, :],
                            s.bank[7 - pb][:, c * P + q * 64:c * P + q * 64 + 64].rearrange("p (g h) -> p g h", g=GP))
                    ins.then_inc(we_ev, 1)
            modulation(2)
            modulation(3)
            dve.wait_ge(gate_abs, 2)
            for n in range(2):
                dve.tensor_scalar(rsg[:, n, :], s.bank[2 + n][0:NB, :], 0.0, 2.0, ALU.is_ge, ALU.mult).then_inc(gate_v, 1)
            dve.wait_ge(gate_v, 2)
            dve.tensor_scalar(rsg[:, :, :], rsg[:, :, :], -1.0, None, ALU.add).then_inc(gate_v, 1)
            dve.tensor_scalar(rabs[:, 0, :], rabs[:, 0, :], 0.25, 0.5, ALU.max, ALU.mult).then_inc(gate_v, 1)
            dve.tensor_scalar(rabs[:, 1, :], rabs[:, 1, :], 0.25, None, ALU.max).then_inc(gate_v, 1)
            dve.wait_ge(gate_v, 5)
            for n in range(2):
                dve.tensor_tensor(rows[:, n, :], rsg[:, n, :], rabs[:, n, :], ALU.mult).then_inc(gate_ready, 1)
            for n in range(2 * NT):
                t, hh = n // 2, n % 2
                dve.wait_ge(w_act, n + 1)
                dve.tensor_tensor(s.w_lo[:, t, 2 * hh:2 * hh + 2, :],
                                  s.bank[hh][:, 0:2 * P].rearrange("p (k r) -> p k r", k=2),
                                  s.w_hi[:, t, 2 * hh:2 * hh + 2, :].bitcast(F32), ALU.subtract).then_inc(w_dve, 1)

        @block.scalar
        def _(act):
            cwv = conv_w.rearrange("(t p) o k -> p t (o k)", p=P)
            cbv = conv_b.rearrange("(t p) -> p t", p=P)
            zbv = z_bias.rearrange("(t p) -> p t", p=P)
            dv = d_skip.rearrange("(h o) -> h o", o=1)
            act.wait_ge(d_c, 16)
            act.activation(th4[:, :], c4[:, :], ACT.Tanh, scale=0.5).then_inc(th_ready, 1)
            with nc.allow_non_contiguous_dma(reason="small vectors laid out by partition"):
                for g in range(GP):
                    for t in range(4):
                        n, o = tile_rows(g, t) // P, t * (KS + 1)
                        act.dma_start(s.gpc[:, g, o:o + KS], cwv[:, n, :]).then_inc(d_small, 16)
                        act.dma_start(s.gpc[:, g, o + KS:o + KS + 1], cbv[:, n:n + 1]).then_inc(d_small, 16)
                    act.dma_start(s.gpc[:, g, 20:22], zbv[:, 2 * g:2 * g + 2]).then_inc(d_small, 16)
                act.dma_start(dcol[0:64, :], dv).then_inc(d_small, 16)
                act.dma_start(dcol[64:128, :], dv).then_inc(d_small, 16)
            act.wait_ge(konst, 16)
            act.wait_ge(wa_pe, 1)
            act.activation(wa_hi[:, :, 64:128], s.bank[5][:, 0:KC * NH].rearrange("p (k h) -> p k h", k=KC),
                           ACT.Copy).then_inc(wa_act, 1)
            act.wait_ge(mod_ready, 2)
            for n in range(NB * KC):
                b, k = n // KC, n % KC
                act.wait_ge(t_pe, 4 * b + 4)
                if n >= 2:
                    act.wait_ge(h_lo, n - 1)
                act.activation(hf[:, n % 2, :], s.bank[k][:, :], ACT.Identity, scale=s.mod_t[:, 0, k, b:b + 1],
                               bias=s.mod_t[:, 1, k, b:b + 1]).then_inc(h_act, 1)
            for pb in range(2):
                n0 = A_ALL * pb
                act.wait_ge(a_v, n0 + 1)
                act.activation(e[:, :], s.bank[4 + pb][:, :], ACT.Abs).then_inc(a_act, 1)
                act.wait_ge(a_act, 5 * pb + 1)
                act.activation(e[:, :], e[:, :], ACT.Exp, scale=-1.0).then_inc(a_act, 1)
                act.wait_ge(a_v, n0 + A_SUM)
                act.activation(tt[:, :], pl[:, :], ACT.Exp).then_inc(a_act, 1)
                act.wait_ge(a_v, n0 + A_END)
                act.activation(tmp[:, :], tmp[:, :], ACT.Exp).then_inc(a_act, 1)
                act.activation(cde[:, :], pl[:, :].rearrange("p (c q) -> p c q", q=Q)[:, :, Q - 1], ACT.Exp)\
                   .then_inc(a_act, 1)
            for n in range(2):
                act.wait_ge(mod_pe, 5 + n)
                act.activation(rabs[:, n, :], s.bank[2 + n][0:NB, :], ACT.Abs).then_inc(gate_abs, 1)
            for n in range(2 * NT):
                t, hh = n // 2, n % 2
                act.wait_ge(wt_pe, n + 1)
                act.activation(s.w_hi[:, t, 2 * hh:2 * hh + 2, :],
                               s.bank[hh][:, 0:2 * P].rearrange("p (k r) -> p k r", k=2), ACT.Copy).then_inc(w_act, 1)

        @block.tensor
        def _(pe):
            pe.wait_ge(sc_ready, 1)
            pe.wait_ge(konst, 8)
            for k in range(KC):
                ins = pe.transpose(s.bank[4][:, k * NB:(k + 1) * NB], sc4[:, k * P:(k + 1) * P], s.ident[0:NB, 0:NB])
            ins.then_inc(sct_pe, 1)

            def section(n):
                pe.wait_ge(d_wm[n % 2], 16 * (n // 2 + 1))
                for m in range(KC):
                    for k in range(KC):
                        ins = pe.matmul(s.bank[MOD_BANK[n]][:, m * NB:(m + 1) * NB],
                                        wm[:, n % 2, k, m * P:(m + 1) * P], scT[:, k, :],
                                        start=(k == 0), stop=(k == KC - 1))
                ins.then_inc(mod_pe, 1)

            pe.wait_ge(sct_ready, 1)
            section(0)
            section(1)
            pe.wait_ge(d_wa, 16)
            for k in range(KC):
                ins = pe.transpose(s.bank[5][:, k * NH:(k + 1) * NH], wa_raw[:, k * P:(k + 1) * P],
                                   s.ident[0:NH, 0:NH])
            ins.then_inc(wa_pe, 1)
            for i in range(16):
                b = i // 4
                pe.wait_ge(ln_n, i + 1)
                if b and i % 4 == 0:
                    pe.wait_ge(h_act, 4 * b)
                for k in range(KC):
                    ins = pe.transpose(s.bank[k][:, (i % 4) * P:(i % 4 + 1) * P], xn[:, i % 2, k * P:(k + 1) * P],
                                       s.ident[:, :])
                ins.then_inc(t_pe, 1)
            for pb in range(2):
                pe.wait_ge(wa_dve, 1)
                pe.wait_ge(h_lo, 8 * pb + 8)
                n = 0
                for q in range(2):
                    b, w = 2 * pb + q, slice(64 - 64 * q, 192 - 64 * q)
                    for k in range(KC):
                        for wt, h in ((wa_hi, s.h_hi), (wa_hi, s.h_lo), (wa_lo, s.h_hi)):
                            ins = pe.matmul(s.bank[4 + pb][:, :], wt[:, k, w], h[:, b, k, :],
                                            start=(n == 0), stop=(n == 23))
                            n += 1
                ins.then_inc(a_pe, 1)
            pe.wait_ge(h_act, 16)
            section(2)
            section(3)
            pe.wait_ge(mod_ready, 2)
            for pb in range(2):
                pe.wait_ge(a_act, 5 * pb + 4)
                for c in range(NC):
                    ins = pe.transpose(s.bank[7 - pb][:, c * P:(c + 1) * P], tmp[:, c * P:(c + 1) * P], s.ident[:, :])
                ins.then_inc(we_pe, 1)
            for n in range(2):
                pe.wait_ge(d_wm[n], 48)
                for k in range(KC):
                    ins = pe.matmul(s.bank[2 + n][0:NB, :], scT[:, k, :], wm[:, n, k, :],
                                    start=(k == 0), stop=(k == KC - 1))
                ins.then_inc(mod_pe, 1)
            for n in range(2 * NT):
                t, hh = n // 2, n % 2
                pe.wait_ge(d_w[t % 2], 16 * (t // 2 + 1))
                if n == 0:
                    pe.wait_ge(mod_ready, 4)
                if n >= 2:
                    pe.wait_ge(w_dve, n - 1)
                for k in range(2):
                    ins = pe.transpose(s.bank[hh][:, k * P:(k + 1) * P],
                                       wraw[:, t % 2, (2 * hh + k) * P:(2 * hh + k + 1) * P], s.ident[:, :])
                ins.then_inc(wt_pe, 1)


def halves_before(b, k):
    return sum(slot < 16 * (b - 2) + k for slot in W_SLOT)


def main_part(nc, s, w_in):
    with ExitStack() as ctx:
        def sb(name, shape, dt=F32):
            return ctx.enter_context(nc.sbuf_tensor("m_" + name, shape, dt))

        def sem(name):
            return ctx.enter_context(nc.semaphore("m_" + name))

        wraw = sb("wraw", [P, 2, D])
        wst = sb("wst", [P, 2, 2 * P])
        gcs = sb("gcs", [P, 22])
        cd = sb("cd", [P, GP, HG, NB * NC])
        cv, th = sb("cv", [P, 2, L]), sb("th", [P, 2, L])
        xs, gate = sb("xs", [P, 2, 2, L]), sb("gate", [P, 2, 2, L])
        Bt = sb("Bt", [P, 2, L])
        Ct = sb("Ct", [P, 2, 2, L])
        ea, dd = sb("ea", [P, 2, 2, L]), sb("dd", [P, 2, 2, L])
        E, M = sb("E", [P, 4, 4 * Q]), sb("M", [P, 4, 4 * Q])
        Gm = sb("Gm", [P, 2, Q])
        Xp = sb("Xp", [P, 2, 2 * HG, 32])
        Xw = sb("Xw", [P, 2, HG * HD])
        BTs = sb("BTs", [P, P])
        S, S1 = sb("S", [P, HG * HD]), sb("S1", [P, HG * HD])
        y1 = sb("y1", [P, 2, 2, L])
        t1 = sb("t1", [P, 2, L])
        A, DB, YB, GB, SB = s.bank[0:2], s.bank[2:4], s.bank[4:6], s.bank[6], s.bank[7]

        cd_ready, zeroed, gcs_ready = sem("cd_ready"), sem("zeroed"), sem("gcs_ready")
        rl_ready, eb_ready, wraw_ready = ([sem(f"{n}{i}") for i in range(2)] for n in ("rl_ready", "eb_ready", "wraw_ready"))
        in_done, lin_done, tap_done, conv_done, tanh_done, silu_done = (
            sem(n) for n in ("in_done", "lin_done", "tap_done", "conv_done", "tanh_done", "silu_done"))
        d_done, exp_done, prep_done, gm_done, m_done, yd_done = (
            sem(n) for n in ("d_done", "exp_done", "prep_done", "gm_done", "m_done", "yd_done"))
        bt_done, bt_read, xp_done, xw_done, st_done, s_part, s_new, yo_done = (
            sem(n) for n in ("bt_done", "bt_read", "xp_done", "xw_done", "st_done", "s_part", "s_new", "yo_done"))
        yo_scaled, y1_done, t1_done, t2_done, y_out, y_stored = (
            sem(n) for n in ("yo_scaled", "y1_done", "t1_done", "t2_done", "y_out", "y_stored"))
        w_pe, w_copied, w_hi_done, w_lo_done = sem("w_pe"), sem("w_copied"), sem("w_hi_done"), sem("w_lo_done")
        block = ctx.enter_context(nc.Block())

        def run(eng, step):
            for b in range(4):
                step(Step(0, b))
            with eng.Fori(1, GP - 1) as gp:
                for b in range(4):
                    step(Step(gp, b))
            for b in range(4):
                step(Step(GP - 1, b))

        def last(st):
            return isinstance(st.gp, int) and st.gp == GP - 1

        def ahead(st):
            return not (last(st) and st.b == 3)

        def nxt(st, c, by=1):
            return (st, c + by) if c + by < NC else (st.next(), c + by - NC)

        def tok(c):
            return slice(c * Q, (c + 1) * Q)

        @block.sync
        def _(sp):
            a_v = s.a_d.rearrange("r (b g q h) t -> r b g q h t", b=NB, g=GP, q=2)
            na_v = s.na_d.rearrange("r (b g q h) t -> r b g q h t", b=NB, g=GP, q=2)
            ea_v = s.ea_d.rearrange("(b g q h) t -> b g q h t", b=NB, g=GP, q=2)
            dd_v = s.dd_d.rearrange("(b g q h) t -> b g q h t", b=NB, g=GP, q=2)
            y_v = s.y_d.rearrange("(g q p) t -> g p q t", q=2, p=P)
            cd_v = s.cd_d.rearrange("(g q h) n -> q g h n", g=GP, q=2)

            def load_decays(st, c):
                for h in range(HG):
                    sp.dma_start(s.R[R_POS + h:R_ALL:HG, c % 2, :, h * Q:(h + 1) * Q].bitcast(F32),
                                 a_v[:, st.b, st.gp, :, h, tok(c)]).then_inc(rl_ready[c % 2], 16)
                for r in range(2):
                    sp.dma_start(s.Lm[R_NEG + r * HG:R_NEG + (r + 1) * HG, c % 2, :, :].bitcast(F32),
                                 na_v[r, st.b, st.gp, :, :, tok(c)].rearrange("q h t -> h q t"))\
                      .then_inc(rl_ready[c % 2], 16)

            def load_scales(st):
                for q in range(2):
                    for dst, src in ((ea, ea_v), (dd, dd_v)):
                        for_heads = src[st.b, st.gp, q].unsqueeze(1).broadcast_to([HG, HD, L])
                        sp.dma_start(dst[:, st.par, q, :], for_heads).then_inc(eb_ready[st.par], 16)

            def load_weights(gp, t):
                for_pair = w_rows(gp, t)
                sp.dma_start(wraw[:, t % 2, :], for_pair).then_inc(wraw_ready[t % 2], 16)

            w_x = w_in[0:DI, :].rearrange("(g q p) d -> g q p d", q=2, p=P)
            w_bc = w_in[DI:2 * DI, :].rearrange("(o g p) d -> o g p d", o=2, p=P)
            w_z = w_in[2 * DI:3 * DI, :].rearrange("(g q p) d -> g q p d", q=2, p=P)

            def w_rows(gp, t):
                return w_x[gp, t] if t < 2 else w_bc[t - 2, gp] if t < 4 else w_z[gp, t - 4]

            def step(st):
                for c in range(NC):
                    j4 = st.n(16, 4 * c)
                    st2, c2 = nxt(st, c, 2)
                    if ahead(st) or c < 2:
                        sp.wait_ge(d_done, j4 + 4)
                        load_decays(st2, c2)
                    if c == 1:
                        if not (isinstance(st.gp, int) and st.gp == 0 and st.b == 0):
                            store(st.prev())
                        if ahead(st):
                            load_scales(st.next())
                    if not last(st):
                        if st.b == 1 and c == 2:
                            wait(sp, w_pe, st.gp * 12)
                            load_weights(st.gp + 1, 0)
                            load_weights(st.gp + 1, 1)
                        if (st.b, c) in ((2, 2), (2, 3), (3, 0), (3, 1)):
                            t = 4 * (st.b - 2) + c
                            sp.wait_ge(w_pe, st.gp * 12 + (2 * t - 2))
                            load_weights(st.gp + 1, t)

            def store(st):
                sp.wait_ge(y_out, st.n(1, 1))
                sp.dma_start(y_v[st.gp][:, :, st.b * L:(st.b + 1) * L], t1[:, :, :]).then_inc(y_stored, 16)

            for q in range(2):
                sp.dma_start(cd[64 * q:64 * q + 64, :, :, :],
                             cd_v[q].unsqueeze(0).broadcast_to([NS, GP, HG, NB * NC])).then_inc(cd_ready, 16)
            load_decays(Step(0, 0), 0)
            load_decays(Step(0, 0), 1)
            load_scales(Step(0, 0))
            run(sp, step)
            store(Step(GP - 1, 3))
            sp.wait_ge(y_stored, 16 * 4 * GP)

        @block.tensor
        def _(pe):
            def project(st, m):
                t, part = m // 3, m % 3
                if part == 0:
                    if st.b == 0 and not (isinstance(st.gp, int) and st.gp == 0):
                        pe.wait_ge(w_lo_done, st.gp * 12 + (2 * t + 2 - 12))
                    if t < 2:
                        wait(pe, lin_done, st.n(6, t - 1))
                    else:
                        pe.wait_ge(conv_done, st.n(4, t - 1))
                for n in range(4 * part, 4 * part + 4):
                    k, w, h = n // 3, (s.w_hi, s.w_hi, s.w_lo)[n % 3], (s.h_hi, s.h_lo, s.h_hi)[n % 3]
                    ins = pe.matmul(A[t % 2][:, :], w[:, t, k, :], h[:, st.b, k, :], start=(n == 0), stop=(n == 11))
                if part == 2:
                    ins.then_inc(in_done, 1)

            def decays(st, c, sl):
                q, hh = sl // 2, sl % 2
                if sl == 0:
                    pe.wait_ge(rl_ready[c % 2], st.n(2 * 160, (c // 2 + 1) * 160))
                wait(pe, exp_done, st.n(16, 4 * c + sl - 1))
                pe.matmul(DB[sl % 2][:, :], s.Lm[:, c % 2, q, :], s.R[:, c % 2, q, hh * 512:(hh + 1) * 512],
                          start=True, stop=True).then_inc(d_done, 1)

            def prepare(st, c):
                if c == 0:
                    pe.wait_ge(silu_done, st.n(6, 4))
                wait(pe, gm_done, st.n(4, c))
                for q in range(2):
                    pe.transpose(GB[:, q * P:(q + 1) * P], xs[:, st.par, q, tok(c)], s.ident[:, :])
                pe.matmul(GB[:, 256:512], Bt[:, st.par, tok(c)], Ct[:, st.par, :, tok(c)],
                          start=True, stop=True).then_inc(prep_done, 1)
                if c < 3:
                    wait(pe, s_new, st.n(3, c))
                    pe.transpose(SB[:, 0:P], Bt[:, st.par, tok(c)], s.ident[:, :]).then_inc(bt_done, 1)

            def weights(gp, n):
                t, hh = n // 2, n % 2
                if hh == 0:
                    pe.wait_ge(wraw_ready[t % 2], gp * 48 + 16 * (t // 2 + 1))
                for k in range(2):
                    ins = pe.transpose(SB[:, 256 + k * P:256 + (k + 1) * P],
                                       wraw[:, t % 2, (2 * hh + k) * P:(2 * hh + k + 1) * P], s.ident[:, :])
                ins.then_inc(w_pe, 1)

            def step(st):
                nx = st.next()
                for k in range(16):
                    c, sl = k // 4, k % 4
                    stn, cn = nxt(st, c)
                    if sl == 0:
                        wait(pe, y1_done, st.n(4, c - 1))
                    if sl == 0 and c > 0:
                        pe.wait_ge(s_new, st.n(3, c))
                        pe.matmul(YB[c % 2][:, 256:512], S[:, :], Ct[:, st.par, :, tok(c)],
                                  start=True, stop=True).then_inc(yo_done, 1)
                    if ahead(st) or c < 3:
                        decays(stn, cn, sl)
                    pe.wait_ge(m_done, st.n(16, 4 * c + sl + 1))
                    if sl == 0:
                        pe.wait_ge(xp_done, st.n(4, c + 1))
                    q = sl // 2
                    for hh in range(4):
                        h = 4 * (sl % 2) + hh
                        j = h // 2
                        ins = pe.matmul(YB[c % 2][32 * j:32 * j + 32, q * Q:(q + 1) * Q], Xp[:, c % 2, q * HG + h, :],
                                        M[:, sl, hh * Q:(hh + 1) * Q], start=(h % 2 == 0), stop=(h % 2 == 1))
                    ins.then_inc(yd_done, 1)
                    if ahead(st):
                        for m in GROUPS[k]:
                            project(nx, m)
                    if sl == 0 and c < 3:
                        pe.wait_ge(xw_done, st.n(3, c + 1))
                        pe.wait_ge(bt_read, st.n(3, c + 1))
                        if halves_before(st.b, k) and not last(st):
                            pe.wait_ge(w_copied, st.gp * 12 + halves_before(st.b, k))
                        for q in range(2):
                            ins = pe.matmul(SB[64 * q:64 * q + 64, P:2 * P], BTs[:, 64 * q:64 * q + 64], Xw[:, q, :],
                                            start=True, stop=True)
                        ins.then_inc(st_done, 1)
                    if sl == PREP and (ahead(st) or c < 3):
                        if halves_before(st.b, k) and not last(st):
                            pe.wait_ge(w_copied, st.gp * 12 + halves_before(st.b, k))
                        prepare(stn, cn)
                    n = halves_before(st.b, k)
                    if halves_before(st.b, k + 1) > n and not last(st):
                        pe.wait_ge(bt_read, st.n(3, bt_count(c, sl)))
                        wait(pe, s_new, st.n(3, min(c + 1, 3)))
                        wait(pe, w_copied, st.gp * 12 + n)
                        weights(st.gp, n)

            def bt_count(c, sl):
                own = min(c + 1, 3) if sl < PREP else min(c + 2, 3)
                return 4 if c == 3 and sl >= PREP else own

            for m in range(18):
                project(Step(0, 0), m)
            for sl in range(4):
                decays(Step(0, 0), 0, sl)
            prepare(Step(0, 0), 0)
            run(pe, step)

        @block.scalar
        def _(act):
            def linear(st, t):
                act.wait_ge(in_done, st.n(6, t + 1))
                wait(act, silu_done, st.n(6, t - 1))
                act.wait_ge(gcs_ready, st.gp + 1)
                o = t * (KS + 1)
                scale, bias = (gcs[:, o + KS - 1:o + KS], gcs[:, o + KS:o + KS + 1]) if t < 4 else (1.0, gcs[:, 16 + t:17 + t])
                act.activation(cv[:, t % 2, :], A[t % 2][:, :], ACT.Identity, scale=scale, bias=bias).then_inc(lin_done, 1)

            def tanh(st, t):
                if t < 4:
                    act.wait_ge(conv_done, st.n(4, t + 1))
                else:
                    act.wait_ge(lin_done, st.n(6, t + 1))
                act.activation(th[:, t % 2, :], cv[:, t % 2, :], ACT.Tanh, scale=0.5).then_inc(tanh_done, 1)

            def exponent(st, c, sl):
                act.wait_ge(d_done, st.n(16, 4 * c + sl + 1))
                wait(act, m_done, st.n(16, 4 * c + sl - 3))
                act.activation(E[:, sl, :], DB[sl % 2][:, :], ACT.Exp).then_inc(exp_done, 1)

            def spread(st, c):
                act.wait_ge(prep_done, st.n(4, c + 1))
                wait(act, yd_done, st.n(16, 4 * (c - 1)))
                wait(act, xw_done, st.n(3, c - 1) if c else st.n(3, 0))
                out = Xp[:, c % 2, :, :].rearrange("p (j e) (m d) -> p j (e m) d", e=2, d=HD)[:, :, 0:4:3, :]
                act.activation(out, GB[:, 0:256].rearrange("p (j e d) -> p j e d", e=2, d=HD), ACT.Copy)\
                   .then_inc(xp_done, 1)
                if c < 3:
                    act.wait_ge(bt_done, st.n(3, c + 1))
                    wait(act, st_done, st.n(3, c))
                    act.activation(BTs[:, :], SB[:, 0:P], ACT.Copy).then_inc(bt_read, 1)

            def step(st):
                nx = st.next()
                for k in range(16):
                    c, sl = k // 4, k % 4
                    stn, cn = nxt(st, c)
                    if ahead(st) or c < 3:
                        exponent(stn, cn, sl)
                    for t in range(NT):
                        if FS[t] + 1 == k and ahead(st):
                            tanh(nx, t)
                        if FS[t] + 1 == k + 16 and not first(st):
                            tanh(st, t)
                    for t in range(NT):
                        if FS[t] == k and ahead(st):
                            linear(nx, t)
                    if sl == PREP and (ahead(st) or c < 3):
                        spread(stn, cn)
                    n = halves_before(st.b, k)
                    if halves_before(st.b, k + 1) > n and not last(st):
                        act.wait_ge(w_pe, st.gp * 12 + n + 1)
                        wait(act, w_lo_done, st.gp * 12 + n - 1)
                        act.activation(s.w_hi[:, n // 2, 2 * (n % 2):2 * (n % 2) + 2, :],
                                       SB[:, 256:512].rearrange("p (k r) -> p k r", k=2), ACT.Copy).then_inc(w_hi_done, 1)
                        act.activation(wst[:, n % 2, :], SB[:, 256:512], ACT.Copy).then_inc(w_copied, 1)

            def first(st):
                return isinstance(st.gp, int) and st.gp == 0 and st.b == 0

            for t in range(NT):
                linear(Step(0, 0), t)
                tanh(Step(0, 0), t)
            act.wait_ge(zeroed, 1)
            for sl in range(4):
                exponent(Step(0, 0), 0, sl)
            spread(Step(0, 0), 0)
            run(act, step)

        @block.vector
        def _(dve):
            def convolve(st, t):
                dve.wait_ge(lin_done, st.n(6, t + 1))
                for k in range(KS - 2, -1, -1):
                    lag, o = KS - 1 - k, t * (KS + 1) + k
                    if lag > 1:
                        dve.wait_ge(tap_done, st.n(8, 2 * t + lag - 1))
                    ins = dve.scalar_tensor_tensor(out=cv[:, t % 2, lag:], in0=A[t % 2][:, 0:L - lag],
                                                   scalar=gcs[:, o:o + 1], in1=cv[:, t % 2, lag:],
                                                   op0=ALU.mult, op1=ALU.add)
                    ins.then_inc(conv_done if k == 0 else tap_done, 1)

            def silu(st, t):
                dve.wait_ge(tanh_done, st.n(6, t + 1))
                if t == 0:
                    wait(dve, y_out, st.n(1, -1))
                if t == 3:
                    for q in range(2):
                        n = slice(64 * q, 64 * q + 64)
                        ins = dve.scalar_tensor_tensor(out=Ct[n, st.par, q, :], in0=th[n, 1, :], scalar=1.0,
                                                       in1=cv[n, 1, :], op0=ALU.add, op1=ALU.mult)
                    ins.then_inc(silu_done, 1)
                    return
                dst = (xs[:, st.par, 0, :], xs[:, st.par, 1, :], Bt[:, st.par, :], None,
                       gate[:, st.par, 0, :], gate[:, st.par, 1, :])[t]
                dve.scalar_tensor_tensor(out=dst, in0=th[:, t % 2, :], scalar=1.0, in1=cv[:, t % 2, :],
                                         op0=ALU.add, op1=ALU.mult).then_inc(silu_done, 1)

            def causal(st, c):
                dve.wait_ge(xp_done, st.n(4, c + 1))
                wait(dve, m_done, st.n(16, 4 * c))
                dve.tensor_tensor(Gm[:, :, :], GB[:, 256:512].rearrange("p (q s) -> p q s", q=2),
                                  s.tri[:, :].unsqueeze(1).broadcast_to([P, 2, Q]), ALU.mult).then_inc(gm_done, 1)

            def mix(st, c, sl):
                dve.wait_ge(exp_done, st.n(16, 4 * c + sl + 1))
                dve.wait_ge(gm_done, st.n(4, c + 1))
                wait(dve, yd_done, st.n(16, 4 * c + sl - 3))
                dve.tensor_tensor(M[:, sl, :].rearrange("p (h s) -> p h s", h=4),
                                  E[:, sl, :].rearrange("p (h s) -> p h s", h=4),
                                  Gm[:, sl // 2, :].unsqueeze(1).broadcast_to([P, 4, Q]), ALU.mult).then_inc(m_done, 1)

            def collect(st, c):
                dve.wait_ge(yd_done, st.n(16, 4 * c + 4))
                own = YB[c % 2][:, 0:256].rearrange("p (q s) -> p q s", q=2)
                if c == 0:
                    wait(dve, y_out, st.n(1, -1))
                    dve.tensor_copy(y1[:, st.par, :, tok(c)], own).then_inc(y1_done, 1)
                    return
                dve.wait_ge(yo_done, st.n(3, c))
                dve.wait_ge(eb_ready[st.par], st_eb(st))
                dve.tensor_tensor(y1[:, st.par, :, tok(c)], YB[c % 2][:, 256:512].rearrange("p (q s) -> p q s", q=2),
                                  ea[:, st.par, :, tok(c)], ALU.mult).then_inc(yo_scaled, 1)
                dve.wait_ge(yo_scaled, st.n(3, c))
                dve.tensor_tensor(y1[:, st.par, :, tok(c)], own, y1[:, st.par, :, tok(c)], ALU.add).then_inc(y1_done, 1)

            def update(st, c):
                dve.wait_ge(st_done, st.n(3, c + 1))
                if c == 0:
                    wait(dve, yo_done, st.n(3, 0))
                    dve.tensor_copy(S[:, :], SB[:, P:2 * P]).then_inc(s_new, 1)
                    return
                dve.wait_ge(s_new, st.n(3, c))
                dve.tensor_tensor(S1[:, :].rearrange("p (h d) -> p h d", h=HG), S[:, :].rearrange("p (h d) -> p h d", h=HG),
                                  cd[:, st.gp, :, st.b * NC + c].unsqueeze(2).broadcast_to([P, HG, HD]),
                                  ALU.mult).then_inc(s_part, 1)
                dve.wait_ge(s_part, st.n(2, c))
                dve.wait_ge(yo_done, st.n(3, c))
                dve.tensor_tensor(S[:, :], S1[:, :], SB[:, P:2 * P], ALU.add).then_inc(s_new, 1)

            def step(st):
                nx = st.next()
                for k in range(16):
                    c, sl = k // 4, k % 4
                    stn, cn = nxt(st, c)
                    more = ahead(st) or c < 3
                    if sl == 0 and not (first(st) and c == 0):
                        collect(st, c - 1) if c else collect(st.prev(), 3)
                    if sl == 0 and c < 3:
                        update(st, c)
                    if sl == PREP + 1 and more:
                        causal(stn, cn)
                        mix(stn, cn, 0)
                        mix(stn, cn, 1)
                    if sl == PREP + 2 and more:
                        mix(stn, cn, 2)
                        mix(stn, cn, 3)
                    for t in range(NT):
                        if FS[t] + 2 == k and ahead(st):
                            silu(nx, t)
                        if FS[t] + 2 == k + 16 and not first(st):
                            silu(st, t)
                    for t in range(4):
                        if FS[t] == k and ahead(st):
                            convolve(nx, t)

            def first(st):
                return isinstance(st.gp, int) and st.gp == 0 and st.b == 0

            def st_eb(st):
                return st.gp * 128 + 64 * (st.b // 2 + 1)

            dve.memset(Ct[:, :, :, :], 0.0)
            dve.memset(Xp[:, :, :, :], 0.0).then_inc(zeroed, 1)
            dve.wait_ge(zeroed, 1)
            dve.wait_ge(gcs_ready, 1)
            for t in range(NT):
                if t < 4:
                    convolve(Step(0, 0), t)
                silu(Step(0, 0), t)
            dve.wait_ge(cd_ready, 32)
            causal(Step(0, 0), 0)
            for sl in range(4):
                mix(Step(0, 0), 0, sl)
            run(dve, step)
            collect(Step(GP - 1, 3), 3)

        @block.gpsimd
        def _(pool):
            def constants(gp):
                pool.tensor_copy(gcs[:, :], s.gpc[:, gp, :]).then_inc(gcs_ready, 1)

            def weigh(st, c):
                pool.wait_ge(xp_done, st.n(4, c + 1))
                wait(pool, st_done, st.n(3, c))
                src = Xp[:, c % 2, :, :].rearrange("p (j e) (m d) -> p j (e m) d", e=2, d=HD)[:, :, 0:4:3, :]
                w = s.wend[:, st.gp, st.b, c, :].rearrange("p (j e) -> p j e", e=2).unsqueeze(3).broadcast_to([P, HG, 2, HD])
                pool.tensor_tensor(Xw[:, :, :].rearrange("p q (j e d) -> p (q j) e d", e=2, d=HD), src, w,
                                   ALU.mult).then_inc(xw_done, 1)

            def skip(st):
                pool.wait_ge(silu_done, st.n(6, 2))
                pool.wait_ge(eb_ready[st.par], st.gp * 128 + 64 * (st.b // 2 + 1))
                wait(pool, y_stored, st.n(16, 0))
                pool.tensor_tensor(t1[:, :, :], xs[:, st.par, :, :], dd[:, st.par, :, :], ALU.mult).then_inc(t1_done, 1)

            def finish(st):
                pool.wait_ge(y1_done, st.n(4, 4))
                pool.wait_ge(t1_done, st.n(1, 1))
                pool.tensor_tensor(t1[:, :, :], t1[:, :, :], y1[:, st.par, :, :], ALU.add).then_inc(t2_done, 1)
                pool.wait_ge(t2_done, st.n(1, 1))
                pool.wait_ge(silu_done, st.n(6, 6))
                pool.tensor_tensor(t1[:, :, :], t1[:, :, :], gate[:, st.par, :, :], ALU.mult).then_inc(y_out, 1)

            def split(gp, n):
                w = slice(2 * (n % 2), 2 * (n % 2) + 2)
                src = wst[:, n % 2, :].rearrange("p (k r) -> p k r", k=2)
                pool.wait_ge(w_copied, gp * 12 + n + 1)
                pool.tensor_tensor(s.w_lo[:, n // 2, w, :], src, s.w_hi[:, n // 2, w, :].bitcast(F32),
                                   ALU.subtract).then_inc(w_lo_done, 1)

            def step(st):
                for c in range(NC):
                    if c == 0:
                        if st.b == 3 and not last(st):
                            pool.wait_ge(lin_done, st.n(6, 6))
                            pool.wait_ge(conv_done, st.n(4, 4))
                            constants(st.gp + 1)
                        if not (isinstance(st.gp, int) and st.gp == 0 and st.b == 0):
                            finish(st.prev())
                    stn, cn = nxt(st, c)
                    if cn < 3 and (ahead(st) or c < 3):
                        weigh(stn, cn)
                    if c == 2:
                        skip(st)
                    if not last(st):
                        for n in range(halves_before(st.b, 4 * c), halves_before(st.b, 4 * c + 4)):
                            split(st.gp, n)

            constants(0)
            weigh(Step(0, 0), 0)
            run(pool, step)
            finish(Step(GP - 1, 3))


def tail_part(nc, s, x, w_out, w_ffn, b_ffn, out):
    with ExitStack() as ctx:
        def sb(name, shape, dt=F32):
            return ctx.enter_context(nc.sbuf_tensor("t_" + name, shape, dt))

        def sem(name):
            return ctx.enter_context(nc.semaphore("t_" + name))

        KI, TT = DI // P, L // P
        wo_hi, wo_lo = sb("wo_hi", [P, KI, D], F32R), sb("wo_lo", [P, KI, D], F32R)
        sign = sb("sign", [P, KC, D], F32R)
        absw = sb("absw", [P, KC, D])
        sgt = sb("sgt", [P, D])
        ones = sb("ones", [P, P])
        half, eps = sb("half", [P, 1]), sb("eps", [P, 1])
        wo_raw, wf_raw = sb("wo_raw", [P, 2, DI]), sb("wf_raw", [P, 2, D])
        alpha, bias = sb("alpha", [P, D]), sb("bias", [P, D])
        ga, gb = sb("ga", [P, NB, D]), sb("gb", [P, NB, D])
        gsc, gbias = sb("gsc", [P, NB, D]), sb("gbias", [P, NB, D])
        yt = sb("yt", [P, TT, KI, P])
        y_hi, y_lo = sb("y_hi", [P, 2, KI, P], F32R), sb("y_lo", [P, 2, KI, P], F32R)
        xt, x2 = sb("xt", [P, TT, D]), sb("x2", [P, TT, D])
        att, xn = sb("att", [P, 2, D]), sb("xn", [P, 2, D])
        st_, mv, rstd = sb("st", [P, 2, 6]), sb("mv", [P, 2, 2]), sb("rstd", [P, 2, 2])
        hf = sb("hf", [P, 2, KC, P])
        h_hi, h_lo = sb("h_hi", [P, 2, KC, P], F32R), sb("h_lo", [P, 2, KC, P], F32R)
        f1, o = sb("f1", [P, 2, D]), sb("o", [P, 2, D])
        OB, TB, FB, WB = s.bank[0:2], s.bank[2:4], s.bank[4:6], s.bank[6:8]

        d_wo, d_wf, d_y, d_x, d_out = (
            [sem(f"{n}{i}") for i in range(m)] for n, m in (("d_wo", 2), ("d_wf", 2), ("d_y", 4), ("d_x", 4), ("d_out", 2)))
        d_g, konst = sem("d_g"), sem("konst")
        w_pe, w_act, w_dve, sg_half = sem("w_pe"), sem("w_act"), sem("w_dve"), sem("sg_half")
        al_pe, al_done, g_done = sem("al_pe"), sem("al_done"), sem("g_done")
        yhi_done, ylo_done, op_done = sem("yhi_done"), sem("ylo_done"), sem("op_done")
        gated, x2_done, bn_done, st_done, eps_done, rs_done, xn_done = (
            sem(n) for n in ("gated", "x2_done", "bn_done", "st_done", "eps_done", "rs_done", "xn_done"))
        tr_done, hf_done, hhi_done, hlo_done, ffn_done, f1_done, res_done, o_done = (
            sem(n) for n in ("tr_done", "hf_done", "hhi_done", "hlo_done", "ffn_done", "f1_done", "res_done", "o_done"))
        block = ctx.enter_context(nc.Block())
        NW = 8 + 4

        def run(eng, step):
            for t in range(TT):
                step(Step(0, t))
            with eng.Fori(1, NB - 1) as b:
                for t in range(TT):
                    step(Step(b, t))
            for t in range(TT):
                step(Step(NB - 1, t))

        def is_last(st):
            return isinstance(st.gp, int) and st.gp == NB - 1 and st.b == TT - 1

        def two_more(st):
            return not (isinstance(st.gp, int) and st.gp == NB - 1 and st.b >= TT - 2)

        def two_back(st):
            return not (isinstance(st.gp, int) and st.gp == 0 and st.b < 2)

        def is_first(st):
            return isinstance(st.gp, int) and st.gp == 0 and st.b == 0

        @block.sync
        def _(sp):
            y_v = s.y_d.rearrange("(k p) (b t n) -> b t p k n", p=P, b=NB, t=TT)
            x_v = x.rearrange("b (t p) d -> b t p d", p=P)
            o_v = out.rearrange("b (t p) d -> b t p d", p=P)

            def load(st):
                sp.dma_start(yt[:, st.b, :, :], y_v[st.gp, st.b]).then_inc(d_y[st.b], 16)
                sp.dma_start(xt[:, st.b, :], x_v[st.gp, st.b]).then_inc(d_x[st.b], 16)

            def store(st):
                sp.wait_ge(o_done, st.n(1, 1))
                sp.dma_start(o_v[st.gp, st.b], o[:, st.b % 2, :]).then_inc(d_out[st.b % 2], 16)

            def step(st):
                if not (isinstance(st.gp, int) and st.gp == NB - 1):
                    sp.wait_ge(ylo_done, st.n(1, 1))
                    sp.wait_ge(x2_done, st.n(1, 1))
                    load(Step(st.gp + 1, st.b))
                if not is_first(st):
                    store(st.prev())

            for r in range(2):
                sp.dma_start(wo_raw[:, r, :], w_out[r * P:(r + 1) * P, :]).then_inc(d_wo[r], 16)
            load(Step(0, 0))
            for r in range(2, 4):
                sp.wait_ge(w_pe, 2 * r - 2)
                sp.dma_start(wo_raw[:, r % 2, :], w_out[r * P:(r + 1) * P, :]).then_inc(d_wo[r % 2], 16)
            load(Step(0, 1))
            for r in range(4):
                if r >= 2:
                    sp.wait_ge(w_pe, 8 + r - 1)
                sp.dma_start(wf_raw[:, r % 2, :], w_ffn[r * P:(r + 1) * P, :]).then_inc(d_wf[r % 2], 16)
            for t in range(2, TT):
                load(Step(0, t))
            run(sp, step)
            store(Step(NB - 1, TT - 1))
            for i in range(2):
                sp.wait_ge(d_out[i], 16 * NB * TT // 2)

        @block.scalar
        def _(act):
            for b in range(NB):
                act.dma_start(ga[:, b, :], s.g_d[0, b:b + 1, :].broadcast_to([P, D])).then_inc(d_g, 16)
                act.dma_start(gb[:, b, :], s.g_d[1, b:b + 1, :].broadcast_to([P, D])).then_inc(d_g, 16)
            act.dma_start(bias[:, :], b_ffn.rearrange("(o n) -> o n", o=1).broadcast_to([P, D])).then_inc(d_g, 16)

            def split(st):
                act.wait_ge(d_y[st.b], st.gp * 16 + 16)
                wait(act, op_done, st.n(1, -1))
                act.activation(y_hi[:, st.b % 2, :, :], yt[:, st.b, :, :], ACT.Copy).then_inc(yhi_done, 1)

            def step(st):
                act.wait_ge(ylo_done, st.n(1, 1))
                if two_more(st):
                    split(st.next().next())
                act.wait_ge(w_act, NW)
                act.wait_ge(tr_done, st.n(1, 1))
                wait(act, hlo_done, st.n(1, -1))
                for k in range(KC):
                    ins = act.activation(hf[:, st.b % 2, k, :], TB[st.b % 2][:, k * P:(k + 1) * P], ACT.Identity,
                                         scale=s.mod_t[:, 2, k, st.gp].unsqueeze(1), bias=s.mod_t[:, 3, k, st.gp].unsqueeze(1))
                ins.then_inc(hf_done, 1)

            for n in range(8):
                r, hh = n // 2, n % 2
                act.wait_ge(w_pe, n + 1)
                act.activation(wo_hi[:, 4 * hh:4 * hh + 4, r * P:(r + 1) * P],
                               WB[hh][:, :].rearrange("p (k e) -> p k e", k=4), ACT.Copy).then_inc(w_act, 1)
            split(Step(0, 0))
            split(Step(0, 1))
            for r in range(4):
                act.wait_ge(w_pe, 8 + r + 1)
                act.activation(absw[:, :, r * P:(r + 1) * P], WB[r % 2][:, :].rearrange("p (k e) -> p k e", k=4),
                               ACT.Abs).then_inc(w_act, 1)
            run(act, step)

        @block.gpsimd
        def _(pool):
            pool.memset(ones[:, :], 1.0).then_inc(konst, 1)
            pool.memset(half[:, :], -0.5).then_inc(konst, 1)
            pool.memset(eps[:, :], EPS).then_inc(konst, 1)

            def split(st):
                pool.wait_ge(yhi_done, st.n(1, 1))
                pool.tensor_tensor(y_lo[:, st.b % 2, :, :], yt[:, st.b, :, :], y_hi[:, st.b % 2, :, :].bitcast(F32),
                                   ALU.subtract).then_inc(ylo_done, 1)

            def step(st):
                pool.wait_ge(st_done, st.n(1, 1))
                pool.tensor_tensor(rstd[:, st.b % 2, 0:1], mv[:, st.b % 2, 1:2], eps[:, :], ALU.add).then_inc(eps_done, 1)
                pool.wait_ge(eps_done, st.n(1, 1))
                pool.tensor_tensor(rstd[:, st.b % 2, 1:2], rstd[:, st.b % 2, 0:1], half[:, :], ALU.pow).then_inc(rs_done, 1)
                if two_more(st):
                    split(st.next().next())
                pool.wait_ge(g_done, 2)
                pool.wait_ge(x2_done, st.n(1, 1))
                wait(pool, o_done, st.n(1, -1))
                pool.tensor_tensor(f1[:, st.b % 2, :], x2[:, st.b, :], gbias[:, st.gp, :], ALU.add).then_inc(res_done, 1)

            pool.wait_ge(konst, 3)
            split(Step(0, 0))
            split(Step(0, 1))
            pool.wait_ge(d_g, 16 * 9)
            pool.wait_ge(al_done, 1)
            pool.tensor_tensor(gsc[:, :, :], gb[:, :, :], alpha[:, :].unsqueeze(1).broadcast_to([P, NB, D]),
                               ALU.mult).then_inc(g_done, 1)
            pool.tensor_tensor(gbias[:, :, :], gb[:, :, :], bias[:, :].unsqueeze(1).broadcast_to([P, NB, D]),
                               ALU.mult).then_inc(g_done, 1)
            pool.wait_ge(g_done, 2)
            run(pool, step)

        @block.vector
        def _(dve):
            def residual(st):
                dve.wait_ge(op_done, st.n(1, 1))
                wait(dve, xn_done, st.n(1, -1))
                dve.wait_ge(d_x[st.b], st.gp * 16 + 16)
                dve.tensor_tensor(att[:, st.b % 2, :], OB[st.b % 2][:, :], ga[:, st.gp, :], ALU.mult).then_inc(gated, 1)
                dve.wait_ge(gated, st.n(1, 1))
                wait(dve, res_done, st.n(1, -3))
                dve.tensor_tensor(x2[:, st.b, :], att[:, st.b % 2, :], xt[:, st.b, :], ALU.add).then_inc(x2_done, 1)
                dve.wait_ge(x2_done, st.n(1, 1))
                dve.bn_stats(st_[:, st.b % 2, :], x2[:, st.b, :]).then_inc(bn_done, 1)
                dve.wait_ge(w_dve, NW)
                dve.wait_ge(bn_done, st.n(1, 1))
                wait(dve, rs_done, st.n(1, -1))
                dve.bn_aggr(mv[:, st.b % 2, :], st_[:, st.b % 2, :]).then_inc(st_done, 1)

            def normalize(st):
                dve.wait_ge(rs_done, st.n(1, 1))
                wait(dve, tr_done, st.n(1, -1))
                dve.tensor_scalar(xn[:, st.b % 2, :], x2[:, st.b, :], mv[:, st.b % 2, 0:1], rstd[:, st.b % 2, 1:2],
                                  ALU.subtract, ALU.mult).then_inc(xn_done, 1)

            def split(st):
                dve.wait_ge(hf_done, st.n(1, 1))
                wait(dve, ffn_done, st.n(1, -1))
                dve.tensor_copy(h_hi[:, st.b % 2, :, :], hf[:, st.b % 2, :, :]).then_inc(hhi_done, 1)
                dve.wait_ge(hhi_done, st.n(1, 1))
                dve.tensor_tensor(h_lo[:, st.b % 2, :, :], hf[:, st.b % 2, :, :], h_hi[:, st.b % 2, :, :].bitcast(F32),
                                  ALU.subtract).then_inc(hlo_done, 1)

            def finish(st):
                dve.wait_ge(ffn_done, st.n(1, 1))
                if st.b >= 2:
                    dve.wait_ge(d_out[st.b % 2], st.gp * 32 + 16)
                elif not (isinstance(st.gp, int) and st.gp == 0):
                    dve.wait_ge(d_out[st.b % 2], st.gp * 32)
                dve.tensor_tensor(o[:, st.b % 2, :], FB[st.b % 2][:, :], gsc[:, st.gp, :], ALU.mult).then_inc(f1_done, 1)
                dve.wait_ge(f1_done, st.n(1, 1))
                dve.wait_ge(res_done, st.n(1, 1))
                dve.tensor_tensor(o[:, st.b % 2, :], o[:, st.b % 2, :], f1[:, st.b % 2, :], ALU.add).then_inc(o_done, 1)

            def step(st):
                residual(st)
                if two_back(st):
                    finish(st.prev().prev())
                normalize(st)
                if not is_first(st):
                    split(st.prev())

            for n in range(8):
                r, hh = n // 2, n % 2
                dve.wait_ge(w_act, n + 1)
                w = wo_hi[:, 4 * hh:4 * hh + 4, r * P:(r + 1) * P]
                dve.tensor_tensor(wo_lo[:, 4 * hh:4 * hh + 4, r * P:(r + 1) * P],
                                  WB[hh][:, :].rearrange("p (k e) -> p k e", k=4), w.bitcast(F32),
                                  ALU.subtract).then_inc(w_dve, 1)
            for r in range(4):
                dve.wait_ge(w_act, 8 + r + 1)
                wait(dve, w_dve, 8 + r)
                dve.tensor_scalar(sgt[:, :], WB[r % 2][:, :], 0.0, 2.0, ALU.is_ge, ALU.mult).then_inc(sg_half, 1)
                dve.wait_ge(sg_half, r + 1)
                dve.tensor_scalar(sign[:, :, r * P:(r + 1) * P], sgt[:, :].rearrange("p (k e) -> p k e", k=4),
                                  -1.0, None, ALU.add).then_inc(w_dve, 1)
            dve.wait_ge(al_pe, 1)
            dve.tensor_scalar(alpha[:, :], FB[0][:, :], 1.0 / D, None, ALU.mult).then_inc(al_done, 1)
            dve.wait_ge(g_done, 2)
            run(dve, step)
            finish(Step(NB - 1, TT - 2))
            split(Step(NB - 1, TT - 1))
            finish(Step(NB - 1, TT - 1))

        @block.tensor
        def _(pe):
            def project(st):
                pe.wait_ge(ylo_done, st.n(1, 1))
                wait(pe, gated, st.n(1, -1))
                i = st.b % 2
                for k in range(KI):
                    for n, (y, w) in enumerate(((y_hi, wo_hi), (y_lo, wo_hi), (y_hi, wo_lo))):
                        ins = pe.matmul(OB[i][:, :], y[:, i, k, :], w[:, k, :], start=(k == 0 and n == 0),
                                        stop=(k == KI - 1 and n == 2))
                ins.then_inc(op_done, 1)

            def turn(st):
                i = st.b % 2
                pe.wait_ge(xn_done, st.n(1, 1))
                wait(pe, hf_done, st.n(1, -1))
                for k in range(KC):
                    ins = pe.transpose(TB[i][:, k * P:(k + 1) * P], xn[:, i, k * P:(k + 1) * P], s.ident[:, :])
                ins.then_inc(tr_done, 1)

            def linear(st):
                i = st.b % 2
                pe.wait_ge(hlo_done, st.n(1, 1))
                wait(pe, f1_done, st.n(1, -1))
                for k in range(KC):
                    for n, h in enumerate((h_hi, h_lo)):
                        ins = pe.matmul(FB[i][:, :], h[:, i, k, :], sign[:, k, :], start=(k == 0 and n == 0),
                                        stop=(k == KC - 1 and n == 1))
                ins.then_inc(ffn_done, 1)

            def step(st):
                if not is_last(st):
                    project(st.next())
                turn(st)
                if not is_first(st):
                    linear(st.prev())

            for n in range(NW):
                r, hh = (n // 2, n % 2) if n < 8 else (n - 8, n % 2)
                if n < 8:
                    pe.wait_ge(d_wo[r % 2], 16 * (r // 2 + 1))
                else:
                    pe.wait_ge(d_wf[r % 2], 16 * (r // 2 + 1))
                if n >= 2:
                    pe.wait_ge(w_dve, n - 1)
                src = wo_raw[:, r % 2, hh * 512:(hh + 1) * 512] if n < 8 else wf_raw[:, r % 2, :]
                for k in range(4):
                    ins = pe.transpose(WB[n % 2][:, k * P:(k + 1) * P], src[:, k * P:(k + 1) * P], s.ident[:, :])
                ins.then_inc(w_pe, 1)
            pe.wait_ge(konst, 3)
            pe.wait_ge(w_act, NW)
            for k in range(KC):
                ins = pe.matmul(FB[0][:, :], ones[:, :], absw[:, k, :], start=(k == 0), stop=(k == KC - 1))
            ins.then_inc(al_pe, 1)
            pe.wait_ge(w_dve, NW)
            pe.wait_ge(al_done, 1)
            project(Step(0, 0))
            run(pe, step)
            linear(Step(NB - 1, TT - 1))


_INS = ['L0_attn_input_', 'L0_attn_in_proj_w', 'L0_attn_conv1d_weight', 'L0_attn_conv1d_bias', 'L0_attn_z_bias',
        'L0_attn_D', 'L0_attn_out_proj_w', 'L0_ffn_weight', 'L0_ffn_bias', 'L0_c', 'L0_wmod']
_OUTS = [((NB, L, D), 'float32')]


def kernel(**inputs):
    import numpy as _np
    import concourse.bacc as _bacc
    from concourse import mybir as _mybir
    from concourse.bass_utils import run_bass_kernel_spmd as _run

    nc = _bacc.Bacc("TRN2", target_bir_lowering=False, num_devices=1)
    arrays, args = {}, {}
    for name in _INS:
        a = _np.ascontiguousarray(inputs[name])
        arrays[f"in_{name}_dram"] = a
        args[name] = nc.dram_tensor(f"in_{name}_dram", a.shape, _mybir.dt.from_np(a.dtype), kind="ExternalInput").ap()
    for i, (shape, dtype) in enumerate(_OUTS):
        dt = _mybir.dt.from_np(_np.dtype(dtype))
        out = nc.dram_tensor(f"out_{i}_dram", shape, dt, kind="ExternalOutput").ap()
    adaln_kernel(nc, args['L0_attn_input_'], args['L0_attn_in_proj_w'], args['L0_attn_conv1d_weight'],
                 args['L0_attn_conv1d_bias'], args['L0_attn_z_bias'], args['L0_attn_D'], args['L0_attn_out_proj_w'],
                 args['L0_ffn_weight'], args['L0_ffn_bias'], args['L0_c'], args['L0_wmod'], out)
    r = _run(nc, [arrays], core_ids=[0])
    got = tuple(r.results[0][f"out_{i}_dram"] for i in range(len(_OUTS)))
    return got[0]
```

```python
from contextlib import ExitStack

import concourse.bass as bass
from concourse import mybir

F32 = mybir.dt.float32
F32R = mybir.dt.float32r
ALU = mybir.AluOpType
ACT = mybir.ActivationFunctionType

P = 128
NB, L, D = 4, 512, 512
DI, NG, NS, NH = 1024, 8, 64, 64
HD = DI // NH
HG = NH // NG
KC = D // P
Q = 128
NC = L // Q
GP = NG // 2
NT = 6
KS = 4
BIG = 16384.0
DT_MAX = 87.0
EPS = 1e-5

R_MASK, R_NEG, R_POS, R_ALL = 0, 64, 80, 96

GROUPS = [[0, 1], [2, 3]] + [[m] for m in range(4, 18)]
FS = [1, 3, 6, 9, 12, 15]
W_SLOT = [6, 7, 10, 11, 14, 15, 18, 19, 22, 23, 26, 27]
PREP = 1


class Step:

    def __init__(self, gp, b):
        self.gp, self.b = gp, b

    def n(self, per_step, off):
        return self.gp * (4 * per_step) + (per_step * self.b + off)

    def next(self):
        return Step(self.gp, self.b + 1) if self.b < 3 else Step(self.gp + 1, 0)

    def prev(self):
        return Step(self.gp, self.b - 1) if self.b else Step(self.gp - 1, 3)

    @property
    def par(self):
        return self.b % 2


def wait(eng, sem, count):
    if not isinstance(count, int) or count > 0:
        eng.wait_ge(sem, count)


class Shared:
    pass


def adaln_kernel(nc, x, w_in, conv_w, conv_b, z_bias, d_skip, w_out, w_ffn, b_ffn, cond, w_mod, out):
    with ExitStack() as ctx:
        s = Shared()

        def sb(name, shape, dt=F32):
            return ctx.enter_context(nc.sbuf_tensor(name, shape, dt))

        s.bank = [ctx.enter_context(nc.psum_tensor(f"bank{i}", [P, 512], F32)) for i in range(8)]
        s.ident = sb("ident", [P, P])
        s.tri = sb("tri", [P, P])
        s.mod_t = sb("mod_t", [P, 4, KC, NB])
        s.y_d = nc.dram_tensor("y_scratch", (NG * P, NB * L), F32).ap()
        s.ea_d = nc.dram_tensor("ea_scratch", (NB * NH, L), F32).ap()
        s.dd_d = nc.dram_tensor("dd_scratch", (NB * NH, L), F32).ap()
        s.a_d = nc.dram_tensor("a_scratch", (2, NB * NH, L), F32).ap()
        s.na_d = nc.dram_tensor("na_scratch", (2, NB * NH, L), F32).ap()
        s.cd_d = nc.dram_tensor("cd_scratch", (NH, NB * NC), F32).ap()
        s.g_d = nc.dram_tensor("gate_scratch", (2, NB, D), F32).ap()
        with ExitStack() as main_ctx:
            def sbm(name, shape, dt=F32):
                return main_ctx.enter_context(nc.sbuf_tensor(name, shape, dt))

            s.h_hi = sbm("h_hi", [P, NB, KC, L], F32R)
            s.h_lo = sbm("h_lo", [P, NB, KC, L], F32R)
            s.w_hi = sbm("w_hi", [P, NT, KC, P], F32R)
            s.w_lo = sbm("w_lo", [P, NT, KC, P], F32R)
            s.R = sbm("R", [R_ALL, 2, 2, HG * Q], F32R)
            s.Lm = sbm("Lm", [R_ALL, 2, 2, Q], F32R)
            s.wend = sbm("wend", [P, GP, NB, NC, 2 * HG])
            s.gpc = sbm("gpc", [P, GP, 4 * (KS + 1) + 2])
            prologue(nc, s, x, w_in, conv_w, conv_b, z_bias, d_skip, cond, w_mod)
            main_part(nc, s, w_in)
        tail_part(nc, s, x, w_out, w_ffn, b_ffn, out)


def tile_rows(gp, t):
    if t < 2:
        return (2 * gp + t) * P
    if t < 4:
        return gp * P + (DI if t == 2 else DI + NG * NS)
    return (2 * gp + t - 4) * P + DI + 2 * NG * NS


def prologue(nc, s, x, w_in, conv_w, conv_b, z_bias, d_skip, cond, w_mod):
    with ExitStack() as ctx:
        def sb(name, shape, dt=F32):
            return ctx.enter_context(nc.sbuf_tensor("p_" + name, shape, dt))

        def sem(name):
            return ctx.enter_context(nc.semaphore("p_" + name))

        scT = sb("scT", [P, KC, NB])
        wm = sb("wm", [P, 2, KC, D])
        xt, xn = sb("xt", [P, 4, D]), sb("xn", [P, 2, D])
        st, mv, rstd = sb("st", [P, 2, 6]), sb("mv", [P, 2, 2]), sb("rstd", [P, 2, 2])
        half = sb("half", [P, 1])
        hf = sb("hf", [P, 2, L])
        stage = sb("stage", [R_ALL, HG * Q])
        lstage = sb("lstage", [R_ALL, Q])
        wa_hi, wa_lo = sb("wa_hi", [P, KC, 192], F32R), sb("wa_lo", [P, KC, 192], F32R)
        wraw, wst = sb("wraw", [P, 2, D]), sb("wst", [P, 2, 2 * P])
        rows, rabs, rsg = sb("rows", [NB, 2, D]), sb("rabs", [NB, 2, D]), sb("rsg", [NB, 2, D])
        c4, th4, sc4 = rsg[:, 0, :], rabs[:, 0, :], rabs[:, 1, :]
        chunk_on = sb("chunk_on", [P, L])
        dcol, dhalf = sb("dcol", [P, 1]), sb("dhalf", [P, 1])
        R_, E_, DEN, SV, TT_, PL, DT, TMP = [sb(f"a{i}", [P, 2, L]) for i in range(8)]
        cde = sb("cde", [P, 2, NC])
        wa_raw = TMP[0:NH, 0, :]

        d_c, d_wa, d_small, d_scr, d_gate = sem("d_c"), sem("d_wa"), sem("d_small"), sem("d_scr"), sem("d_gate")
        d_x, d_wm, d_w = [sem(f"d_x{i}") for i in range(4)], [sem(f"d_wm{i}") for i in range(2)], [sem(f"d_w{i}") for i in range(2)]
        konst, kcopy = sem("konst"), sem("kcopy")
        sc_ready, sct_pe, sct_ready = sem("sc_ready"), sem("sct_pe"), sem("sct_ready")
        th_ready, mod_pe, mod_ready = sem("th_ready"), sem("mod_pe"), sem("mod_ready")
        gate_abs, gate_v, gate_ready = sem("gate_abs"), sem("gate_v"), sem("gate_ready")
        ln_bn, ln_st, ln_eps, ln_rs, ln_n = sem("ln_bn"), sem("ln_st"), sem("ln_eps"), sem("ln_rs"), sem("ln_n")
        t_pe, h_hi, h_act = sem("t_pe"), sem("h_hi"), sem("h_act")
        h_lo = [sem("h_lo_pool"), sem("h_lo_dve")]
        wa_pe, wa_act, wa_dve, dh_ready = sem("wa_pe"), sem("wa_act"), sem("wa_dve"), sem("dh_ready")
        wt_pe, w_act, w_pool = sem("wt_pe"), sem("w_act"), sem("w_pool")
        a_pe, a_act, a_v, a_pool, we_pe, we_ev = sem("a_pe"), sem("a_act"), sem("a_v"), sem("a_pool"), sem("we_pe"), sem("we_ev")
        N_SMALL = 10 + 2
        A_SUM, A_END, A_DD, A_LO, A_ALL = 17, 18, 20, 21, 21
        B_ABS, B_EXP, B_HI, B_EA, B_CD, B_WE, B_NEG, B_ALL = 1, 2, 3, 4, 5, 6, 7, 7
        SEC = [1, 0, 4, 3, 2, 5]
        MOD, DTB, GATE, WB, WE = (s.bank[6], s.bank[2]), s.bank[0:2], s.bank[3:5], s.bank[5:7], (s.bank[7], s.bank[0])
        block = ctx.enter_context(nc.Block())

        @block.sync
        def _(sp):
            wmv = w_mod.rearrange("(k p) n -> p k n", p=P)
            xv = x.rearrange("b (t p) d -> (b t) p d", p=P)

            def load_x(i):
                if i >= 4:
                    sp.wait_ge(ln_n, i - 3)
                sp.dma_start(xt[:, i % 4, :], xv[i]).then_inc(d_x[i % 4], 16)

            def load_section(n):
                if n >= 2:
                    sp.wait_ge(mod_pe, n - 1)
                sp.dma_start(wm[:, n % 2, :, :], wmv[:, :, SEC[n] * D:(SEC[n] + 1) * D]).then_inc(d_wm[n % 2], 16)

            def load_weights(t):
                if t >= 2:
                    sp.wait_ge(wt_pe, 2 * (t - 2) + 2)
                sp.dma_start(wraw[:, t % 2, :], w_in[tile_rows(0, t):tile_rows(0, t) + P, :]).then_inc(d_w[t % 2], 16)

            sp.dma_start(c4, cond).then_inc(d_c, 16)
            load_section(0)
            load_x(0)
            load_x(1)
            load_section(1)
            load_x(2)
            load_x(3)
            sp.dma_start(wa_raw, w_in[2 * DI + 2 * NG * NS:, :]).then_inc(d_wa, 16)
            for i in range(4, 16):
                load_x(i)
            load_section(2)
            load_section(3)
            for t in range(NT):
                load_weights(t)
            load_section(4)
            load_section(5)
            for pb in range(2):
                rows2 = slice(pb * P, pb * P + P)
                sp.wait_ge(a_v, A_ALL * pb + A_DD)
                sp.dma_start(s.dd_d[rows2, :], DEN[:, pb, :]).then_inc(d_scr, 16)
                sp.wait_ge(a_v, A_ALL * pb + A_LO)
                sp.dma_start(s.a_d[0, rows2, :], E_[:, pb, :]).then_inc(d_scr, 16)
                sp.dma_start(s.a_d[1, rows2, :], SV[:, pb, :]).then_inc(d_scr, 16)
                sp.wait_ge(a_act, B_ALL * pb + B_NEG)
                sp.dma_start(s.na_d[0, rows2, :], R_[:, pb, :]).then_inc(d_scr, 16)
                sp.wait_ge(a_pool, 2 * pb + 2)
                sp.dma_start(s.na_d[1, rows2, :], DT[:, pb, :]).then_inc(d_scr, 16)
                sp.dma_start(s.ea_d[rows2, :], TT_[:, pb, :]).then_inc(d_scr, 16)
                for q in range(2):
                    b = 2 * pb + q
                    with nc.allow_non_contiguous_dma(reason="a few decays per head"):
                        sp.dma_start(s.cd_d[:, b * NC:(b + 1) * NC], cde[64 * q:64 * q + 64, pb, :]).then_inc(d_scr, 16)
            sp.wait_ge(gate_ready, 2)
            sp.dma_start(s.g_d.rearrange("g b d -> b g d"), rows[:, :, :]).then_inc(d_gate, 16)
            sp.wait_ge(d_scr, 16 * 16)
            sp.wait_ge(d_gate, 16)

        @block.gpsimd
        def _(pool):
            pool.memset(half[:, :], -0.5).then_inc(konst, 1)
            pool.wait_ge(konst, 1)
            pool.memset(s.ident[:, :], 0.0).then_inc(konst, 1)
            pool.wait_ge(konst, 2)
            pool.affine_select(out=s.ident[:, :], in_=s.ident[:, :], compare_op=ALU.not_equal, fill=1.0,
                               base=0, pattern=[[-1, P]], channel_multiplier=1).then_inc(konst, 1)
            pool.wait_ge(konst, 3)
            pool.memset(wa_hi[:, :, :].bitcast(F32), 0.0).then_inc(konst, 1)
            pool.wait_ge(konst, 4)
            pool.memset(wa_lo[:, :, :].bitcast(F32), 0.0).then_inc(konst, 1)

            def low_part(n):
                b, k = n // KC, n % KC
                pool.wait_ge(h_act, n + 1)
                pool.tensor_tensor(s.h_lo[:, b, k, :], hf[:, n % 2, :], s.h_hi[:, b, k, :].bitcast(F32),
                                   ALU.subtract).then_inc(h_lo[0], 1)

            def decay_constants():
                pool.memset(s.tri[:, :], 0.125).then_inc(konst, 1)
                pool.wait_ge(konst, 6)
                pool.memset(stage[:, :], 0.0).then_inc(konst, 1)
                pool.wait_ge(konst, 7)
                pool.memset(lstage[0:64, :], 0.0).then_inc(konst, 1)
                pool.wait_ge(konst, 8)
                pool.memset(lstage[64:96, :], 1.0).then_inc(konst, 1)
                pool.wait_ge(konst, 9)
                pool.memset(chunk_on[:, :], 1.0).then_inc(konst, 1)
                pool.wait_ge(konst, 10)
                pool.affine_select(out=s.tri[:, :], in_=s.tri[:, :], compare_op=ALU.is_ge, fill=0.0,
                                   base=0, pattern=[[1, P]], channel_multiplier=-1).then_inc(konst, 1)
                mrow = stage[0:64, :].rearrange("p (h s) -> p h s", h=HG)
                pool.wait_ge(konst, 11)
                pool.affine_select(out=mrow, in_=mrow, compare_op=ALU.is_ge, fill=-BIG,
                                   base=0, pattern=[[0, HG], [1, Q]], channel_multiplier=-2).then_inc(konst, 1)
                lrow = lstage[0:64, :].rearrange("p (z r) -> p z r", r=2)
                pool.wait_ge(konst, 12)
                pool.affine_select(out=lrow, in_=lrow, compare_op=ALU.not_equal, fill=1.0,
                                   base=0, pattern=[[-1, Q // 2], [0, 2]], channel_multiplier=1).then_inc(konst, 1)
                drow = stage[64:80, :].rearrange("p (h s) -> p h s", h=HG)
                pool.wait_ge(konst, 13)
                pool.affine_select(out=drow, in_=drow, compare_op=ALU.not_equal, fill=1.0,
                                   base=0, pattern=[[-1, HG], [0, Q]], channel_multiplier=1).then_inc(konst, 1)
                pool.wait_ge(konst, 14)
                pool.affine_select(out=drow, in_=drow, compare_op=ALU.not_equal, fill=1.0,
                                   base=-HG, pattern=[[-1, HG], [0, Q]], channel_multiplier=1).then_inc(konst, 1)
                cmv = chunk_on[:, :].rearrange("p (c q) -> p c q", q=Q)
                pool.wait_ge(konst, 15)
                pool.affine_select(out=cmv, in_=cmv, compare_op=ALU.not_equal, fill=0.0,
                                   base=0, pattern=[[0, NC], [1, Q]], channel_multiplier=0).then_inc(konst, 1)

            for i in range(16 + 5):
                if i < 16:
                    pool.wait_ge(ln_st, i + 1)
                    if i >= 2:
                        pool.wait_ge(ln_n, i - 1)
                    pool.tensor_scalar(rstd[:, i % 2, 0:1], mv[:, i % 2, 1:2], EPS, None, ALU.add).then_inc(ln_eps, 1)
                    pool.wait_ge(ln_eps, i + 1)
                    pool.tensor_tensor(rstd[:, i % 2, 1:2], rstd[:, i % 2, 0:1], half[:, :], ALU.pow).then_inc(ln_rs, 1)
                if i >= 5 and i % 2 == 1:
                    low_part(i - 5)
            pool.wait_ge(konst, 5)
            decay_constants()

            def scale(pb):
                pool.wait_ge(a_act, B_ALL * pb + B_EA)
                pool.tensor_scalar(TT_[:, pb, :], TT_[:, pb, :], 0.125, None, ALU.mult).then_inc(a_pool, 1)
                pool.wait_ge(a_v, A_ALL * pb + A_LO)
                pool.tensor_scalar(DT[:, pb, :], SV[:, pb, :], -1.0, None, ALU.mult).then_inc(a_pool, 1)

            def weights(n):
                t, w = n // 2, slice(2 * (n % 2), 2 * (n % 2) + 2)
                pool.wait_ge(w_act, n + 1)
                pool.tensor_tensor(s.w_lo[:, t, w, :], wst[:, n % 2, :].rearrange("p (k r) -> p k r", k=2),
                                   s.w_hi[:, t, w, :].bitcast(F32), ALU.subtract).then_inc(w_pool, 1)

            for pb in range(2):
                for n in range(NT * pb, NT * pb + NT):
                    weights(n)
                scale(pb)
            pool.wait_ge(d_small, 16 * N_SMALL)

        @block.vector
        def _(dve):
            dve.wait_ge(d_c, 16)
            dve.wait_ge(th_ready, 1)
            dve.scalar_tensor_tensor(out=sc4, in0=th4, scalar=1.0, in1=c4,
                                     op0=ALU.add, op1=ALU.mult).then_inc(sc_ready, 1)
            dve.wait_ge(sct_pe, 1)
            dve.tensor_scalar(scT[:, :, :], s.bank[4][:, 0:KC * NB].rearrange("p (k b) -> p k b", k=KC),
                              0.5, None, ALU.mult).then_inc(sct_ready, 1)

            def modulation(n):
                dve.wait_ge(mod_pe, n // 2 * 2 + 2)
                dve.tensor_scalar(s.mod_t[:, n, :, :],
                                  MOD[n // 2][:, n * KC * NB:(n + 1) * KC * NB].rearrange("p (k b) -> p k b", k=KC),
                                  1.0 - n % 2, None, ALU.add).then_inc(mod_ready, 1)

            def statistics(i):
                dve.wait_ge(d_x[i % 4], 16 * (i // 4 + 1))
                dve.bn_stats(st[:, i % 2, :], xt[:, i % 4, :]).then_inc(ln_bn, 1)
                dve.wait_ge(ln_bn, i + 1)
                if i >= 2:
                    dve.wait_ge(ln_rs, i - 1)
                    dve.wait_ge(ln_n, i - 1)
                dve.bn_aggr(mv[:, i % 2, :], st[:, i % 2, :]).then_inc(ln_st, 1)

            def normalize(i):
                dve.wait_ge(ln_rs, i + 1)
                if i >= 2:
                    dve.wait_ge(t_pe, i - 1)
                dve.tensor_scalar(xn[:, i % 2, :], xt[:, i % 4, :], mv[:, i % 2, 0:1], rstd[:, i % 2, 1:2],
                                  ALU.subtract, ALU.mult).then_inc(ln_n, 1)

            def low_part(n):
                b, k = n // KC, n % KC
                dve.wait_ge(h_act, n + 1)
                dve.tensor_tensor(s.h_lo[:, b, k, :], hf[:, n % 2, :], s.h_hi[:, b, k, :].bitcast(F32),
                                  ALU.subtract).then_inc(h_lo[1], 1)

            statistics(0)
            for i in range(16 + 5):
                if i < 15:
                    statistics(i + 1)
                if i >= 5 and i % 2 == 0:
                    low_part(i - 5)
                if i < 16:
                    normalize(i)
                if i == 3:
                    modulation(0)
                    modulation(1)
                    dve.wait_ge(wa_act, 1)
                    dve.tensor_tensor(wa_lo[:, :, 64:128], s.bank[5][:, 0:KC * NH].rearrange("p (k h) -> p k h", k=KC),
                                      wa_hi[:, :, 64:128].bitcast(F32), ALU.subtract).then_inc(wa_dve, 1)
            dve.wait_ge(d_small, 16 * N_SMALL)
            dve.tensor_scalar(dhalf[:, :], dcol[:, :], 0.5, None, ALU.mult).then_inc(dh_ready, 1)
            count = [0]

            def link(ins):
                count[0] += 1
                ins.then_inc(a_v, 1)
                dve.wait_ge(a_v, count[0])

            for pb in range(2):
                r, e, den, sv, tt, pl, dt, tmp = (t[:, pb, :] for t in (R_, E_, DEN, SV, TT_, PL, DT, TMP))
                dve.wait_ge(a_pe, pb + 1)
                link(dve.tensor_scalar(r, DTB[pb][:, :], 0.0, None, ALU.max))
                dve.wait_ge(a_act, B_ALL * pb + B_EXP)
                link(dve.tensor_scalar(den, e, 2.0, None, ALU.add))
                link(dve.reciprocal(tmp, den))
                link(dve.tensor_tensor(sv, e, tmp, ALU.mult))
                link(dve.tensor_tensor(tt, sv, sv, ALU.mult))
                link(dve.tensor_scalar(pl, tt, 1.0 / 17, None, ALU.mult))
                for k in (15, 13, 11, 9, 7, 5, 3):
                    link(dve.scalar_tensor_tensor(out=pl, in0=pl, scalar=1.0 / k, in1=tt, op0=ALU.add, op1=ALU.mult))
                link(dve.scalar_tensor_tensor(out=pl, in0=pl, scalar=1.0, in1=sv, op0=ALU.add, op1=ALU.mult))
                link(dve.scalar_tensor_tensor(out=dt, in0=pl, scalar=2.0, in1=r, op0=ALU.mult, op1=ALU.add))
                link(dve.tensor_scalar(tmp, dt, DT_MAX, -1.0, ALU.min, ALU.mult))
                dve.wait_ge(konst, 16)
                link(dve.tensor_tensor_scan(out=pl, data0=chunk_on[:, :], data1=tmp, initial=0.0,
                                            op0=ALU.mult, op1=ALU.add))
                assert count[0] == A_ALL * pb + A_SUM
                plv = pl.rearrange("p (c q) -> p c q", q=Q)
                link(dve.tensor_tensor(tmp.rearrange("p (c q) -> p c q", q=Q),
                                       plv[:, :, Q - 1:Q].broadcast_to([P, NC, Q]), plv, ALU.subtract))
                link(dve.reciprocal(den, dt))
                dve.wait_ge(dh_ready, 1)
                link(dve.tensor_scalar(den, den, dhalf[:, 0:1], None, ALU.mult))
                dve.wait_ge(a_act, B_ALL * pb + B_HI)
                link(dve.tensor_tensor(sv, pl, e, ALU.subtract))
                assert count[0] == A_ALL * pb + A_LO
            modulation(2)
            modulation(3)
            dve.wait_ge(gate_abs, 2)
            for n in range(2):
                dve.tensor_scalar(rsg[:, n, :], GATE[n][0:NB, :], 0.0, 2.0, ALU.is_ge, ALU.mult).then_inc(gate_v, 1)
            dve.wait_ge(gate_v, 2)
            dve.tensor_scalar(rsg[:, :, :], rsg[:, :, :], -1.0, None, ALU.add).then_inc(gate_v, 1)
            dve.tensor_scalar(rabs[:, 0, :], rabs[:, 0, :], 0.25, 0.5, ALU.max, ALU.mult).then_inc(gate_v, 1)
            dve.tensor_scalar(rabs[:, 1, :], rabs[:, 1, :], 0.25, None, ALU.max).then_inc(gate_v, 1)
            dve.wait_ge(gate_v, 5)
            for n in range(2):
                dve.tensor_tensor(rows[:, n, :], rsg[:, n, :], rabs[:, n, :], ALU.mult).then_inc(gate_ready, 1)

        @block.scalar
        def _(act):
            cwv = conv_w.rearrange("(g p) o k -> p g (o k)", p=P)
            cbv = conv_b.rearrange("(g p o) -> p g o", p=P, o=1)
            zbv = z_bias.rearrange("(g p o) -> p g o", p=P, o=1)
            dv = d_skip.rearrange("(h o) -> h o", o=1)
            act.wait_ge(d_c, 16)
            act.activation(th4, c4, ACT.Tanh, scale=0.5).then_inc(th_ready, 1)
            with nc.allow_non_contiguous_dma(reason="small vectors laid out by partition"):
                for t in range(4):
                    n = slice(t, 8, 2) if t < 2 else slice(4 * t, 4 * t + 4)
                    o = t * (KS + 1)
                    act.dma_start(s.gpc[:, :, o:o + KS], cwv[:, n, :]).then_inc(d_small, 16)
                    act.dma_start(s.gpc[:, :, o + KS:o + KS + 1], cbv[:, n, :]).then_inc(d_small, 16)
                for t in range(2):
                    act.dma_start(s.gpc[:, :, 20 + t:21 + t], zbv[:, t:8:2, :]).then_inc(d_small, 16)
                act.dma_start(dcol[0:64, :], dv).then_inc(d_small, 16)
                act.dma_start(dcol[64:128, :], dv).then_inc(d_small, 16)
            act.wait_ge(konst, 5)
            act.wait_ge(wa_pe, 1)
            act.activation(wa_hi[:, :, 64:128], s.bank[5][:, 0:KC * NH].rearrange("p (k h) -> p k h", k=KC),
                           ACT.Copy).then_inc(wa_act, 1)
            act.wait_ge(mod_ready, 2)

            def make_h(n):
                b, k = n // KC, n % KC
                act.wait_ge(t_pe, 4 * b + 4)
                scale, bias = s.mod_t[:, 0, k, b:b + 1], s.mod_t[:, 1, k, b:b + 1]
                act.activation(s.h_hi[:, b, k, :], s.bank[4 * (b % 2) + k][:, :], ACT.Identity, scale=scale, bias=bias).then_inc(h_hi, 1)
                if n >= 2:
                    act.wait_ge(h_lo[n % 2], n // 2)
                act.activation(hf[:, n % 2, :], s.bank[4 * (b % 2) + k][:, :], ACT.Identity, scale=scale, bias=bias).then_inc(h_act, 1)

            def softplus_inputs(pb):
                act.wait_ge(a_v, A_ALL * pb + 1)
                act.activation(E_[:, pb, :], DTB[pb][:, :], ACT.Abs).then_inc(a_act, 1)
                act.wait_ge(a_act, B_ALL * pb + B_ABS)
                act.activation(E_[:, pb, :], E_[:, pb, :], ACT.Exp, scale=-1.0).then_inc(a_act, 1)

            def decays(pb):
                act.wait_ge(a_v, A_ALL * pb + A_SUM)
                act.activation(E_[:, pb, :].bitcast(F32R), PL[:, pb, :], ACT.Copy).then_inc(a_act, 1)
                act.activation(TT_[:, pb, :], PL[:, pb, :], ACT.Exp).then_inc(a_act, 1)
                act.activation(cde[:, pb, :], PL[:, pb, :].rearrange("p (c q) -> p c q", q=Q)[:, :, Q - 1], ACT.Exp)\
                   .then_inc(a_act, 1)
                act.wait_ge(a_v, A_ALL * pb + A_END)
                act.activation(TMP[:, pb, :], TMP[:, pb, :], ACT.Exp).then_inc(a_act, 1)
                act.wait_ge(a_act, B_ALL * pb + B_HI)
                act.activation(R_[:, pb, :], E_[:, pb, :], ACT.Copy, scale=-1.0).then_inc(a_act, 1)

            def end_decays(pb):
                act.wait_ge(we_pe, pb + 1)
                for c in range(NC):
                    act.activation(s.wend[:, :, 2 * pb:2 * pb + 2, c, :],
                                   WE[pb][:, c * P:(c + 1) * P].rearrange("p (q g h) -> p g q h", q=2, g=GP),
                                   ACT.Copy).then_inc(we_ev, 1)

            def weights(n):
                t, hh = n // 2, n % 2
                act.wait_ge(wt_pe, n + 1)
                act.activation(s.w_hi[:, t, 2 * hh:2 * hh + 2, :],
                               WB[hh][:, 0:2 * P].rearrange("p (k r) -> p k r", k=2), ACT.Copy)
                if n >= 2:
                    act.wait_ge(w_pool, n - 1)
                act.activation(wst[:, hh, :], WB[hh][:, 0:2 * P], ACT.Copy).then_inc(w_act, 1)

            for n in range(16):
                make_h(n)
            softplus_inputs(0)
            act.wait_ge(konst, 16)
            for i in range(4):
                act.activation(s.R[:, i // 2, i % 2, :], stage[:, :], ACT.Copy).then_inc(kcopy, 1)
                act.activation(s.Lm[:, i // 2, i % 2, :], lstage[:, :], ACT.Copy).then_inc(kcopy, 1)
            for n in range(NT):
                weights(n)
            decays(0)
            softplus_inputs(1)
            for n in range(NT, 2 * NT):
                weights(n)
            decays(1)
            end_decays(0)
            end_decays(1)
            for n in range(2):
                act.wait_ge(mod_pe, 5 + n)
                act.activation(rabs[:, n, :], GATE[n][0:NB, :], ACT.Abs).then_inc(gate_abs, 1)

        @block.tensor
        def _(pe):
            pe.wait_ge(sc_ready, 1)
            pe.wait_ge(konst, 3)
            for k in range(KC):
                ins = pe.transpose(s.bank[4][:, k * NB:(k + 1) * NB], sc4[:, k * P:(k + 1) * P], s.ident[0:NB, 0:NB])
            ins.then_inc(sct_pe, 1)

            def section(n):
                pe.wait_ge(d_wm[n % 2], 16 * (n // 2 + 1))
                if n >= 2:
                    pe.wait_ge(mod_ready, 2)
                for m in range(KC):
                    for k in range(KC):
                        ins = pe.matmul(MOD[n // 2][:, (n * KC + m) * NB:(n * KC + m + 1) * NB],
                                        wm[:, n % 2, k, m * P:(m + 1) * P], scT[:, k, :],
                                        start=(k == 0), stop=(k == KC - 1))
                ins.then_inc(mod_pe, 1)

            def turn(i):
                b = i // 4
                pe.wait_ge(ln_n, i + 1)
                if i == 4:
                    pe.wait_ge(mod_ready, 2)
                    pe.wait_ge(wa_dve, 1)
                if b >= 2 and i % 4 == 0:
                    pe.wait_ge(h_act, 4 * (b - 1))
                for k in range(KC):
                    ins = pe.transpose(s.bank[4 * (b % 2) + k][:, (i % 4) * P:(i % 4 + 1) * P], xn[:, i % 2, k * P:(k + 1) * P],
                                       s.ident[:, :])
                ins.then_inc(t_pe, 1)

            def dt_inputs(pb):
                pe.wait_ge(wa_dve, 1)
                for i in range(2):
                    pe.wait_ge(h_lo[i], 4 * pb + 4)
                n = 0
                for q in range(2):
                    b, w = 2 * pb + q, slice(64 - 64 * q, 192 - 64 * q)
                    for k in range(KC):
                        for wt, h in ((wa_hi, s.h_hi), (wa_hi, s.h_lo), (wa_lo, s.h_hi)):
                            ins = pe.matmul(DTB[pb][:, :], wt[:, k, w], h[:, b, k, :],
                                            start=(n == 0), stop=(n == 23))
                            n += 1
                ins.then_inc(a_pe, 1)

            def end_decays(pb):
                pe.wait_ge(a_act, B_ALL * pb + B_WE)
                for c in range(NC):
                    ins = pe.transpose(WE[pb][:, c * P:(c + 1) * P], TMP[:, pb, c * P:(c + 1) * P], s.ident[:, :])
                ins.then_inc(we_pe, 1)

            pe.wait_ge(sct_ready, 1)
            section(0)
            section(1)
            pe.wait_ge(d_wa, 16)
            for k in range(KC):
                ins = pe.transpose(s.bank[5][:, k * NH:(k + 1) * NH], wa_raw[:, k * P:(k + 1) * P],
                                   s.ident[0:NH, 0:NH])
            ins.then_inc(wa_pe, 1)
            for i in range(4):
                turn(i)
            for i in range(4, 16):
                turn(i)
            pe.wait_ge(h_act, 12)
            dt_inputs(0)
            section(2)
            section(3)
            dt_inputs(1)
            pe.wait_ge(h_act, 16)
            for n in range(2 * NT):
                t, hh = n // 2, n % 2
                pe.wait_ge(d_w[t % 2], 16 * (t // 2 + 1))
                if n >= 2:
                    pe.wait_ge(w_act, n - 1)
                for k in range(2):
                    ins = pe.transpose(WB[hh][:, k * P:(k + 1) * P],
                                       wraw[:, t % 2, (2 * hh + k) * P:(2 * hh + k + 1) * P], s.ident[:, :])
                ins.then_inc(wt_pe, 1)
            for n in range(2):
                pe.wait_ge(d_wm[n], 48)
                for k in range(KC):
                    ins = pe.matmul(GATE[n][0:NB, :], scT[:, k, :], wm[:, n, k, :],
                                    start=(k == 0), stop=(k == KC - 1))
                ins.then_inc(mod_pe, 1)
            for pb in range(2):
                end_decays(pb)


def halves_before(b, k):
    return sum(slot < 16 * (b - 2) + k for slot in W_SLOT)


def main_part(nc, s, w_in):
    with ExitStack() as ctx:
        def sb(name, shape, dt=F32):
            return ctx.enter_context(nc.sbuf_tensor("m_" + name, shape, dt))

        def sem(name):
            return ctx.enter_context(nc.semaphore("m_" + name))

        wraw = sb("wraw", [P, 2, D])
        wst = sb("wst", [P, 2, 2 * P])
        gcs = sb("gcs", [P, 22])
        cd = sb("cd", [P, GP, HG, NB * NC])
        cv, th = sb("cv", [P, 2, L]), sb("th", [P, 2, L])
        xs, gate = sb("xs", [P, 2, 2, L]), sb("gate", [P, 2, 2, L])
        Bt = sb("Bt", [P, 2, L])
        Ct = sb("Ct", [P, 2, 2, L])
        ea, dd = sb("ea", [P, 2, 2, L]), sb("dd", [P, 2, 2, L])
        E, M = sb("E", [P, 4, 4 * Q]), sb("M", [P, 4, 4 * Q])
        Gm = sb("Gm", [P, 2, Q])
        Xp = sb("Xp", [P, 2, 2 * HG, 32])
        Xw = sb("Xw", [P, 2, HG * HD])
        BTs = sb("BTs", [P, P])
        S, S1 = sb("S", [P, HG * HD]), sb("S1", [P, HG * HD])
        y1 = sb("y1", [P, 2, 2, L])
        t1 = sb("t1", [P, 2, L])
        A, DB, YB, GB, SB = s.bank[0:2], s.bank[2:4], s.bank[4:6], s.bank[6], s.bank[7]

        cd_ready, zeroed, gcs_ready = sem("cd_ready"), sem("zeroed"), sem("gcs_ready")
        rl_ready, eb_ready, wraw_ready = ([sem(f"{n}{i}") for i in range(2)] for n in ("rl_ready", "eb_ready", "wraw_ready"))
        in_done, lin_done, tap_done, conv_done, tanh_done, silu_done = (
            sem(n) for n in ("in_done", "lin_done", "tap_done", "conv_done", "tanh_done", "silu_done"))
        d_done, exp_done, prep_done, gm_done, m_done, yd_done = (
            sem(n) for n in ("d_done", "exp_done", "prep_done", "gm_done", "m_done", "yd_done"))
        bt_done, bt_read, xp_done, xw_done, st_done, s_part, s_new, yo_done = (
            sem(n) for n in ("bt_done", "bt_read", "xp_done", "xw_done", "st_done", "s_part", "s_new", "yo_done"))
        yo_scaled, y1_done, t1_done, t2_done, y_out, y_stored = (
            sem(n) for n in ("yo_scaled", "y1_done", "t1_done", "t2_done", "y_out", "y_stored"))
        w_pe, w_copied, w_hi_done, w_lo_done = sem("w_pe"), sem("w_copied"), sem("w_hi_done"), sem("w_lo_done")
        block = ctx.enter_context(nc.Block())

        def run(eng, step):
            for b in range(4):
                step(Step(0, b))
            with eng.Fori(1, GP - 1) as gp:
                for b in range(4):
                    step(Step(gp, b))
            for b in range(4):
                step(Step(GP - 1, b))

        def last(st):
            return isinstance(st.gp, int) and st.gp == GP - 1

        def ahead(st):
            return not (last(st) and st.b == 3)

        def nxt(st, c, by=1):
            return (st, c + by) if c + by < NC else (st.next(), c + by - NC)

        def tok(c):
            return slice(c * Q, (c + 1) * Q)

        @block.sync
        def _(sp):
            a_v = s.a_d.rearrange("r (b g q h) t -> r b g q h t", b=NB, g=GP, q=2)
            na_v = s.na_d.rearrange("r (b g q h) t -> r b g q h t", b=NB, g=GP, q=2)
            ea_v = s.ea_d.rearrange("(b g q h) t -> b g q h t", b=NB, g=GP, q=2)
            dd_v = s.dd_d.rearrange("(b g q h) t -> b g q h t", b=NB, g=GP, q=2)
            y_v = s.y_d.rearrange("(g q p) t -> g p q t", q=2, p=P)
            cd_v = s.cd_d.rearrange("(g q h) n -> q g h n", g=GP, q=2)

            def load_decays(st, c):
                for h in range(HG):
                    sp.dma_start(s.R[R_POS + h:R_ALL:HG, c % 2, :, h * Q:(h + 1) * Q].bitcast(F32),
                                 a_v[:, st.b, st.gp, :, h, tok(c)]).then_inc(rl_ready[c % 2], 16)
                for r in range(2):
                    sp.dma_start(s.Lm[R_NEG + r * HG:R_NEG + (r + 1) * HG, c % 2, :, :].bitcast(F32),
                                 na_v[r, st.b, st.gp, :, :, tok(c)].rearrange("q h t -> h q t"))\
                      .then_inc(rl_ready[c % 2], 16)

            def load_scales(st):
                for q in range(2):
                    for dst, src in ((ea, ea_v), (dd, dd_v)):
                        for_heads = src[st.b, st.gp, q].unsqueeze(1).broadcast_to([HG, HD, L])
                        sp.dma_start(dst[:, st.par, q, :], for_heads).then_inc(eb_ready[st.par], 16)

            def load_weights(gp, t):
                for_pair = w_rows(gp, t)
                sp.dma_start(wraw[:, t % 2, :], for_pair).then_inc(wraw_ready[t % 2], 16)

            w_x = w_in[0:DI, :].rearrange("(g q p) d -> g q p d", q=2, p=P)
            w_bc = w_in[DI:2 * DI, :].rearrange("(o g p) d -> o g p d", o=2, p=P)
            w_z = w_in[2 * DI:3 * DI, :].rearrange("(g q p) d -> g q p d", q=2, p=P)

            def w_rows(gp, t):
                return w_x[gp, t] if t < 2 else w_bc[t - 2, gp] if t < 4 else w_z[gp, t - 4]

            def step(st):
                for c in range(NC):
                    j4 = st.n(16, 4 * c)
                    st2, c2 = nxt(st, c, 2)
                    if ahead(st) or c < 2:
                        sp.wait_ge(d_done, j4 + 4)
                        load_decays(st2, c2)
                    if c == 1:
                        if not (isinstance(st.gp, int) and st.gp == 0 and st.b == 0):
                            store(st.prev())
                        if ahead(st):
                            load_scales(st.next())
                    if not last(st):
                        if st.b == 1 and c == 2:
                            wait(sp, w_pe, st.gp * 12)
                            load_weights(st.gp + 1, 0)
                            load_weights(st.gp + 1, 1)
                        if (st.b, c) in ((2, 2), (2, 3), (3, 0), (3, 1)):
                            t = 4 * (st.b - 2) + c
                            sp.wait_ge(w_pe, st.gp * 12 + (2 * t - 2))
                            load_weights(st.gp + 1, t)

            def store(st):
                sp.wait_ge(y_out, st.n(1, 1))
                sp.dma_start(y_v[st.gp][:, :, st.b * L:(st.b + 1) * L], t1[:, :, :]).then_inc(y_stored, 16)

            for q in range(2):
                sp.dma_start(cd[64 * q:64 * q + 64, :, :, :],
                             cd_v[q].unsqueeze(0).broadcast_to([NS, GP, HG, NB * NC])).then_inc(cd_ready, 16)
            load_decays(Step(0, 0), 0)
            load_decays(Step(0, 0), 1)
            load_scales(Step(0, 0))
            run(sp, step)
            store(Step(GP - 1, 3))
            sp.wait_ge(y_stored, 16 * 4 * GP)

        @block.tensor
        def _(pe):
            def project(st, m):
                t, part = m // 3, m % 3
                if part == 0:
                    if st.b == 0 and not (isinstance(st.gp, int) and st.gp == 0):
                        pe.wait_ge(w_lo_done, st.gp * 12 + (2 * t + 2 - 12))
                    if t < 2:
                        wait(pe, lin_done, st.n(6, t - 1))
                    else:
                        pe.wait_ge(conv_done, st.n(4, t - 1))
                for n in range(4 * part, 4 * part + 4):
                    k, w, h = n // 3, (s.w_hi, s.w_hi, s.w_lo)[n % 3], (s.h_hi, s.h_lo, s.h_hi)[n % 3]
                    ins = pe.matmul(A[t % 2][:, :], w[:, t, k, :], h[:, st.b, k, :], start=(n == 0), stop=(n == 11))
                if part == 2:
                    ins.then_inc(in_done, 1)

            def decays(st, c, sl):
                q, hh = sl // 2, sl % 2
                if sl == 0:
                    pe.wait_ge(rl_ready[c % 2], st.n(2 * 160, (c // 2 + 1) * 160))
                wait(pe, exp_done, st.n(16, 4 * c + sl - 1))
                pe.matmul(DB[sl % 2][:, :], s.Lm[:, c % 2, q, :], s.R[:, c % 2, q, hh * 512:(hh + 1) * 512],
                          start=True, stop=True).then_inc(d_done, 1)

            def prepare(st, c):
                if c == 0:
                    pe.wait_ge(silu_done, st.n(6, 4))
                wait(pe, gm_done, st.n(4, c))
                for q in range(2):
                    pe.transpose(GB[:, q * P:(q + 1) * P], xs[:, st.par, q, tok(c)], s.ident[:, :])
                pe.matmul(GB[:, 256:512], Bt[:, st.par, tok(c)], Ct[:, st.par, :, tok(c)],
                          start=True, stop=True).then_inc(prep_done, 1)
                if c < 3:
                    wait(pe, s_new, st.n(3, c))
                    pe.transpose(SB[:, 0:P], Bt[:, st.par, tok(c)], s.ident[:, :]).then_inc(bt_done, 1)

            def weights(gp, n):
                t, hh = n // 2, n % 2
                if hh == 0:
                    pe.wait_ge(wraw_ready[t % 2], gp * 48 + 16 * (t // 2 + 1))
                for k in range(2):
                    ins = pe.transpose(SB[:, 256 + k * P:256 + (k + 1) * P],
                                       wraw[:, t % 2, (2 * hh + k) * P:(2 * hh + k + 1) * P], s.ident[:, :])
                ins.then_inc(w_pe, 1)

            def step(st):
                nx = st.next()
                for k in range(16):
                    c, sl = k // 4, k % 4
                    stn, cn = nxt(st, c)
                    if sl == 0:
                        wait(pe, y1_done, st.n(4, c - 1))
                    if sl == 0 and c > 0:
                        pe.wait_ge(s_new, st.n(3, c))
                        pe.matmul(YB[c % 2][:, 256:512], S[:, :], Ct[:, st.par, :, tok(c)],
                                  start=True, stop=True).then_inc(yo_done, 1)
                    if ahead(st) or c < 3:
                        decays(stn, cn, sl)
                    pe.wait_ge(m_done, st.n(16, 4 * c + sl + 1))
                    if sl == 0:
                        pe.wait_ge(xp_done, st.n(4, c + 1))
                    q = sl // 2
                    for hh in range(4):
                        h = 4 * (sl % 2) + hh
                        j = h // 2
                        ins = pe.matmul(YB[c % 2][32 * j:32 * j + 32, q * Q:(q + 1) * Q], Xp[:, c % 2, q * HG + h, :],
                                        M[:, sl, hh * Q:(hh + 1) * Q], start=(h % 2 == 0), stop=(h % 2 == 1))
                    ins.then_inc(yd_done, 1)
                    if ahead(st):
                        for m in GROUPS[k]:
                            project(nx, m)
                    if sl == 0 and c < 3:
                        pe.wait_ge(xw_done, st.n(3, c + 1))
                        pe.wait_ge(bt_read, st.n(3, c + 1))
                        if halves_before(st.b, k) and not last(st):
                            pe.wait_ge(w_copied, st.gp * 12 + halves_before(st.b, k))
                        for q in range(2):
                            ins = pe.matmul(SB[64 * q:64 * q + 64, P:2 * P], BTs[:, 64 * q:64 * q + 64], Xw[:, q, :],
                                            start=True, stop=True)
                        ins.then_inc(st_done, 1)
                    if sl == PREP and (ahead(st) or c < 3):
                        if halves_before(st.b, k) and not last(st):
                            pe.wait_ge(w_copied, st.gp * 12 + halves_before(st.b, k))
                        prepare(stn, cn)
                    n = halves_before(st.b, k)
                    if halves_before(st.b, k + 1) > n and not last(st):
                        pe.wait_ge(bt_read, st.n(3, bt_count(c, sl)))
                        wait(pe, s_new, st.n(3, min(c + 1, 3)))
                        wait(pe, w_copied, st.gp * 12 + n)
                        weights(st.gp, n)

            def bt_count(c, sl):
                own = min(c + 1, 3) if sl < PREP else min(c + 2, 3)
                return 4 if c == 3 and sl >= PREP else own

            for m in range(18):
                project(Step(0, 0), m)
            for sl in range(4):
                decays(Step(0, 0), 0, sl)
            prepare(Step(0, 0), 0)
            run(pe, step)

        @block.scalar
        def _(act):
            def linear(st, t):
                act.wait_ge(in_done, st.n(6, t + 1))
                wait(act, silu_done, st.n(6, t - 1))
                act.wait_ge(gcs_ready, st.gp + 1)
                o = t * (KS + 1)
                scale, bias = (gcs[:, o + KS - 1:o + KS], gcs[:, o + KS:o + KS + 1]) if t < 4 else (1.0, gcs[:, 16 + t:17 + t])
                act.activation(cv[:, t % 2, :], A[t % 2][:, :], ACT.Identity, scale=scale, bias=bias).then_inc(lin_done, 1)

            def tanh(st, t):
                if t < 4:
                    act.wait_ge(conv_done, st.n(4, t + 1))
                else:
                    act.wait_ge(lin_done, st.n(6, t + 1))
                act.activation(th[:, t % 2, :], cv[:, t % 2, :], ACT.Tanh, scale=0.5).then_inc(tanh_done, 1)

            def exponent(st, c, sl):
                act.wait_ge(d_done, st.n(16, 4 * c + sl + 1))
                wait(act, m_done, st.n(16, 4 * c + sl - 3))
                act.activation(E[:, sl, :], DB[sl % 2][:, :], ACT.Exp).then_inc(exp_done, 1)

            def spread(st, c):
                act.wait_ge(prep_done, st.n(4, c + 1))
                wait(act, yd_done, st.n(16, 4 * (c - 1)))
                wait(act, xw_done, st.n(3, c - 1) if c else st.n(3, 0))
                out = Xp[:, c % 2, :, :].rearrange("p (j e) (m d) -> p j (e m) d", e=2, d=HD)[:, :, 0:4:3, :]
                act.activation(out, GB[:, 0:256].rearrange("p (j e d) -> p j e d", e=2, d=HD), ACT.Copy)\
                   .then_inc(xp_done, 1)
                if c < 3:
                    act.wait_ge(bt_done, st.n(3, c + 1))
                    wait(act, st_done, st.n(3, c))
                    act.activation(BTs[:, :], SB[:, 0:P], ACT.Copy).then_inc(bt_read, 1)

            def step(st):
                nx = st.next()
                for k in range(16):
                    c, sl = k // 4, k % 4
                    stn, cn = nxt(st, c)
                    if ahead(st) or c < 3:
                        exponent(stn, cn, sl)
                    for t in range(NT):
                        if FS[t] + 1 == k and ahead(st):
                            tanh(nx, t)
                        if FS[t] + 1 == k + 16 and not first(st):
                            tanh(st, t)
                    for t in range(NT):
                        if FS[t] == k and ahead(st):
                            linear(nx, t)
                    if sl == PREP and (ahead(st) or c < 3):
                        spread(stn, cn)
                    n = halves_before(st.b, k)
                    if halves_before(st.b, k + 1) > n and not last(st):
                        act.wait_ge(w_pe, st.gp * 12 + n + 1)
                        wait(act, w_lo_done, st.gp * 12 + n - 1)
                        act.activation(s.w_hi[:, n // 2, 2 * (n % 2):2 * (n % 2) + 2, :],
                                       SB[:, 256:512].rearrange("p (k r) -> p k r", k=2), ACT.Copy).then_inc(w_hi_done, 1)
                        act.activation(wst[:, n % 2, :], SB[:, 256:512], ACT.Copy).then_inc(w_copied, 1)

            def first(st):
                return isinstance(st.gp, int) and st.gp == 0 and st.b == 0

            for t in range(NT):
                linear(Step(0, 0), t)
                tanh(Step(0, 0), t)
            act.wait_ge(zeroed, 1)
            for sl in range(4):
                exponent(Step(0, 0), 0, sl)
            spread(Step(0, 0), 0)
            run(act, step)

        @block.vector
        def _(dve):
            def convolve(st, t):
                dve.wait_ge(lin_done, st.n(6, t + 1))
                for k in range(KS - 2, -1, -1):
                    lag, o = KS - 1 - k, t * (KS + 1) + k
                    if lag > 1:
                        dve.wait_ge(tap_done, st.n(8, 2 * t + lag - 1))
                    ins = dve.scalar_tensor_tensor(out=cv[:, t % 2, lag:], in0=A[t % 2][:, 0:L - lag],
                                                   scalar=gcs[:, o:o + 1], in1=cv[:, t % 2, lag:],
                                                   op0=ALU.mult, op1=ALU.add)
                    ins.then_inc(conv_done if k == 0 else tap_done, 1)

            def silu(st, t):
                dve.wait_ge(tanh_done, st.n(6, t + 1))
                if t == 0:
                    wait(dve, y_out, st.n(1, -1))
                if t == 3:
                    for q in range(2):
                        n = slice(64 * q, 64 * q + 64)
                        ins = dve.scalar_tensor_tensor(out=Ct[n, st.par, q, :], in0=th[n, 1, :], scalar=1.0,
                                                       in1=cv[n, 1, :], op0=ALU.add, op1=ALU.mult)
                    ins.then_inc(silu_done, 1)
                    return
                dst = (xs[:, st.par, 0, :], xs[:, st.par, 1, :], Bt[:, st.par, :], None,
                       gate[:, st.par, 0, :], gate[:, st.par, 1, :])[t]
                dve.scalar_tensor_tensor(out=dst, in0=th[:, t % 2, :], scalar=1.0, in1=cv[:, t % 2, :],
                                         op0=ALU.add, op1=ALU.mult).then_inc(silu_done, 1)

            def causal(st, c):
                dve.wait_ge(xp_done, st.n(4, c + 1))
                wait(dve, m_done, st.n(16, 4 * c))
                dve.tensor_tensor(Gm[:, :, :], GB[:, 256:512].rearrange("p (q s) -> p q s", q=2),
                                  s.tri[:, :].unsqueeze(1).broadcast_to([P, 2, Q]), ALU.mult).then_inc(gm_done, 1)

            def mix(st, c, sl):
                dve.wait_ge(exp_done, st.n(16, 4 * c + sl + 1))
                dve.wait_ge(gm_done, st.n(4, c + 1))
                wait(dve, yd_done, st.n(16, 4 * c + sl - 3))
                dve.tensor_tensor(M[:, sl, :].rearrange("p (h s) -> p h s", h=4),
                                  E[:, sl, :].rearrange("p (h s) -> p h s", h=4),
                                  Gm[:, sl // 2, :].unsqueeze(1).broadcast_to([P, 4, Q]), ALU.mult).then_inc(m_done, 1)

            def collect(st, c):
                dve.wait_ge(yd_done, st.n(16, 4 * c + 4))
                own = YB[c % 2][:, 0:256].rearrange("p (q s) -> p q s", q=2)
                if c == 0:
                    wait(dve, y_out, st.n(1, -1))
                    dve.tensor_copy(y1[:, st.par, :, tok(c)], own).then_inc(y1_done, 1)
                    return
                dve.wait_ge(yo_done, st.n(3, c))
                dve.wait_ge(eb_ready[st.par], st_eb(st))
                dve.tensor_tensor(y1[:, st.par, :, tok(c)], YB[c % 2][:, 256:512].rearrange("p (q s) -> p q s", q=2),
                                  ea[:, st.par, :, tok(c)], ALU.mult).then_inc(yo_scaled, 1)
                dve.wait_ge(yo_scaled, st.n(3, c))
                dve.tensor_tensor(y1[:, st.par, :, tok(c)], own, y1[:, st.par, :, tok(c)], ALU.add).then_inc(y1_done, 1)

            def update(st, c):
                dve.wait_ge(st_done, st.n(3, c + 1))
                if c == 0:
                    wait(dve, yo_done, st.n(3, 0))
                    dve.tensor_copy(S[:, :], SB[:, P:2 * P]).then_inc(s_new, 1)
                    return
                dve.wait_ge(s_new, st.n(3, c))
                dve.tensor_tensor(S1[:, :].rearrange("p (h d) -> p h d", h=HG), S[:, :].rearrange("p (h d) -> p h d", h=HG),
                                  cd[:, st.gp, :, st.b * NC + c].unsqueeze(2).broadcast_to([P, HG, HD]),
                                  ALU.mult).then_inc(s_part, 1)
                dve.wait_ge(s_part, st.n(2, c))
                dve.wait_ge(yo_done, st.n(3, c))
                dve.tensor_tensor(S[:, :], S1[:, :], SB[:, P:2 * P], ALU.add).then_inc(s_new, 1)

            def step(st):
                nx = st.next()
                for k in range(16):
                    c, sl = k // 4, k % 4
                    stn, cn = nxt(st, c)
                    more = ahead(st) or c < 3
                    if sl == 0 and not (first(st) and c == 0):
                        collect(st, c - 1) if c else collect(st.prev(), 3)
                    if sl == 0 and c < 3:
                        update(st, c)
                    if sl == PREP + 1 and more:
                        causal(stn, cn)
                        mix(stn, cn, 0)
                        mix(stn, cn, 1)
                    if sl == PREP + 2 and more:
                        mix(stn, cn, 2)
                        mix(stn, cn, 3)
                    for t in range(NT):
                        if FS[t] + 2 == k and ahead(st):
                            silu(nx, t)
                        if FS[t] + 2 == k + 16 and not first(st):
                            silu(st, t)
                    for t in range(4):
                        if FS[t] == k and ahead(st):
                            convolve(nx, t)

            def first(st):
                return isinstance(st.gp, int) and st.gp == 0 and st.b == 0

            def st_eb(st):
                return st.gp * 128 + 64 * (st.b // 2 + 1)

            dve.memset(Ct[:, :, :, :], 0.0)
            dve.memset(Xp[:, :, :, :], 0.0).then_inc(zeroed, 1)
            dve.wait_ge(zeroed, 1)
            dve.wait_ge(gcs_ready, 1)
            for t in range(NT):
                if t < 4:
                    convolve(Step(0, 0), t)
                silu(Step(0, 0), t)
            dve.wait_ge(cd_ready, 32)
            causal(Step(0, 0), 0)
            for sl in range(4):
                mix(Step(0, 0), 0, sl)
            run(dve, step)
            collect(Step(GP - 1, 3), 3)

        @block.gpsimd
        def _(pool):
            def constants(gp):
                pool.tensor_copy(gcs[:, :], s.gpc[:, gp, :]).then_inc(gcs_ready, 1)

            def weigh(st, c):
                pool.wait_ge(xp_done, st.n(4, c + 1))
                wait(pool, st_done, st.n(3, c))
                src = Xp[:, c % 2, :, :].rearrange("p (j e) (m d) -> p j (e m) d", e=2, d=HD)[:, :, 0:4:3, :]
                w = s.wend[:, st.gp, st.b, c, :].rearrange("p (j e) -> p j e", e=2).unsqueeze(3).broadcast_to([P, HG, 2, HD])
                pool.tensor_tensor(Xw[:, :, :].rearrange("p q (j e d) -> p (q j) e d", e=2, d=HD), src, w,
                                   ALU.mult).then_inc(xw_done, 1)

            def skip(st):
                pool.wait_ge(silu_done, st.n(6, 2))
                pool.wait_ge(eb_ready[st.par], st.gp * 128 + 64 * (st.b // 2 + 1))
                wait(pool, y_stored, st.n(16, 0))
                pool.tensor_tensor(t1[:, :, :], xs[:, st.par, :, :], dd[:, st.par, :, :], ALU.mult).then_inc(t1_done, 1)

            def finish(st):
                pool.wait_ge(y1_done, st.n(4, 4))
                pool.wait_ge(t1_done, st.n(1, 1))
                pool.tensor_tensor(t1[:, :, :], t1[:, :, :], y1[:, st.par, :, :], ALU.add).then_inc(t2_done, 1)
                pool.wait_ge(t2_done, st.n(1, 1))
                pool.wait_ge(silu_done, st.n(6, 6))
                pool.tensor_tensor(t1[:, :, :], t1[:, :, :], gate[:, st.par, :, :], ALU.mult).then_inc(y_out, 1)

            def split(gp, n):
                w = slice(2 * (n % 2), 2 * (n % 2) + 2)
                src = wst[:, n % 2, :].rearrange("p (k r) -> p k r", k=2)
                pool.wait_ge(w_copied, gp * 12 + n + 1)
                pool.tensor_tensor(s.w_lo[:, n // 2, w, :], src, s.w_hi[:, n // 2, w, :].bitcast(F32),
                                   ALU.subtract).then_inc(w_lo_done, 1)

            def step(st):
                for c in range(NC):
                    if c == 0:
                        if st.b == 3 and not last(st):
                            pool.wait_ge(lin_done, st.n(6, 6))
                            pool.wait_ge(conv_done, st.n(4, 4))
                            constants(st.gp + 1)
                        if not (isinstance(st.gp, int) and st.gp == 0 and st.b == 0):
                            finish(st.prev())
                    stn, cn = nxt(st, c)
                    if cn < 3 and (ahead(st) or c < 3):
                        weigh(stn, cn)
                    if c == 2:
                        skip(st)
                    if not last(st):
                        for n in range(halves_before(st.b, 4 * c), halves_before(st.b, 4 * c + 4)):
                            split(st.gp, n)

            constants(0)
            weigh(Step(0, 0), 0)
            run(pool, step)
            finish(Step(GP - 1, 3))


def tail_part(nc, s, x, w_out, w_ffn, b_ffn, out):
    with ExitStack() as ctx:
        def sb(name, shape, dt=F32):
            return ctx.enter_context(nc.sbuf_tensor("t_" + name, shape, dt))

        def sem(name):
            return ctx.enter_context(nc.semaphore("t_" + name))

        KI, TT = DI // P, L // P
        wo_hi, wo_lo = sb("wo_hi", [P, KI, D], F32R), sb("wo_lo", [P, KI, D], F32R)
        sign = sb("sign", [P, KC, D], F32R)
        absw = sb("absw", [P, KC, D])
        sgt = sb("sgt", [P, D])
        ones = sb("ones", [P, P])
        half, eps = sb("half", [P, 1]), sb("eps", [P, 1])
        wo_raw, wf_raw = sb("wo_raw", [P, 2, DI]), sb("wf_raw", [P, 2, D])
        alpha, bias = sb("alpha", [P, D]), sb("bias", [P, D])
        ga, gb = sb("ga", [P, NB, D]), sb("gb", [P, NB, D])
        gsc, gbias = sb("gsc", [P, NB, D]), sb("gbias", [P, NB, D])
        yt = sb("yt", [P, TT, KI, P])
        y_hi, y_lo = sb("y_hi", [P, 2, KI, P], F32R), sb("y_lo", [P, 2, KI, P], F32R)
        xt, x2 = sb("xt", [P, TT, D]), sb("x2", [P, TT, D])
        att, xn = sb("att", [P, 2, D]), sb("xn", [P, 2, D])
        st_, mv, rstd = sb("st", [P, 2, 6]), sb("mv", [P, 2, 2]), sb("rstd", [P, 2, 2])
        hf = sb("hf", [P, 2, KC, P])
        h_hi, h_lo = sb("h_hi", [P, 2, KC, P], F32R), sb("h_lo", [P, 2, KC, P], F32R)
        f1, o = sb("f1", [P, 2, D]), sb("o", [P, 2, D])
        OB, TB, FB, WB = s.bank[0:2], s.bank[2:4], s.bank[4:6], s.bank[6:8]

        d_wo, d_wf, d_y, d_x, d_out = (
            [sem(f"{n}{i}") for i in range(m)] for n, m in (("d_wo", 2), ("d_wf", 2), ("d_y", 4), ("d_x", 4), ("d_out", 2)))
        d_g, konst = sem("d_g"), sem("konst")
        w_pe, w_act, w_dve, sg_half = sem("w_pe"), sem("w_act"), sem("w_dve"), sem("sg_half")
        al_pe, al_done, g_done = sem("al_pe"), sem("al_done"), sem("g_done")
        yhi_done, ylo_done, op_done = sem("yhi_done"), sem("ylo_done"), sem("op_done")
        gated, x2_done, bn_done, st_done, eps_done, rs_done, xn_done = (
            sem(n) for n in ("gated", "x2_done", "bn_done", "st_done", "eps_done", "rs_done", "xn_done"))
        tr_done, hf_done, hhi_done, hlo_done, ffn_done, f1_done, res_done, o_done = (
            sem(n) for n in ("tr_done", "hf_done", "hhi_done", "hlo_done", "ffn_done", "f1_done", "res_done", "o_done"))
        block = ctx.enter_context(nc.Block())
        NW = 8 + 4

        def run(eng, step):
            for t in range(TT):
                step(Step(0, t))
            with eng.Fori(1, NB - 1) as b:
                for t in range(TT):
                    step(Step(b, t))
            for t in range(TT):
                step(Step(NB - 1, t))

        def is_last(st):
            return isinstance(st.gp, int) and st.gp == NB - 1 and st.b == TT - 1

        def two_more(st):
            return not (isinstance(st.gp, int) and st.gp == NB - 1 and st.b >= TT - 2)

        def two_back(st):
            return not (isinstance(st.gp, int) and st.gp == 0 and st.b < 2)

        def is_first(st):
            return isinstance(st.gp, int) and st.gp == 0 and st.b == 0

        @block.sync
        def _(sp):
            y_v = s.y_d.rearrange("(k p) (b t n) -> b t p k n", p=P, b=NB, t=TT)
            x_v = x.rearrange("b (t p) d -> b t p d", p=P)
            o_v = out.rearrange("b (t p) d -> b t p d", p=P)

            def load(st):
                sp.dma_start(yt[:, st.b, :, :], y_v[st.gp, st.b]).then_inc(d_y[st.b], 16)
                sp.dma_start(xt[:, st.b, :], x_v[st.gp, st.b]).then_inc(d_x[st.b], 16)

            def store(st):
                sp.wait_ge(o_done, st.n(1, 1))
                sp.dma_start(o_v[st.gp, st.b], o[:, st.b % 2, :]).then_inc(d_out[st.b % 2], 16)

            def step(st):
                if not (isinstance(st.gp, int) and st.gp == NB - 1):
                    sp.wait_ge(ylo_done, st.n(1, 1))
                    sp.wait_ge(x2_done, st.n(1, 1))
                    load(Step(st.gp + 1, st.b))
                if not is_first(st):
                    store(st.prev())

            for r in range(2):
                sp.dma_start(wo_raw[:, r, :], w_out[r * P:(r + 1) * P, :]).then_inc(d_wo[r], 16)
            load(Step(0, 0))
            for r in range(2, 4):
                sp.wait_ge(w_pe, 2 * r - 2)
                sp.dma_start(wo_raw[:, r % 2, :], w_out[r * P:(r + 1) * P, :]).then_inc(d_wo[r % 2], 16)
            load(Step(0, 1))
            for r in range(4):
                if r >= 2:
                    sp.wait_ge(w_pe, 8 + r - 1)
                sp.dma_start(wf_raw[:, r % 2, :], w_ffn[r * P:(r + 1) * P, :]).then_inc(d_wf[r % 2], 16)
            for t in range(2, TT):
                load(Step(0, t))
            run(sp, step)
            store(Step(NB - 1, TT - 1))
            for i in range(2):
                sp.wait_ge(d_out[i], 16 * NB * TT // 2)

        @block.scalar
        def _(act):
            for b in range(NB):
                act.dma_start(ga[:, b, :], s.g_d[0, b:b + 1, :].broadcast_to([P, D])).then_inc(d_g, 16)
                act.dma_start(gb[:, b, :], s.g_d[1, b:b + 1, :].broadcast_to([P, D])).then_inc(d_g, 16)
            act.dma_start(bias[:, :], b_ffn.rearrange("(o n) -> o n", o=1).broadcast_to([P, D])).then_inc(d_g, 16)

            def split(st):
                act.wait_ge(d_y[st.b], st.gp * 16 + 16)
                wait(act, op_done, st.n(1, -1))
                act.activation(y_hi[:, st.b % 2, :, :], yt[:, st.b, :, :], ACT.Copy).then_inc(yhi_done, 1)

            def step(st):
                act.wait_ge(ylo_done, st.n(1, 1))
                if two_more(st):
                    split(st.next().next())
                act.wait_ge(w_act, NW)
                act.wait_ge(tr_done, st.n(1, 1))
                wait(act, hlo_done, st.n(1, -1))
                for k in range(KC):
                    ins = act.activation(hf[:, st.b % 2, k, :], TB[st.b % 2][:, k * P:(k + 1) * P], ACT.Identity,
                                         scale=s.mod_t[:, 2, k, st.gp].unsqueeze(1), bias=s.mod_t[:, 3, k, st.gp].unsqueeze(1))
                ins.then_inc(hf_done, 1)

            for n in range(8):
                r, hh = n // 2, n % 2
                act.wait_ge(w_pe, n + 1)
                act.activation(wo_hi[:, 4 * hh:4 * hh + 4, r * P:(r + 1) * P],
                               WB[hh][:, :].rearrange("p (k e) -> p k e", k=4), ACT.Copy).then_inc(w_act, 1)
            split(Step(0, 0))
            split(Step(0, 1))
            for r in range(4):
                act.wait_ge(w_pe, 8 + r + 1)
                act.activation(absw[:, :, r * P:(r + 1) * P], WB[r % 2][:, :].rearrange("p (k e) -> p k e", k=4),
                               ACT.Abs).then_inc(w_act, 1)
            run(act, step)

        @block.gpsimd
        def _(pool):
            pool.memset(ones[:, :], 1.0).then_inc(konst, 1)
            pool.memset(half[:, :], -0.5).then_inc(konst, 1)
            pool.memset(eps[:, :], EPS).then_inc(konst, 1)

            def split(st):
                pool.wait_ge(yhi_done, st.n(1, 1))
                pool.tensor_tensor(y_lo[:, st.b % 2, :, :], yt[:, st.b, :, :], y_hi[:, st.b % 2, :, :].bitcast(F32),
                                   ALU.subtract).then_inc(ylo_done, 1)

            def step(st):
                pool.wait_ge(st_done, st.n(1, 1))
                pool.tensor_tensor(rstd[:, st.b % 2, 0:1], mv[:, st.b % 2, 1:2], eps[:, :], ALU.add).then_inc(eps_done, 1)
                pool.wait_ge(eps_done, st.n(1, 1))
                pool.tensor_tensor(rstd[:, st.b % 2, 1:2], rstd[:, st.b % 2, 0:1], half[:, :], ALU.pow).then_inc(rs_done, 1)
                if two_more(st):
                    split(st.next().next())
                pool.wait_ge(g_done, 2)
                pool.wait_ge(x2_done, st.n(1, 1))
                wait(pool, o_done, st.n(1, -1))
                pool.tensor_tensor(f1[:, st.b % 2, :], x2[:, st.b, :], gbias[:, st.gp, :], ALU.add).then_inc(res_done, 1)

            pool.wait_ge(konst, 3)
            split(Step(0, 0))
            split(Step(0, 1))
            pool.wait_ge(d_g, 16 * 9)
            pool.wait_ge(al_done, 1)
            pool.tensor_tensor(gsc[:, :, :], gb[:, :, :], alpha[:, :].unsqueeze(1).broadcast_to([P, NB, D]),
                               ALU.mult).then_inc(g_done, 1)
            pool.tensor_tensor(gbias[:, :, :], gb[:, :, :], bias[:, :].unsqueeze(1).broadcast_to([P, NB, D]),
                               ALU.mult).then_inc(g_done, 1)
            pool.wait_ge(g_done, 2)
            run(pool, step)

        @block.vector
        def _(dve):
            def residual(st):
                dve.wait_ge(op_done, st.n(1, 1))
                wait(dve, xn_done, st.n(1, -1))
                dve.wait_ge(d_x[st.b], st.gp * 16 + 16)
                dve.tensor_tensor(att[:, st.b % 2, :], OB[st.b % 2][:, :], ga[:, st.gp, :], ALU.mult).then_inc(gated, 1)
                dve.wait_ge(gated, st.n(1, 1))
                wait(dve, res_done, st.n(1, -3))
                dve.tensor_tensor(x2[:, st.b, :], att[:, st.b % 2, :], xt[:, st.b, :], ALU.add).then_inc(x2_done, 1)
                dve.wait_ge(x2_done, st.n(1, 1))
                dve.bn_stats(st_[:, st.b % 2, :], x2[:, st.b, :]).then_inc(bn_done, 1)
                dve.wait_ge(w_dve, NW)
                dve.wait_ge(bn_done, st.n(1, 1))
                wait(dve, rs_done, st.n(1, -1))
                dve.bn_aggr(mv[:, st.b % 2, :], st_[:, st.b % 2, :]).then_inc(st_done, 1)

            def normalize(st):
                dve.wait_ge(rs_done, st.n(1, 1))
                wait(dve, tr_done, st.n(1, -1))
                dve.tensor_scalar(xn[:, st.b % 2, :], x2[:, st.b, :], mv[:, st.b % 2, 0:1], rstd[:, st.b % 2, 1:2],
                                  ALU.subtract, ALU.mult).then_inc(xn_done, 1)

            def split(st):
                dve.wait_ge(hf_done, st.n(1, 1))
                wait(dve, ffn_done, st.n(1, -1))
                dve.tensor_copy(h_hi[:, st.b % 2, :, :], hf[:, st.b % 2, :, :]).then_inc(hhi_done, 1)
                dve.wait_ge(hhi_done, st.n(1, 1))
                dve.tensor_tensor(h_lo[:, st.b % 2, :, :], hf[:, st.b % 2, :, :], h_hi[:, st.b % 2, :, :].bitcast(F32),
                                  ALU.subtract).then_inc(hlo_done, 1)

            def finish(st):
                dve.wait_ge(ffn_done, st.n(1, 1))
                if st.b >= 2:
                    dve.wait_ge(d_out[st.b % 2], st.gp * 32 + 16)
                elif not (isinstance(st.gp, int) and st.gp == 0):
                    dve.wait_ge(d_out[st.b % 2], st.gp * 32)
                dve.tensor_tensor(o[:, st.b % 2, :], FB[st.b % 2][:, :], gsc[:, st.gp, :], ALU.mult).then_inc(f1_done, 1)
                dve.wait_ge(f1_done, st.n(1, 1))
                dve.wait_ge(res_done, st.n(1, 1))
                dve.tensor_tensor(o[:, st.b % 2, :], o[:, st.b % 2, :], f1[:, st.b % 2, :], ALU.add).then_inc(o_done, 1)

            def step(st):
                residual(st)
                if two_back(st):
                    finish(st.prev().prev())
                normalize(st)
                if not is_first(st):
                    split(st.prev())

            for n in range(8):
                r, hh = n // 2, n % 2
                dve.wait_ge(w_act, n + 1)
                w = wo_hi[:, 4 * hh:4 * hh + 4, r * P:(r + 1) * P]
                dve.tensor_tensor(wo_lo[:, 4 * hh:4 * hh + 4, r * P:(r + 1) * P],
                                  WB[hh][:, :].rearrange("p (k e) -> p k e", k=4), w.bitcast(F32),
                                  ALU.subtract).then_inc(w_dve, 1)
            for r in range(4):
                dve.wait_ge(w_act, 8 + r + 1)
                wait(dve, w_dve, 8 + r)
                dve.tensor_scalar(sgt[:, :], WB[r % 2][:, :], 0.0, 2.0, ALU.is_ge, ALU.mult).then_inc(sg_half, 1)
                dve.wait_ge(sg_half, r + 1)
                dve.tensor_scalar(sign[:, :, r * P:(r + 1) * P], sgt[:, :].rearrange("p (k e) -> p k e", k=4),
                                  -1.0, None, ALU.add).then_inc(w_dve, 1)
            dve.wait_ge(al_pe, 1)
            dve.tensor_scalar(alpha[:, :], FB[0][:, :], 1.0 / D, None, ALU.mult).then_inc(al_done, 1)
            dve.wait_ge(g_done, 2)
            run(dve, step)
            finish(Step(NB - 1, TT - 2))
            split(Step(NB - 1, TT - 1))
            finish(Step(NB - 1, TT - 1))

        @block.tensor
        def _(pe):
            def project(st):
                pe.wait_ge(ylo_done, st.n(1, 1))
                wait(pe, gated, st.n(1, -1))
                i = st.b % 2
                for k in range(KI):
                    for n, (y, w) in enumerate(((y_hi, wo_hi), (y_lo, wo_hi), (y_hi, wo_lo))):
                        ins = pe.matmul(OB[i][:, :], y[:, i, k, :], w[:, k, :], start=(k == 0 and n == 0),
                                        stop=(k == KI - 1 and n == 2))
                ins.then_inc(op_done, 1)

            def turn(st):
                i = st.b % 2
                pe.wait_ge(xn_done, st.n(1, 1))
                wait(pe, hf_done, st.n(1, -1))
                for k in range(KC):
                    ins = pe.transpose(TB[i][:, k * P:(k + 1) * P], xn[:, i, k * P:(k + 1) * P], s.ident[:, :])
                ins.then_inc(tr_done, 1)

            def linear(st):
                i = st.b % 2
                pe.wait_ge(hlo_done, st.n(1, 1))
                wait(pe, f1_done, st.n(1, -1))
                for k in range(KC):
                    for n, h in enumerate((h_hi, h_lo)):
                        ins = pe.matmul(FB[i][:, :], h[:, i, k, :], sign[:, k, :], start=(k == 0 and n == 0),
                                        stop=(k == KC - 1 and n == 1))
                ins.then_inc(ffn_done, 1)

            def step(st):
                if not is_last(st):
                    project(st.next())
                turn(st)
                if not is_first(st):
                    linear(st.prev())

            for n in range(NW):
                r, hh = (n // 2, n % 2) if n < 8 else (n - 8, n % 2)
                if n < 8:
                    pe.wait_ge(d_wo[r % 2], 16 * (r // 2 + 1))
                else:
                    pe.wait_ge(d_wf[r % 2], 16 * (r // 2 + 1))
                if n >= 2:
                    pe.wait_ge(w_dve, n - 1)
                src = wo_raw[:, r % 2, hh * 512:(hh + 1) * 512] if n < 8 else wf_raw[:, r % 2, :]
                for k in range(4):
                    ins = pe.transpose(WB[n % 2][:, k * P:(k + 1) * P], src[:, k * P:(k + 1) * P], s.ident[:, :])
                ins.then_inc(w_pe, 1)
            pe.wait_ge(konst, 3)
            pe.wait_ge(w_act, NW)
            for k in range(KC):
                ins = pe.matmul(FB[0][:, :], ones[:, :], absw[:, k, :], start=(k == 0), stop=(k == KC - 1))
            ins.then_inc(al_pe, 1)
            pe.wait_ge(w_dve, NW)
            pe.wait_ge(al_done, 1)
            project(Step(0, 0))
            run(pe, step)
            linear(Step(NB - 1, TT - 1))


_INS = ['L0_attn_input_', 'L0_attn_in_proj_w', 'L0_attn_conv1d_weight', 'L0_attn_conv1d_bias', 'L0_attn_z_bias',
        'L0_attn_D', 'L0_attn_out_proj_w', 'L0_ffn_weight', 'L0_ffn_bias', 'L0_c', 'L0_wmod']
_OUTS = [((NB, L, D), 'float32')]


def kernel(**inputs):
    import numpy as _np
    import concourse.bacc as _bacc
    from concourse import mybir as _mybir
    from concourse.bass_utils import run_bass_kernel_spmd as _run

    nc = _bacc.Bacc("TRN2", target_bir_lowering=False, num_devices=1)
    arrays, args = {}, {}
    for name in _INS:
        a = _np.ascontiguousarray(inputs[name])
        arrays[f"in_{name}_dram"] = a
        args[name] = nc.dram_tensor(f"in_{name}_dram", a.shape, _mybir.dt.from_np(a.dtype), kind="ExternalInput").ap()
    for i, (shape, dtype) in enumerate(_OUTS):
        dt = _mybir.dt.from_np(_np.dtype(dtype))
        out = nc.dram_tensor(f"out_{i}_dram", shape, dt, kind="ExternalOutput").ap()
    adaln_kernel(nc, args['L0_attn_input_'], args['L0_attn_in_proj_w'], args['L0_attn_conv1d_weight'],
                 args['L0_attn_conv1d_bias'], args['L0_attn_z_bias'], args['L0_attn_D'], args['L0_attn_out_proj_w'],
                 args['L0_ffn_weight'], args['L0_ffn_bias'], args['L0_c'], args['L0_wmod'], out)
    r = _run(nc, [arrays], core_ids=[0])
    got = tuple(r.results[0][f"out_{i}_dram"] for i in range(len(_OUTS)))
    return got[0]
```

```python
from contextlib import ExitStack

import concourse.bass as bass
from concourse import mybir

F32 = mybir.dt.float32
F32R = mybir.dt.float32r
ALU = mybir.AluOpType
ACT = mybir.ActivationFunctionType

P = 128
NB, L, D = 4, 512, 512
DI, NG, NS, NH = 1024, 8, 64, 64
HD = DI // NH
HG = NH // NG
KC = D // P
Q = 128
NC = L // Q
GP = NG // 2
NT = 6
KS = 4
BIG = 16384.0
DT_MAX = 87.0
EPS = 1e-5

R_NEG, R_POS, R_ALL = 64, 80, 82

GROUPS = [[0], [1], [2, 3], [4, 5]] + [[m] for m in range(6, 18)]
FS = [2, 3, 6, 9, 12, 15]
W_SLOT = [6, 7, 10, 11, 14, 15, 18, 19, 22, 23, 26, 27]
PREP = 1


class Step:

    def __init__(self, gp, b):
        self.gp, self.b = gp, b

    def n(self, per_step, off):
        return self.gp * (4 * per_step) + (per_step * self.b + off)

    def next(self):
        return Step(self.gp, self.b + 1) if self.b < 3 else Step(self.gp + 1, 0)

    def prev(self):
        return Step(self.gp, self.b - 1) if self.b else Step(self.gp - 1, 3)

    @property
    def par(self):
        return self.b % 2


def wait(eng, sem, count):
    if not isinstance(count, int) or count > 0:
        eng.wait_ge(sem, count)


class Shared:
    pass


def overlaid(nc, ctx, name, shape):
    with nc.sbuf_tensor(name, shape, F32R) as early:
        pass
    late = ctx.enter_context(nc.sbuf_tensor(name + "_place", shape, F32))
    return early, late


def adaln_kernel(nc, x, w_in, conv_w, conv_b, z_bias, d_skip, w_out, w_ffn, b_ffn, cond, w_mod, out):
    with ExitStack() as ctx:
        s = Shared()

        def sb(name, shape, dt=F32):
            return ctx.enter_context(nc.sbuf_tensor(name, shape, dt))

        s.bank = [ctx.enter_context(nc.psum_tensor(f"bank{i}", [P, 512], F32)) for i in range(8)]
        s.ident = sb("ident", [P, P])
        s.tri = sb("tri", [P, P])
        s.mod_t = sb("mod_t", [P, 4, KC, NB])
        s.h_hi = sb("h_hi", [P, NB, KC, L], F32R)
        s.h_lo, h_place = overlaid(nc, ctx, "h_lo", [P, NB, KC, L])
        s.wo_hi = [s.h_hi[:, k // 4, k % 4, :] for k in range(DI // P)]
        s.wo_lo = [s.h_hi[:, 2 + k // 4, k % 4, :] for k in range(DI // P)]
        s.sign = s.h_lo[:, 0, :, :]
        s.absw = h_place[:, 1, :, :]
        s.yt = [h_place[:, 2 + t // 2, 2 * (t % 2):2 * (t % 2) + 2, :] for t in range(4)]
        s.w_lo, s.w_place = overlaid(nc, ctx, "w_lo", [P, NT, KC, P])
        s.xt = [s.w_place[:, 1 + t, :, :].rearrange("p k n -> p (k n)") for t in range(4)]
        s.alpha = s.w_place[:, 5, :, :].rearrange("p k n -> p (k n)")
        s.ones = sb("ones", [P, P])
        s.d_y = [ctx.enter_context(nc.semaphore(f"d_y{t}")) for t in range(4)]
        s.d_x = [ctx.enter_context(nc.semaphore(f"d_x{t}")) for t in range(4)]
        s.y_d = nc.dram_tensor("y_scratch", (NG * P, NB * L), F32).ap()
        s.ea_d = nc.dram_tensor("ea_scratch", (NB * NH, L), F32).ap()
        s.dd_d = nc.dram_tensor("dd_scratch", (NB * NH, L), F32).ap()
        s.a_d = nc.dram_tensor("a_scratch", (2, NB * NH, L), F32).ap()
        s.na_d = nc.dram_tensor("na_scratch", (2, NB * NH, L), F32).ap()
        s.cd_d = nc.dram_tensor("cd_scratch", (NH, NB * NC), F32).ap()
        s.g_d = nc.dram_tensor("gate_scratch", (2, NB, D), F32).ap()
        with ExitStack() as main_ctx:
            def sbm(name, shape, dt=F32):
                return main_ctx.enter_context(nc.sbuf_tensor(name, shape, dt))

            s.w_hi, s.raw_lin = overlaid(nc, main_ctx, "w_hi", [P, NT, KC, P])
            s.R = sbm("R", [R_ALL, 2, 2, HG * Q], F32R)
            s.Lm = sbm("Lm", [R_ALL, 2, 2, Q], F32R)
            s.wend = sbm("wend", [P, GP, NB, NC, 2 * HG])
            s.gpc = sbm("gpc", [P, GP, 4 * (KS + 1) + 2])
            prologue(nc, s, x, w_in, conv_w, conv_b, z_bias, d_skip, cond, w_mod)
            main_part(nc, s, x, w_in, w_out, w_ffn)
        tail_part(nc, s, x, b_ffn, out)


def tile_rows(gp, t):
    if t < 2:
        return (2 * gp + t) * P
    if t < 4:
        return gp * P + (DI if t == 2 else DI + NG * NS)
    return (2 * gp + t - 4) * P + DI + 2 * NG * NS


def prologue(nc, s, x, w_in, conv_w, conv_b, z_bias, d_skip, cond, w_mod):
    with ExitStack() as ctx:
        def sb(name, shape, dt=F32):
            return ctx.enter_context(nc.sbuf_tensor("p_" + name, shape, dt))

        def sem(name):
            return ctx.enter_context(nc.semaphore("p_" + name))

        scT = sb("scT", [P, KC, NB])
        wm = sb("wm", [P, 2, KC, D])
        xt, xn = sb("xt", [P, 4, D]), sb("xn", [P, 2, D])
        st, mv, rstd = sb("st", [P, 2, 6]), sb("mv", [P, 2, 2]), sb("rstd", [P, 2, 2])
        half = sb("half", [P, 1])
        hf = sb("hf", [P, 2, L])
        stage = sb("stage", [R_ALL, HG * Q])
        lstage = sb("lstage", [R_ALL, Q])
        wa_hi, wa_lo = sb("wa_hi", [P, KC, 192], F32R), sb("wa_lo", [P, KC, 192], F32R)
        wraw, wst = sb("wraw", [P, 2, D]), sb("wst", [P, 2, 2 * P])
        rows, rabs, rsg = sb("rows", [NB, 2, D]), sb("rabs", [NB, 2, D]), sb("rsg", [NB, 2, D])
        c4, th4, sc4 = rsg[:, 0, :], rabs[:, 0, :], rabs[:, 1, :]
        chunk_on = sb("chunk_on", [P, L])
        dcol, dhalf = sb("dcol", [P, 1]), sb("dhalf", [P, 1])
        R_, E_, DEN, SV, TT_, PL, DT, TMP = [sb(f"a{i}", [P, 2, L]) for i in range(8)]
        cde = sb("cde", [P, 2, NC])
        wa_raw = TMP[0:NH, 0, :]

        d_c, d_wa, d_small, d_scr, d_gate = sem("d_c"), sem("d_wa"), sem("d_small"), sem("d_scr"), sem("d_gate")
        d_x, d_wm, d_w = [sem(f"d_x{i}") for i in range(4)], [sem(f"d_wm{i}") for i in range(2)], [sem(f"d_w{i}") for i in range(2)]
        konst, kcopy = sem("konst"), sem("kcopy")
        sc_ready, sct_pe, sct_ready = sem("sc_ready"), sem("sct_pe"), sem("sct_ready")
        th_ready, mod_pe, mod_ready = sem("th_ready"), sem("mod_pe"), sem("mod_ready")
        gate_abs, gate_v, gate_ready = sem("gate_abs"), sem("gate_v"), sem("gate_ready")
        ln_bn, ln_st, ln_eps, ln_rs, ln_n = sem("ln_bn"), sem("ln_st"), sem("ln_eps"), sem("ln_rs"), sem("ln_n")
        t_pe, h_hi, h_act = sem("t_pe"), sem("h_hi"), sem("h_act")
        h_lo = [sem("h_lo_pool"), sem("h_lo_dve")]
        wa_pe, wa_act, wa_dve, dh_ready = sem("wa_pe"), sem("wa_act"), sem("wa_dve"), sem("dh_ready")
        wt_pe, w_act, w_pool = sem("wt_pe"), sem("w_act"), sem("w_pool")
        a_pe, we_pe, we_ev = sem("a_pe"), sem("we_pe"), sem("we_ev")
        a_exp, a_act, a_v, a_pool = ([sem(f"{n}{i}") for i in range(2)] for n in ("a_exp", "a_act", "a_v", "a_pool"))
        N_SMALL = 10 + 2
        A_SUM, A_END, A_LO, A_DD = 17, 18, 19, 21
        B_HI, B_EA, B_CD, B_WE, B_NEG = 1, 2, 3, 4, 5
        SEC = [1, 0, 4, 3, 2, 5]
        MOD, DTB, GATE, WB, WE = (s.bank[6], s.bank[2]), s.bank[0:2], s.bank[3:5], s.bank[5:7], (s.bank[7], s.bank[0])
        block = ctx.enter_context(nc.Block())

        @block.sync
        def _(sp):
            wmv = w_mod.rearrange("(k p) n -> p k n", p=P)
            xv = x.rearrange("b (t p) d -> (b t) p d", p=P)

            def load_x(i):
                if i >= 4:
                    sp.wait_ge(ln_n, i - 3)
                sp.dma_start(xt[:, i % 4, :], xv[i]).then_inc(d_x[i % 4], 16)

            def load_section(n):
                if n >= 2:
                    sp.wait_ge(mod_pe, n - 1)
                sp.dma_start(wm[:, n % 2, :, :], wmv[:, :, SEC[n] * D:(SEC[n] + 1) * D]).then_inc(d_wm[n % 2], 16)

            def load_weights(t):
                if t >= 2:
                    sp.wait_ge(wt_pe, 2 * (t - 2) + 2)
                sp.dma_start(wraw[:, t % 2, :], w_in[tile_rows(0, t):tile_rows(0, t) + P, :]).then_inc(d_w[t % 2], 16)

            sp.dma_start(c4, cond).then_inc(d_c, 16)
            load_section(0)
            load_x(0)
            load_x(1)
            load_section(1)
            load_x(2)
            load_x(3)
            sp.dma_start(wa_raw, w_in[2 * DI + 2 * NG * NS:, :]).then_inc(d_wa, 16)
            for i in range(4, 16):
                load_x(i)
            load_section(2)
            load_section(3)
            for t in range(NT):
                load_weights(t)
            load_section(4)
            load_section(5)
            for pb in range(2):
                rows2 = slice(pb * P, pb * P + P)
                sp.wait_ge(a_v[pb], A_DD)
                sp.dma_start(s.dd_d[rows2, :], DEN[:, pb, :]).then_inc(d_scr, 16)
                sp.wait_ge(a_v[pb], A_LO)
                sp.dma_start(s.a_d[0, rows2, :], E_[:, pb, :]).then_inc(d_scr, 16)
                sp.dma_start(s.a_d[1, rows2, :], SV[:, pb, :]).then_inc(d_scr, 16)
                sp.wait_ge(a_act[pb], B_NEG)
                sp.dma_start(s.na_d[0, rows2, :], R_[:, pb, :]).then_inc(d_scr, 16)
                sp.wait_ge(a_pool[pb], 2)
                sp.dma_start(s.na_d[1, rows2, :], PL[:, pb, :]).then_inc(d_scr, 16)
                sp.dma_start(s.ea_d[rows2, :], TT_[:, pb, :]).then_inc(d_scr, 16)
                for q in range(2):
                    b = 2 * pb + q
                    with nc.allow_non_contiguous_dma(reason="a few decays per head"):
                        sp.dma_start(s.cd_d[:, b * NC:(b + 1) * NC], cde[64 * q:64 * q + 64, pb, :]).then_inc(d_scr, 16)
            sp.wait_ge(gate_ready, 2)
            sp.dma_start(s.g_d.rearrange("g b d -> b g d"), rows[:, :, :]).then_inc(d_gate, 16)
            sp.wait_ge(d_scr, 16 * 16)
            sp.wait_ge(d_gate, 16)

        @block.gpsimd
        def _(pool):
            pool.memset(half[:, :], -0.5).then_inc(konst, 1)
            pool.wait_ge(konst, 1)
            pool.memset(s.ident[:, :], 0.0).then_inc(konst, 1)
            pool.wait_ge(konst, 2)
            pool.affine_select(out=s.ident[:, :], in_=s.ident[:, :], compare_op=ALU.not_equal, fill=1.0,
                               base=0, pattern=[[-1, P]], channel_multiplier=1).then_inc(konst, 1)
            pool.wait_ge(konst, 3)
            pool.memset(wa_hi[:, :, :].bitcast(F32), 0.0).then_inc(konst, 1)
            pool.wait_ge(konst, 4)
            pool.memset(wa_lo[:, :, :].bitcast(F32), 0.0).then_inc(konst, 1)

            def low_part(n):
                b, k = n // KC, n % KC
                pool.wait_ge(h_act, n + 1)
                pool.tensor_tensor(s.h_lo[:, b, k, :], hf[:, n % 2, :], s.h_hi[:, b, k, :].bitcast(F32),
                                   ALU.subtract).then_inc(h_lo[0], 1)

            def decay_constants():
                pool.memset(s.tri[:, :], 0.125).then_inc(konst, 1)
                pool.wait_ge(konst, 6)
                pool.memset(stage[:, :], 0.0).then_inc(konst, 1)
                pool.wait_ge(konst, 7)
                pool.memset(lstage[0:64, :], 0.0).then_inc(konst, 1)
                pool.wait_ge(konst, 8)
                pool.memset(lstage[64:R_ALL, :], 1.0).then_inc(konst, 1)
                pool.wait_ge(konst, 9)
                pool.memset(chunk_on[:, :], 1.0).then_inc(konst, 1)
                pool.wait_ge(konst, 10)
                pool.affine_select(out=s.tri[:, :], in_=s.tri[:, :], compare_op=ALU.is_ge, fill=0.0,
                                   base=0, pattern=[[1, P]], channel_multiplier=-1).then_inc(konst, 1)
                mrow = stage[0:64, :].rearrange("p (h s) -> p h s", h=HG)
                pool.wait_ge(konst, 11)
                pool.affine_select(out=mrow, in_=mrow, compare_op=ALU.is_ge, fill=-BIG,
                                   base=0, pattern=[[0, HG], [1, Q]], channel_multiplier=-2).then_inc(konst, 1)
                lrow = lstage[0:64, :].rearrange("p (z r) -> p z r", r=2)
                pool.wait_ge(konst, 12)
                pool.affine_select(out=lrow, in_=lrow, compare_op=ALU.not_equal, fill=1.0,
                                   base=0, pattern=[[-1, Q // 2], [0, 2]], channel_multiplier=1).then_inc(konst, 1)
                drow = stage[64:80, :].rearrange("p (h s) -> p h s", h=HG)
                pool.wait_ge(konst, 13)
                pool.affine_select(out=drow, in_=drow, compare_op=ALU.not_equal, fill=1.0,
                                   base=0, pattern=[[-1, HG], [0, Q]], channel_multiplier=1).then_inc(konst, 1)
                pool.wait_ge(konst, 14)
                pool.affine_select(out=drow, in_=drow, compare_op=ALU.not_equal, fill=1.0,
                                   base=-HG, pattern=[[-1, HG], [0, Q]], channel_multiplier=1).then_inc(konst, 1)
                cmv = chunk_on[:, :].rearrange("p (c q) -> p c q", q=Q)
                pool.wait_ge(konst, 15)
                pool.affine_select(out=cmv, in_=cmv, compare_op=ALU.not_equal, fill=0.0,
                                   base=0, pattern=[[0, NC], [1, Q]], channel_multiplier=0).then_inc(konst, 1)

            for i in range(16 + 5):
                if i < 16:
                    pool.wait_ge(ln_st, i + 1)
                    if i >= 2:
                        pool.wait_ge(ln_n, i - 1)
                    pool.tensor_scalar(rstd[:, i % 2, 0:1], mv[:, i % 2, 1:2], EPS, None, ALU.add).then_inc(ln_eps, 1)
                    pool.wait_ge(ln_eps, i + 1)
                    pool.tensor_tensor(rstd[:, i % 2, 1:2], rstd[:, i % 2, 0:1], half[:, :], ALU.pow).then_inc(ln_rs, 1)
                if i >= 5 and i % 2 == 1:
                    low_part(i - 5)
            pool.wait_ge(konst, 5)
            decay_constants()

            def scale(pb):
                pool.wait_ge(a_act[pb], B_EA)
                pool.tensor_scalar(TT_[:, pb, :], TT_[:, pb, :], 0.125, None, ALU.mult).then_inc(a_pool[pb], 1)
                pool.wait_ge(a_act[pb], B_CD)
                pool.wait_ge(a_v[pb], A_LO)
                pool.tensor_scalar(PL[:, pb, :], SV[:, pb, :], -1.0, None, ALU.mult).then_inc(a_pool[pb], 1)

            def weights(n):
                t, w = n // 2, slice(2 * (n % 2), 2 * (n % 2) + 2)
                pool.wait_ge(w_act, n + 1)
                pool.tensor_tensor(s.w_lo[:, t, w, :], wst[:, n % 2, :].rearrange("p (k r) -> p k r", k=2),
                                   s.w_hi[:, t, w, :].bitcast(F32), ALU.subtract).then_inc(w_pool, 1)

            for pb in range(2):
                for n in range(NT * pb, NT * pb + NT):
                    weights(n)
            for pb in range(2):
                scale(pb)
            pool.wait_ge(d_small, 16 * N_SMALL)

        @block.vector
        def _(dve):
            dve.wait_ge(d_c, 16)
            dve.wait_ge(th_ready, 1)
            dve.scalar_tensor_tensor(out=sc4, in0=th4, scalar=1.0, in1=c4,
                                     op0=ALU.add, op1=ALU.mult).then_inc(sc_ready, 1)
            dve.wait_ge(sct_pe, 1)
            dve.tensor_scalar(scT[:, :, :], s.bank[4][:, 0:KC * NB].rearrange("p (k b) -> p k b", k=KC),
                              0.5, None, ALU.mult).then_inc(sct_ready, 1)

            def modulation(n):
                dve.wait_ge(mod_pe, n // 2 * 2 + 2)
                dve.tensor_scalar(s.mod_t[:, n, :, :],
                                  MOD[n // 2][:, n * KC * NB:(n + 1) * KC * NB].rearrange("p (k b) -> p k b", k=KC),
                                  1.0 - n % 2, None, ALU.add).then_inc(mod_ready, 1)

            def statistics(i):
                dve.wait_ge(d_x[i % 4], 16 * (i // 4 + 1))
                dve.bn_stats(st[:, i % 2, :], xt[:, i % 4, :]).then_inc(ln_bn, 1)
                dve.wait_ge(ln_bn, i + 1)
                if i >= 2:
                    dve.wait_ge(ln_rs, i - 1)
                    dve.wait_ge(ln_n, i - 1)
                dve.bn_aggr(mv[:, i % 2, :], st[:, i % 2, :]).then_inc(ln_st, 1)

            def normalize(i):
                dve.wait_ge(ln_rs, i + 1)
                if i >= 2:
                    dve.wait_ge(t_pe, i - 1)
                dve.tensor_scalar(xn[:, i % 2, :], xt[:, i % 4, :], mv[:, i % 2, 0:1], rstd[:, i % 2, 1:2],
                                  ALU.subtract, ALU.mult).then_inc(ln_n, 1)

            def low_part(n):
                b, k = n // KC, n % KC
                dve.wait_ge(h_act, n + 1)
                dve.tensor_tensor(s.h_lo[:, b, k, :], hf[:, n % 2, :], s.h_hi[:, b, k, :].bitcast(F32),
                                  ALU.subtract).then_inc(h_lo[1], 1)

            statistics(0)
            for i in range(16 + 5):
                if i < 15:
                    statistics(i + 1)
                if i >= 5 and i % 2 == 0:
                    low_part(i - 5)
                if i < 16:
                    normalize(i)
                if i == 3:
                    modulation(0)
                    modulation(1)
                    dve.wait_ge(wa_act, 1)
                    dve.tensor_tensor(wa_lo[:, :, 64:128], s.bank[5][:, 0:KC * NH].rearrange("p (k h) -> p k h", k=KC),
                                      wa_hi[:, :, 64:128].bitcast(F32), ALU.subtract).then_inc(wa_dve, 1)
            dve.wait_ge(d_small, 16 * N_SMALL)
            dve.tensor_scalar(dhalf[:, :], dcol[:, :], 0.5, None, ALU.mult).then_inc(dh_ready, 1)
            done = [0, 0]

            def link(pb, ins):
                done[pb] += 1
                ins.then_inc(a_v[pb], 1)

            def linked(pb):
                dve.wait_ge(a_v[pb], done[pb])

            def half_of(pb):
                return (t[:, pb, :] for t in (R_, E_, DEN, SV, TT_, PL, DT, TMP))

            for pb in range(2):
                r, e, den, sv, tt, pl, dt, tmp = half_of(pb)
                dve.wait_ge(a_pe, pb + 1)
                link(pb, dve.tensor_scalar(r, DTB[pb][:, :], 0.0, None, ALU.max))
                dve.wait_ge(a_exp[pb], 2)
                link(pb, dve.tensor_scalar(den, e, 2.0, None, ALU.add))
                linked(pb)
                link(pb, dve.reciprocal(tmp, den))
            for pb in range(2):
                r, e, den, sv, tt, pl, dt, tmp = half_of(pb)
                linked(pb)
                link(pb, dve.tensor_tensor(sv, e, tmp, ALU.mult))
            for pb in range(2):
                r, e, den, sv, tt, pl, dt, tmp = half_of(pb)
                linked(pb)
                link(pb, dve.tensor_tensor(tt, sv, sv, ALU.mult))
            for pb in range(2):
                r, e, den, sv, tt, pl, dt, tmp = half_of(pb)
                linked(pb)
                link(pb, dve.tensor_scalar(pl, tt, 1.0 / 17, None, ALU.mult))
            for k in (15, 13, 11, 9, 7, 5, 3):
                for pb in range(2):
                    r, e, den, sv, tt, pl, dt, tmp = half_of(pb)
                    linked(pb)
                    link(pb, dve.scalar_tensor_tensor(out=pl, in0=pl, scalar=1.0 / k, in1=tt, op0=ALU.add, op1=ALU.mult))
            for pb in range(2):
                r, e, den, sv, tt, pl, dt, tmp = half_of(pb)
                linked(pb)
                link(pb, dve.scalar_tensor_tensor(out=pl, in0=pl, scalar=1.0, in1=sv, op0=ALU.add, op1=ALU.mult))
            for pb in range(2):
                r, e, den, sv, tt, pl, dt, tmp = half_of(pb)
                linked(pb)
                link(pb, dve.scalar_tensor_tensor(out=dt, in0=pl, scalar=2.0, in1=r, op0=ALU.mult, op1=ALU.add))
            for pb in range(2):
                r, e, den, sv, tt, pl, dt, tmp = half_of(pb)
                linked(pb)
                link(pb, dve.tensor_scalar(tmp, dt, DT_MAX, -1.0, ALU.min, ALU.mult))
            dve.wait_ge(konst, 16)
            for pb in range(2):
                r, e, den, sv, tt, pl, dt, tmp = half_of(pb)
                linked(pb)
                link(pb, dve.tensor_tensor_scan(out=pl, data0=chunk_on[:, :], data1=tmp, initial=0.0,
                                                op0=ALU.mult, op1=ALU.add))
                assert done[pb] == A_SUM
            for pb in range(2):
                r, e, den, sv, tt, pl, dt, tmp = half_of(pb)
                plv = pl.rearrange("p (c q) -> p c q", q=Q)
                linked(pb)
                link(pb, dve.tensor_tensor(tmp.rearrange("p (c q) -> p c q", q=Q),
                                           plv[:, :, Q - 1:Q].broadcast_to([P, NC, Q]), plv, ALU.subtract))
                assert done[pb] == A_END
            for pb in range(2):
                r, e, den, sv, tt, pl, dt, tmp = half_of(pb)
                dve.wait_ge(a_act[pb], B_HI)
                link(pb, dve.tensor_tensor(sv, pl, e, ALU.subtract))
                assert done[pb] == A_LO
            dve.wait_ge(dh_ready, 1)
            for pb in range(2):
                r, e, den, sv, tt, pl, dt, tmp = half_of(pb)
                link(pb, dve.reciprocal(den, dt))
                linked(pb)
                link(pb, dve.tensor_scalar(den, den, dhalf[:, 0:1], None, ALU.mult))
                assert done[pb] == A_DD
            modulation(2)
            modulation(3)
            dve.wait_ge(gate_abs, 2)
            for n in range(2):
                dve.tensor_scalar(rsg[:, n, :], GATE[n][0:NB, :], 0.0, 2.0, ALU.is_ge, ALU.mult).then_inc(gate_v, 1)
            dve.wait_ge(gate_v, 2)
            dve.tensor_scalar(rsg[:, :, :], rsg[:, :, :], -1.0, None, ALU.add).then_inc(gate_v, 1)
            dve.tensor_scalar(rabs[:, 0, :], rabs[:, 0, :], 0.25, 0.5, ALU.max, ALU.mult).then_inc(gate_v, 1)
            dve.tensor_scalar(rabs[:, 1, :], rabs[:, 1, :], 0.25, None, ALU.max).then_inc(gate_v, 1)
            dve.wait_ge(gate_v, 5)
            for n in range(2):
                dve.tensor_tensor(rows[:, n, :], rsg[:, n, :], rabs[:, n, :], ALU.mult).then_inc(gate_ready, 1)

        @block.scalar
        def _(act):
            cwv = conv_w.rearrange("(g p) o k -> p g (o k)", p=P)
            cbv = conv_b.rearrange("(g p o) -> p g o", p=P, o=1)
            zbv = z_bias.rearrange("(g p o) -> p g o", p=P, o=1)
            dv = d_skip.rearrange("(h o) -> h o", o=1)
            act.wait_ge(d_c, 16)
            act.activation(th4, c4, ACT.Tanh, scale=0.5).then_inc(th_ready, 1)
            with nc.allow_non_contiguous_dma(reason="small vectors laid out by partition"):
                for t in range(4):
                    n = slice(t, 8, 2) if t < 2 else slice(4 * t, 4 * t + 4)
                    o = t * (KS + 1)
                    act.dma_start(s.gpc[:, :, o:o + KS], cwv[:, n, :]).then_inc(d_small, 16)
                    act.dma_start(s.gpc[:, :, o + KS:o + KS + 1], cbv[:, n, :]).then_inc(d_small, 16)
                for t in range(2):
                    act.dma_start(s.gpc[:, :, 20 + t:21 + t], zbv[:, t:8:2, :]).then_inc(d_small, 16)
                act.dma_start(dcol[0:64, :], dv).then_inc(d_small, 16)
                act.dma_start(dcol[64:128, :], dv).then_inc(d_small, 16)
            act.wait_ge(konst, 5)
            act.wait_ge(wa_pe, 1)
            act.activation(wa_hi[:, :, 64:128], s.bank[5][:, 0:KC * NH].rearrange("p (k h) -> p k h", k=KC),
                           ACT.Copy).then_inc(wa_act, 1)
            act.wait_ge(mod_ready, 2)

            def make_h(n):
                b, k = n // KC, n % KC
                act.wait_ge(t_pe, 4 * b + 4)
                scale, bias = s.mod_t[:, 0, k, b:b + 1], s.mod_t[:, 1, k, b:b + 1]
                act.activation(s.h_hi[:, b, k, :], s.bank[4 * (b % 2) + k][:, :], ACT.Identity, scale=scale, bias=bias).then_inc(h_hi, 1)
                if n >= 2:
                    act.wait_ge(h_lo[n % 2], n // 2)
                act.activation(hf[:, n % 2, :], s.bank[4 * (b % 2) + k][:, :], ACT.Identity, scale=scale, bias=bias).then_inc(h_act, 1)

            def softplus_inputs(pb):
                act.wait_ge(a_v[pb], 1)
                act.activation(E_[:, pb, :], DTB[pb][:, :], ACT.Abs).then_inc(a_exp[pb], 1)
                act.wait_ge(a_exp[pb], 1)
                act.activation(E_[:, pb, :], E_[:, pb, :], ACT.Exp, scale=-1.0).then_inc(a_exp[pb], 1)

            def decays(pb):
                act.wait_ge(a_v[pb], A_SUM)
                act.activation(E_[:, pb, :].bitcast(F32R), PL[:, pb, :], ACT.Copy).then_inc(a_act[pb], 1)
                act.activation(TT_[:, pb, :], PL[:, pb, :], ACT.Exp).then_inc(a_act[pb], 1)
                act.activation(cde[:, pb, :], PL[:, pb, :].rearrange("p (c q) -> p c q", q=Q)[:, :, Q - 1], ACT.Exp)\
                   .then_inc(a_act[pb], 1)
                act.wait_ge(a_v[pb], A_END)
                act.activation(TMP[:, pb, :], TMP[:, pb, :], ACT.Exp).then_inc(a_act[pb], 1)
                act.wait_ge(a_act[pb], B_HI)
                act.activation(R_[:, pb, :], E_[:, pb, :], ACT.Copy, scale=-1.0).then_inc(a_act[pb], 1)

            def end_decays(pb):
                act.wait_ge(we_pe, pb + 1)
                for c in range(NC):
                    act.activation(s.wend[:, :, 2 * pb:2 * pb + 2, c, :],
                                   WE[pb][:, c * P:(c + 1) * P].rearrange("p (q g h) -> p g q h", q=2, g=GP),
                                   ACT.Copy).then_inc(we_ev, 1)

            def weights(n):
                t, hh = n // 2, n % 2
                act.wait_ge(wt_pe, n + 1)
                act.activation(s.w_hi[:, t, 2 * hh:2 * hh + 2, :],
                               WB[hh][:, 0:2 * P].rearrange("p (k r) -> p k r", k=2), ACT.Copy)
                if n >= 2:
                    act.wait_ge(w_pool, n - 1)
                act.activation(wst[:, hh, :], WB[hh][:, 0:2 * P], ACT.Copy).then_inc(w_act, 1)

            for n in range(16):
                make_h(n)
            softplus_inputs(0)
            softplus_inputs(1)
            act.wait_ge(konst, 16)
            for i in range(4):
                act.activation(s.R[:, i // 2, i % 2, :], stage[:, :], ACT.Copy).then_inc(kcopy, 1)
                act.activation(s.Lm[:, i // 2, i % 2, :], lstage[:, :], ACT.Copy).then_inc(kcopy, 1)
            for n in range(2 * NT):
                weights(n)
            decays(0)
            decays(1)
            end_decays(0)
            end_decays(1)
            for n in range(2):
                act.wait_ge(mod_pe, 5 + n)
                act.activation(rabs[:, n, :], GATE[n][0:NB, :], ACT.Abs).then_inc(gate_abs, 1)

        @block.tensor
        def _(pe):
            pe.wait_ge(sc_ready, 1)
            pe.wait_ge(konst, 3)
            for k in range(KC):
                ins = pe.transpose(s.bank[4][:, k * NB:(k + 1) * NB], sc4[:, k * P:(k + 1) * P], s.ident[0:NB, 0:NB])
            ins.then_inc(sct_pe, 1)

            def section(n):
                pe.wait_ge(d_wm[n % 2], 16 * (n // 2 + 1))
                if n >= 2:
                    pe.wait_ge(mod_ready, 2)
                for m in range(KC):
                    for k in range(KC):
                        ins = pe.matmul(MOD[n // 2][:, (n * KC + m) * NB:(n * KC + m + 1) * NB],
                                        wm[:, n % 2, k, m * P:(m + 1) * P], scT[:, k, :],
                                        start=(k == 0), stop=(k == KC - 1))
                ins.then_inc(mod_pe, 1)

            def turn(i):
                b = i // 4
                pe.wait_ge(ln_n, i + 1)
                if i == 4:
                    pe.wait_ge(mod_ready, 2)
                    pe.wait_ge(wa_dve, 1)
                if b >= 2 and i % 4 == 0:
                    pe.wait_ge(h_act, 4 * (b - 1))
                for k in range(KC):
                    ins = pe.transpose(s.bank[4 * (b % 2) + k][:, (i % 4) * P:(i % 4 + 1) * P], xn[:, i % 2, k * P:(k + 1) * P],
                                       s.ident[:, :])
                ins.then_inc(t_pe, 1)

            def dt_inputs(pb):
                pe.wait_ge(wa_dve, 1)
                for i in range(2):
                    pe.wait_ge(h_lo[i], 4 * pb + 4)
                n = 0
                for q in range(2):
                    b, w = 2 * pb + q, slice(64 - 64 * q, 192 - 64 * q)
                    for k in range(KC):
                        for wt, h in ((wa_hi, s.h_hi), (wa_hi, s.h_lo), (wa_lo, s.h_hi)):
                            ins = pe.matmul(DTB[pb][:, :], wt[:, k, w], h[:, b, k, :],
                                            start=(n == 0), stop=(n == 23))
                            n += 1
                ins.then_inc(a_pe, 1)

            def end_decays(pb):
                pe.wait_ge(a_act[pb], B_WE)
                for c in range(NC):
                    ins = pe.transpose(WE[pb][:, c * P:(c + 1) * P], TMP[:, pb, c * P:(c + 1) * P], s.ident[:, :])
                ins.then_inc(we_pe, 1)

            pe.wait_ge(sct_ready, 1)
            section(0)
            section(1)
            pe.wait_ge(d_wa, 16)
            for k in range(KC):
                ins = pe.transpose(s.bank[5][:, k * NH:(k + 1) * NH], wa_raw[:, k * P:(k + 1) * P],
                                   s.ident[0:NH, 0:NH])
            ins.then_inc(wa_pe, 1)
            for i in range(4):
                turn(i)
            for i in range(4, 16):
                turn(i)
            pe.wait_ge(h_act, 12)
            dt_inputs(0)
            dt_inputs(1)
            section(2)
            section(3)
            pe.wait_ge(h_act, 16)
            for n in range(2 * NT):
                t, hh = n // 2, n % 2
                pe.wait_ge(d_w[t % 2], 16 * (t // 2 + 1))
                if n >= 2:
                    pe.wait_ge(w_act, n - 1)
                for k in range(2):
                    ins = pe.transpose(WB[hh][:, k * P:(k + 1) * P],
                                       wraw[:, t % 2, (2 * hh + k) * P:(2 * hh + k + 1) * P], s.ident[:, :])
                ins.then_inc(wt_pe, 1)
            for n in range(2):
                pe.wait_ge(d_wm[n], 48)
                for k in range(KC):
                    ins = pe.matmul(GATE[n][0:NB, :], scT[:, k, :], wm[:, n, k, :],
                                    start=(k == 0), stop=(k == KC - 1))
                ins.then_inc(mod_pe, 1)
            for pb in range(2):
                end_decays(pb)


def halves_before(b, k):
    return sum(slot < 16 * (b - 2) + k for slot in W_SLOT)


def main_part(nc, s, x, w_in, w_out, w_ffn):
    with ExitStack() as ctx:
        def sb(name, shape, dt=F32):
            return ctx.enter_context(nc.sbuf_tensor("m_" + name, shape, dt))

        def sem(name):
            return ctx.enter_context(nc.semaphore("m_" + name))

        wraw = sb("wraw", [P, 2, D])
        wst = sb("wst", [P, 2, 2 * P])
        gcs = sb("gcs", [P, 22])
        cd = sb("cd", [P, GP, HG, NB * NC])
        cv, th = sb("cv", [P, 2, L]), sb("th", [P, 2, L])
        xs, gate = sb("xs", [P, 2, 2, L]), sb("gate", [P, 2, 2, L])
        Bt = sb("Bt", [P, 2, L])
        Ct = sb("Ct", [P, 2, 2, L])
        ea, dd = sb("ea", [P, 2, 2, L]), sb("dd", [P, 2, 2, L])
        E, M = sb("E", [P, 4, 4 * Q]), sb("M", [P, 4, 4 * Q])
        Gm = sb("Gm", [P, 2, Q])
        Xp = sb("Xp", [P, 2, 2 * HG, 32])
        Xw = sb("Xw", [P, 2, HG * HD])
        BTs = sb("BTs", [P, P])
        S, S1 = sb("S", [P, HG * HD]), sb("S1", [P, HG * HD])
        y1 = sb("y1", [P, 2, 2, L])
        t1 = sb("t1", [P, 2, L])
        A, DB, YB, GB, SB = s.bank[0:2], s.bank[2:4], s.bank[4:6], s.bank[6], s.bank[7]

        cd_ready, zeroed, gcs_ready = sem("cd_ready"), sem("zeroed"), sem("gcs_ready")
        rl_ready, eb_ready, wraw_ready = ([sem(f"{n}{i}") for i in range(2)] for n in ("rl_ready", "eb_ready", "wraw_ready"))
        in_done, lin_done, tap_done, conv_done, tanh_done, silu_done = (
            sem(n) for n in ("in_done", "lin_done", "tap_done", "conv_done", "tanh_done", "silu_done"))
        d_done, exp_done, prep_done, gm_done, m_done, yd_done = (
            sem(n) for n in ("d_done", "exp_done", "prep_done", "gm_done", "m_done", "yd_done"))
        bt_done, bt_read, xp_done, xw_done, st_done, s_part, s_new, yo_done = (
            sem(n) for n in ("bt_done", "bt_read", "xp_done", "xw_done", "st_done", "s_part", "s_new", "yo_done"))
        yo_scaled, y1_done, t1_done, t2_done, y_out, y_stored = (
            sem(n) for n in ("yo_scaled", "y1_done", "t1_done", "t2_done", "y_out", "y_stored"))
        w_pe, w_copied, w_hi_done, w_lo_done = sem("w_pe"), sem("w_copied"), sem("w_hi_done"), sem("w_lo_done")
        NOUT, NW, TAIL_SLOT = 8, 12, 4
        raw_out = s.yt
        raw_lin = [s.raw_lin[:, r, :, :] for r in range(4)]
        sgt = s.w_place[:, 0, :, :]
        raw_ready, tw_pe, tw_act, tw_half, tw_dve, al_pe, al_done = (
            [sem(f"raw_ready{i}") for i in range(8)], sem("tw_pe"), sem("tw_act"), sem("tw_half"), sem("tw_dve"), sem("al_pe"), sem("al_done"))
        ones_ready = sem("ones_ready")
        FIN = Step(GP - 1, 3)
        block = ctx.enter_context(nc.Block())

        def run(eng, step):
            for b in range(4):
                step(Step(0, b))
            with eng.Fori(1, GP - 1) as gp:
                for b in range(4):
                    step(Step(gp, b))
            for b in range(4):
                step(Step(GP - 1, b))

        def last(st):
            return isinstance(st.gp, int) and st.gp == GP - 1

        def ahead(st):
            return not (last(st) and st.b == 3)

        def nxt(st, c, by=1):
            return (st, c + by) if c + by < NC else (st.next(), c + by - NC)

        def tok(c):
            return slice(c * Q, (c + 1) * Q)

        @block.sync
        def _(sp):
            a_v = s.a_d.rearrange("r (b g n) t -> r b g n t", b=NB, g=GP)
            na_v = s.na_d.rearrange("r (b g q h) t -> r b g q h t", b=NB, g=GP, q=2)
            ea_v = s.ea_d.rearrange("(b g q h) t -> b g q h t", b=NB, g=GP, q=2)
            dd_v = s.dd_d.rearrange("(b g q h) t -> b g q h t", b=NB, g=GP, q=2)
            y_v = s.y_d.rearrange("(g q p) t -> g p q t", q=2, p=P)
            cd_v = s.cd_d.rearrange("(g q h) n -> q g h n", g=GP, q=2)

            def load_decays(st, c):
                sp.dma_start(s.R[R_POS:R_ALL, c % 2, :, :].bitcast(F32).rearrange("r q (h s) -> r (q h) s", s=Q),
                             a_v[:, st.b, st.gp, :, tok(c)]).then_inc(rl_ready[c % 2], 16)
                for r in range(2):
                    sp.dma_start(s.Lm[R_NEG + r * HG:R_NEG + (r + 1) * HG, c % 2, :, :].bitcast(F32),
                                 na_v[r, st.b, st.gp, :, :, tok(c)].rearrange("q h t -> h q t"))\
                      .then_inc(rl_ready[c % 2], 16)

            def load_scales(st):
                for q in range(2):
                    for dst, src in ((ea, ea_v), (dd, dd_v)):
                        for_heads = src[st.b, st.gp, q].unsqueeze(1).broadcast_to([HG, HD, L])
                        sp.dma_start(dst[:, st.par, q, :], for_heads).then_inc(eb_ready[st.par], 16)

            def load_weights(gp, t):
                for_pair = w_rows(gp, t)
                sp.dma_start(wraw[:, t % 2, :], for_pair).then_inc(wraw_ready[t % 2], 16)

            w_x = w_in[0:DI, :].rearrange("(g q p) d -> g q p d", q=2, p=P)
            w_bc = w_in[DI:2 * DI, :].rearrange("(o g p) d -> o g p d", o=2, p=P)
            w_z = w_in[2 * DI:3 * DI, :].rearrange("(g q p) d -> g q p d", q=2, p=P)

            def w_rows(gp, t):
                return w_x[gp, t] if t < 2 else w_bc[t - 2, gp] if t < 4 else w_z[gp, t - 4]

            def step(st):
                for c in range(NC):
                    j4 = st.n(16, 4 * c)
                    st2, c2 = nxt(st, c, 2)
                    if ahead(st) or c < 2:
                        sp.wait_ge(d_done, j4 + 4)
                        load_decays(st2, c2)
                    if c == 1:
                        if not (isinstance(st.gp, int) and st.gp == 0 and st.b == 0):
                            store(st.prev())
                        if ahead(st):
                            load_scales(st.next())
                    if last(st) and st.b == 3 and c < 2:
                        sp.wait_ge(in_done, FIN.n(6, 6))
                        for r in range(4):
                            if c == 0:
                                dst, src = raw_out[r].rearrange("p a n -> p (a n)"), w_out[r * P:(r + 1) * P, :]
                            else:
                                dst, src = raw_lin[r].rearrange("p k n -> p (k n)"), w_ffn[r * P:(r + 1) * P, :]
                            sp.dma_start(dst, src).then_inc(raw_ready[4 * c + r], 16)
                    if last(st) and st.b == 3 and c == 3:
                        for t in range(4):
                            load_tail_x(nc, s, sp, x, 0, t)
                        sp.wait_ge(tw_pe, NOUT)
                        sp.wait_ge(y_stored, 16 * 4 * (GP - 1) + 16)
                        for t in range(4):
                            load_tail_y(nc, s, sp, 0, t)
                    if not last(st):
                        if st.b == 1 and c == 2:
                            wait(sp, w_pe, st.gp * 12)
                            load_weights(st.gp + 1, 0)
                            load_weights(st.gp + 1, 1)
                        if (st.b, c) in ((2, 2), (2, 3), (3, 0), (3, 1)):
                            t = 4 * (st.b - 2) + c
                            sp.wait_ge(w_pe, st.gp * 12 + (2 * t - 2))
                            load_weights(st.gp + 1, t)

            def store(st):
                sp.wait_ge(y_out, st.n(1, 1))
                sp.dma_start(y_v[st.gp][:, :, st.b * L:(st.b + 1) * L], t1[:, :, :]).then_inc(y_stored, 16)

            for q in range(2):
                sp.dma_start(cd[64 * q:64 * q + 64, :, :, :],
                             cd_v[q].unsqueeze(0).broadcast_to([NS, GP, HG, NB * NC])).then_inc(cd_ready, 16)
            load_decays(Step(0, 0), 0)
            load_decays(Step(0, 0), 1)
            load_scales(Step(0, 0))
            run(sp, step)
            store(Step(GP - 1, 3))
            sp.wait_ge(y_stored, 16 * 4 * GP)

        @block.tensor
        def _(pe):
            def project(st, m):
                t, part = m // 3, m % 3
                if part == 0:
                    if st.b == 0 and not (isinstance(st.gp, int) and st.gp == 0):
                        pe.wait_ge(w_lo_done, st.gp * 12 + (2 * t + 2 - 12))
                    if t < 2:
                        wait(pe, lin_done, st.n(6, t - 1))
                    else:
                        pe.wait_ge(conv_done, st.n(4, t - 1))
                for n in range(4 * part, 4 * part + 4):
                    k, w, h = n // 3, (s.w_hi, s.w_hi, s.w_lo)[n % 3], (s.h_hi, s.h_lo, s.h_hi)[n % 3]
                    ins = pe.matmul(A[t % 2][:, :], w[:, t, k, :], h[:, st.b, k, :], start=(n == 0), stop=(n == 11))
                if part == 2:
                    ins.then_inc(in_done, 1)

            def decays(st, c, sl):
                q, hh = sl // 2, sl % 2
                if sl == 0:
                    pe.wait_ge(rl_ready[c % 2], st.n(2 * 48, (c // 2 + 1) * 48))
                wait(pe, exp_done, st.n(16, 4 * c + sl - 1))
                pe.matmul(DB[sl % 2][:, :], s.Lm[:, c % 2, q, :], s.R[:, c % 2, q, hh * 512:(hh + 1) * 512],
                          start=True, stop=True).then_inc(d_done, 1)

            def prepare(st, c):
                if c == 0:
                    pe.wait_ge(silu_done, st.n(6, 4))
                wait(pe, gm_done, st.n(4, c))
                for q in range(2):
                    pe.transpose(GB[:, q * P:(q + 1) * P], xs[:, st.par, q, tok(c)], s.ident[:, :])
                pe.matmul(GB[:, 256:512], Bt[:, st.par, tok(c)], Ct[:, st.par, :, tok(c)],
                          start=True, stop=True).then_inc(prep_done, 1)

            def turn_b(st, c):
                wait(pe, s_new, st.n(3, c))
                pe.transpose(SB[:, 0:P], Bt[:, st.par, tok(c)], s.ident[:, :]).then_inc(bt_done, 1)

            def weights(gp, n):
                t, hh = n // 2, n % 2
                if hh == 0:
                    pe.wait_ge(wraw_ready[t % 2], gp * 48 + 16 * (t // 2 + 1))
                for k in range(2):
                    ins = pe.transpose(SB[:, 256 + k * P:256 + (k + 1) * P],
                                       wraw[:, t % 2, (2 * hh + k) * P:(2 * hh + k + 1) * P], s.ident[:, :])
                ins.then_inc(w_pe, 1)

            def tail_weights(n):
                r, hh = (n // 2, n % 2) if n < NOUT else (n - NOUT, 0)
                pe.wait_ge(raw_ready[r if n < NOUT else 4 + r], 16)
                if n < 2:
                    pe.wait_ge(lin_done, FIN.n(6, 6))
                else:
                    pe.wait_ge(tw_dve, n - 1)
                for k in range(4):
                    src = raw_out[r][:, hh, k * P:(k + 1) * P] if n < NOUT else raw_lin[r][:, k, :]
                    ins = pe.transpose(A[n % 2][:, k * P:(k + 1) * P], src, s.ident[:, :])
                ins.then_inc(tw_pe, 1)

            def step(st):
                nx = st.next()
                for k in range(16):
                    c, sl = k // 4, k % 4
                    stn, cn = nxt(st, c)
                    if sl == 0:
                        wait(pe, y1_done, st.n(4, c - 1))
                    if sl == 0 and c > 0:
                        pe.wait_ge(s_new, st.n(3, c))
                        pe.matmul(YB[c % 2][:, 256:512], S[:, :], Ct[:, st.par, :, tok(c)],
                                  start=True, stop=True).then_inc(yo_done, 1)
                    if ahead(st) or c < 3:
                        decays(stn, cn, sl)
                    pe.wait_ge(m_done, st.n(16, 4 * c + sl + 1))
                    if sl == 0:
                        pe.wait_ge(xp_done, st.n(4, c + 1))
                    q = sl // 2
                    for hh in range(4):
                        h = 4 * (sl % 2) + hh
                        j = h // 2
                        ins = pe.matmul(YB[c % 2][32 * j:32 * j + 32, q * Q:(q + 1) * Q], Xp[:, c % 2, q * HG + h, :],
                                        M[:, sl, hh * Q:(hh + 1) * Q], start=(h % 2 == 0), stop=(h % 2 == 1))
                    ins.then_inc(yd_done, 1)
                    if ahead(st):
                        for m in GROUPS[k]:
                            project(nx, m)
                    elif k >= TAIL_SLOT:
                        tail_weights(k - TAIL_SLOT)
                    if sl == 0 and c < 3:
                        pe.wait_ge(xw_done, st.n(3, c + 1))
                        pe.wait_ge(bt_read, st.n(3, c + 1))
                        if halves_before(st.b, k) and not last(st):
                            pe.wait_ge(w_copied, st.gp * 12 + halves_before(st.b, k))
                        for q in range(2):
                            ins = pe.matmul(SB[64 * q:64 * q + 64, P:2 * P], BTs[:, 64 * q:64 * q + 64], Xw[:, q, :],
                                            start=True, stop=True)
                        ins.then_inc(st_done, 1)
                    if sl == PREP and (ahead(st) or c < 3):
                        prepare(stn, cn)
                    if sl == PREP + 1 and cn < 3 and (ahead(st) or c < 3):
                        if halves_before(st.b, k) and not last(st):
                            pe.wait_ge(w_copied, st.gp * 12 + halves_before(st.b, k))
                        turn_b(stn, cn)
                    n = halves_before(st.b, k)
                    if halves_before(st.b, k + 1) > n and not last(st):
                        pe.wait_ge(bt_read, st.n(3, bt_count(c, sl)))
                        wait(pe, s_new, st.n(3, min(c + 1, 3)))
                        wait(pe, w_copied, st.gp * 12 + n)
                        weights(st.gp, n)

            def bt_count(c, sl):
                own = min(c + 1, 3) if sl <= PREP else min(c + 2, 3)
                return 4 if c == 3 and sl > PREP else own

            for m in range(18):
                project(Step(0, 0), m)
            for sl in range(4):
                decays(Step(0, 0), 0, sl)
            prepare(Step(0, 0), 0)
            turn_b(Step(0, 0), 0)
            run(pe, step)
            pe.wait_ge(ones_ready, 1)
            pe.wait_ge(tw_act, NW)
            pe.wait_ge(tw_dve, NW)
            for k in range(KC):
                ins = pe.matmul(A[0][:, :], s.ones[:, :], s.absw[:, k, :], start=(k == 0), stop=(k == KC - 1))
            ins.then_inc(al_pe, 1)

        @block.scalar
        def _(act):
            def linear(st, t):
                act.wait_ge(in_done, st.n(6, t + 1))
                wait(act, silu_done, st.n(6, t - 1))
                act.wait_ge(gcs_ready, st.gp + 1)
                o = t * (KS + 1)
                scale, bias = (gcs[:, o + KS - 1:o + KS], gcs[:, o + KS:o + KS + 1]) if t < 4 else (1.0, gcs[:, 16 + t:17 + t])
                act.activation(cv[:, t % 2, :], A[t % 2][:, :], ACT.Identity, scale=scale, bias=bias).then_inc(lin_done, 1)

            def tanh(st, t):
                if t < 4:
                    act.wait_ge(conv_done, st.n(4, t + 1))
                else:
                    act.wait_ge(lin_done, st.n(6, t + 1))
                act.activation(th[:, t % 2, :], cv[:, t % 2, :], ACT.Tanh, scale=0.5).then_inc(tanh_done, 1)

            def exponent(st, c, sl):
                act.wait_ge(d_done, st.n(16, 4 * c + sl + 1))
                wait(act, m_done, st.n(16, 4 * c + sl - 3))
                act.activation(E[:, sl, :], DB[sl % 2][:, :], ACT.Exp).then_inc(exp_done, 1)

            def spread(st, c):
                act.wait_ge(prep_done, st.n(4, c + 1))
                wait(act, yd_done, st.n(16, 4 * (c - 1)))
                wait(act, xw_done, st.n(3, c - 1) if c else st.n(3, 0))
                out = Xp[:, c % 2, :, :].rearrange("p (j e) (m d) -> p j (e m) d", e=2, d=HD)[:, :, 0:4:3, :]
                act.activation(out, GB[:, 0:256].rearrange("p (j e d) -> p j e d", e=2, d=HD), ACT.Copy)\
                   .then_inc(xp_done, 1)

            def copy_b(st, c):
                act.wait_ge(bt_done, st.n(3, c + 1))
                wait(act, st_done, st.n(3, c))
                act.activation(BTs[:, :], SB[:, 0:P], ACT.Copy).then_inc(bt_read, 1)

            def step(st):
                nx = st.next()
                for k in range(16):
                    c, sl = k // 4, k % 4
                    stn, cn = nxt(st, c)
                    if ahead(st) or c < 3:
                        exponent(stn, cn, sl)
                    for t in range(NT):
                        if FS[t] + 1 == k and ahead(st):
                            tanh(nx, t)
                        if FS[t] + 1 == k + 16 and not first(st):
                            tanh(st, t)
                    for t in range(NT):
                        if FS[t] == k and ahead(st):
                            linear(nx, t)
                    if sl == PREP and (ahead(st) or c < 3):
                        spread(stn, cn)
                    if sl == PREP + 1 and cn < 3 and (ahead(st) or c < 3):
                        copy_b(stn, cn)
                    if not ahead(st) and k >= TAIL_SLOT:
                        tail_weights(k - TAIL_SLOT)
                    n = halves_before(st.b, k)
                    if halves_before(st.b, k + 1) > n and not last(st):
                        act.wait_ge(w_pe, st.gp * 12 + n + 1)
                        wait(act, w_lo_done, st.gp * 12 + n - 1)
                        act.activation(s.w_hi[:, n // 2, 2 * (n % 2):2 * (n % 2) + 2, :],
                                       SB[:, 256:512].rearrange("p (k r) -> p k r", k=2), ACT.Copy).then_inc(w_hi_done, 1)
                        act.activation(wst[:, n % 2, :], SB[:, 256:512], ACT.Copy).then_inc(w_copied, 1)

            def tail_weights(n):
                act.wait_ge(tw_pe, n + 1)
                src = A[n % 2][:, :].rearrange("p (k e) -> p k e", k=4)
                if n < NOUT:
                    r, hh = n // 2, n % 2
                    act.activation(s.h_hi[:, hh, :, r * P:(r + 1) * P], src, ACT.Copy).then_inc(tw_act, 1)
                else:
                    r = n - NOUT
                    act.activation(s.absw[:, :, r * P:(r + 1) * P], src, ACT.Abs).then_inc(tw_act, 1)

            def first(st):
                return isinstance(st.gp, int) and st.gp == 0 and st.b == 0

            for t in range(NT):
                linear(Step(0, 0), t)
                tanh(Step(0, 0), t)
            act.wait_ge(zeroed, 1)
            for sl in range(4):
                exponent(Step(0, 0), 0, sl)
            spread(Step(0, 0), 0)
            copy_b(Step(0, 0), 0)
            run(act, step)

        @block.vector
        def _(dve):
            def convolve(st, t):
                dve.wait_ge(lin_done, st.n(6, t + 1))
                for k in range(KS - 2, -1, -1):
                    lag, o = KS - 1 - k, t * (KS + 1) + k
                    if lag > 1:
                        dve.wait_ge(tap_done, st.n(8, 2 * t + lag - 1))
                    ins = dve.scalar_tensor_tensor(out=cv[:, t % 2, lag:], in0=A[t % 2][:, 0:L - lag],
                                                   scalar=gcs[:, o:o + 1], in1=cv[:, t % 2, lag:],
                                                   op0=ALU.mult, op1=ALU.add)
                    ins.then_inc(conv_done if k == 0 else tap_done, 1)

            def silu(st, t):
                dve.wait_ge(tanh_done, st.n(6, t + 1))
                if t == 0:
                    wait(dve, y_out, st.n(1, -1))
                if t == 3:
                    for q in range(2):
                        n = slice(64 * q, 64 * q + 64)
                        ins = dve.scalar_tensor_tensor(out=Ct[n, st.par, q, :], in0=th[n, 1, :], scalar=1.0,
                                                       in1=cv[n, 1, :], op0=ALU.add, op1=ALU.mult)
                    ins.then_inc(silu_done, 1)
                    return
                dst = (xs[:, st.par, 0, :], xs[:, st.par, 1, :], Bt[:, st.par, :], None,
                       gate[:, st.par, 0, :], gate[:, st.par, 1, :])[t]
                dve.scalar_tensor_tensor(out=dst, in0=th[:, t % 2, :], scalar=1.0, in1=cv[:, t % 2, :],
                                         op0=ALU.add, op1=ALU.mult).then_inc(silu_done, 1)

            def causal(st, c):
                dve.wait_ge(xp_done, st.n(4, c + 1))
                wait(dve, m_done, st.n(16, 4 * c))
                dve.tensor_tensor(Gm[:, :, :], GB[:, 256:512].rearrange("p (q s) -> p q s", q=2),
                                  s.tri[:, :].unsqueeze(1).broadcast_to([P, 2, Q]), ALU.mult).then_inc(gm_done, 1)

            def mix(st, c, sl):
                dve.wait_ge(exp_done, st.n(16, 4 * c + sl + 1))
                dve.wait_ge(gm_done, st.n(4, c + 1))
                wait(dve, yd_done, st.n(16, 4 * c + sl - 3))
                dve.tensor_tensor(M[:, sl, :].rearrange("p (h s) -> p h s", h=4),
                                  E[:, sl, :].rearrange("p (h s) -> p h s", h=4),
                                  Gm[:, sl // 2, :].unsqueeze(1).broadcast_to([P, 4, Q]), ALU.mult).then_inc(m_done, 1)

            def collect(st, c):
                dve.wait_ge(yd_done, st.n(16, 4 * c + 4))
                own = YB[c % 2][:, 0:256].rearrange("p (q s) -> p q s", q=2)
                if c == 0:
                    wait(dve, y_out, st.n(1, -1))
                    dve.tensor_copy(y1[:, st.par, :, tok(c)], own).then_inc(y1_done, 1)
                    return
                dve.wait_ge(yo_done, st.n(3, c))
                dve.wait_ge(eb_ready[st.par], st_eb(st))
                dve.tensor_tensor(y1[:, st.par, :, tok(c)], YB[c % 2][:, 256:512].rearrange("p (q s) -> p q s", q=2),
                                  ea[:, st.par, :, tok(c)], ALU.mult).then_inc(yo_scaled, 1)
                dve.wait_ge(yo_scaled, st.n(3, c))
                dve.tensor_tensor(y1[:, st.par, :, tok(c)], own, y1[:, st.par, :, tok(c)], ALU.add).then_inc(y1_done, 1)

            def update(st, c):
                dve.wait_ge(st_done, st.n(3, c + 1))
                if c == 0:
                    wait(dve, yo_done, st.n(3, 0))
                    dve.tensor_copy(S[:, :], SB[:, P:2 * P]).then_inc(s_new, 1)
                    return
                dve.wait_ge(s_new, st.n(3, c))
                dve.tensor_tensor(S1[:, :].rearrange("p (h d) -> p h d", h=HG), S[:, :].rearrange("p (h d) -> p h d", h=HG),
                                  cd[:, st.gp, :, st.b * NC + c].unsqueeze(2).broadcast_to([P, HG, HD]),
                                  ALU.mult).then_inc(s_part, 1)
                dve.wait_ge(s_part, st.n(2, c))
                dve.wait_ge(yo_done, st.n(3, c))
                dve.tensor_tensor(S[:, :], S1[:, :], SB[:, P:2 * P], ALU.add).then_inc(s_new, 1)

            def step(st):
                nx = st.next()
                for k in range(16):
                    c, sl = k // 4, k % 4
                    stn, cn = nxt(st, c)
                    more = ahead(st) or c < 3
                    if sl == 0 and not (first(st) and c == 0):
                        collect(st, c - 1) if c else collect(st.prev(), 3)
                    if sl == 0 and c < 3:
                        update(st, c)
                    if sl == PREP + 1 and more:
                        causal(stn, cn)
                        mix(stn, cn, 0)
                        mix(stn, cn, 1)
                    if sl == PREP + 2 and more:
                        mix(stn, cn, 2)
                        mix(stn, cn, 3)
                    for t in range(NT):
                        if FS[t] + 2 == k and ahead(st):
                            silu(nx, t)
                        if FS[t] + 2 == k + 16 and not first(st):
                            silu(st, t)
                    for t in range(4):
                        if FS[t] == k and ahead(st):
                            convolve(nx, t)
                    if not ahead(st) and k >= TAIL_SLOT:
                        tail_weights(k - TAIL_SLOT)

            def first(st):
                return isinstance(st.gp, int) and st.gp == 0 and st.b == 0

            def tail_weights(n):
                dve.wait_ge(tw_act, n + 1)
                if n < NOUT:
                    r, hh = n // 2, n % 2
                    dve.tensor_tensor(s.h_hi[:, 2 + hh, :, r * P:(r + 1) * P],
                                      A[n % 2][:, :].rearrange("p (k e) -> p k e", k=4),
                                      s.h_hi[:, hh, :, r * P:(r + 1) * P].bitcast(F32), ALU.subtract).then_inc(tw_dve, 1)
                    return
                r = n - NOUT
                if r:
                    dve.wait_ge(tw_dve, n)
                dve.tensor_scalar(sgt, A[n % 2][:, :].rearrange("p (k e) -> p k e", k=4), 0.0, 2.0,
                                  ALU.is_ge, ALU.mult).then_inc(tw_half, 1)
                dve.wait_ge(tw_half, r + 1)
                dve.tensor_scalar(s.sign[:, :, r * P:(r + 1) * P], sgt, -1.0, None, ALU.add).then_inc(tw_dve, 1)

            def st_eb(st):
                return st.gp * 128 + 64 * (st.b // 2 + 1)

            dve.memset(Ct[:, :, :, :], 0.0)
            dve.memset(Xp[:, :, :, :], 0.0).then_inc(zeroed, 1)
            dve.wait_ge(zeroed, 1)
            dve.wait_ge(gcs_ready, 1)
            for t in range(NT):
                if t < 4:
                    convolve(Step(0, 0), t)
                silu(Step(0, 0), t)
            dve.wait_ge(cd_ready, 32)
            causal(Step(0, 0), 0)
            for sl in range(4):
                mix(Step(0, 0), 0, sl)
            run(dve, step)
            collect(FIN, 3)
            dve.wait_ge(y1_done, FIN.n(4, 4))
            dve.wait_ge(t1_done, FIN.n(1, 1))
            dve.tensor_tensor(t1[:, :, :], t1[:, :, :], y1[:, FIN.par, :, :], ALU.add).then_inc(t2_done, 1)
            dve.wait_ge(t2_done, FIN.n(1, 1))
            dve.wait_ge(silu_done, FIN.n(6, 6))
            dve.tensor_tensor(t1[:, :, :], t1[:, :, :], gate[:, FIN.par, :, :], ALU.mult).then_inc(y_out, 1)
            dve.wait_ge(al_pe, 1)
            dve.tensor_scalar(s.alpha, A[0][:, :], 1.0 / D, None, ALU.mult).then_inc(al_done, 1)

        @block.gpsimd
        def _(pool):
            def constants(gp):
                pool.tensor_copy(gcs[:, :], s.gpc[:, gp, :]).then_inc(gcs_ready, 1)

            def weigh(st, c):
                pool.wait_ge(xp_done, st.n(4, c + 1))
                wait(pool, st_done, st.n(3, c))
                src = Xp[:, c % 2, :, :].rearrange("p (j e) (m d) -> p j (e m) d", e=2, d=HD)[:, :, 0:4:3, :]
                w = s.wend[:, st.gp, st.b, c, :].rearrange("p (j e) -> p j e", e=2).unsqueeze(3).broadcast_to([P, HG, 2, HD])
                pool.tensor_tensor(Xw[:, :, :].rearrange("p q (j e d) -> p (q j) e d", e=2, d=HD), src, w,
                                   ALU.mult).then_inc(xw_done, 1)

            def skip(st):
                pool.wait_ge(silu_done, st.n(6, 2))
                pool.wait_ge(eb_ready[st.par], st.gp * 128 + 64 * (st.b // 2 + 1))
                wait(pool, y_stored, st.n(16, 0))
                pool.tensor_tensor(t1[:, :, :], xs[:, st.par, :, :], dd[:, st.par, :, :], ALU.mult).then_inc(t1_done, 1)

            def finish(st):
                pool.wait_ge(y1_done, st.n(4, 4))
                pool.wait_ge(t1_done, st.n(1, 1))
                pool.tensor_tensor(t1[:, :, :], t1[:, :, :], y1[:, st.par, :, :], ALU.add).then_inc(t2_done, 1)
                pool.wait_ge(t2_done, st.n(1, 1))
                pool.wait_ge(silu_done, st.n(6, 6))
                pool.tensor_tensor(t1[:, :, :], t1[:, :, :], gate[:, st.par, :, :], ALU.mult).then_inc(y_out, 1)

            def split(gp, n):
                w = slice(2 * (n % 2), 2 * (n % 2) + 2)
                src = wst[:, n % 2, :].rearrange("p (k r) -> p k r", k=2)
                pool.wait_ge(w_copied, gp * 12 + n + 1)
                pool.tensor_tensor(s.w_lo[:, n // 2, w, :], src, s.w_hi[:, n // 2, w, :].bitcast(F32),
                                   ALU.subtract).then_inc(w_lo_done, 1)

            def step(st):
                for c in range(NC):
                    if c == 0:
                        if st.b == 3 and not last(st):
                            pool.wait_ge(lin_done, st.n(6, 6))
                            pool.wait_ge(conv_done, st.n(4, 4))
                            constants(st.gp + 1)
                        if not (isinstance(st.gp, int) and st.gp == 0 and st.b == 0):
                            finish(st.prev())
                    stn, cn = nxt(st, c)
                    if cn < 3 and (ahead(st) or c < 3):
                        weigh(stn, cn)
                    if c == 2:
                        skip(st)
                    if not last(st):
                        for n in range(halves_before(st.b, 4 * c), halves_before(st.b, 4 * c + 4)):
                            split(st.gp, n)

            pool.memset(s.ones[:, :], 1.0).then_inc(ones_ready, 1)
            constants(0)
            weigh(Step(0, 0), 0)
            run(pool, step)


def load_tail_y(nc, s, sp, b, t):
    y_v = s.y_d.rearrange("(k p) (b t n) -> b t p k n", p=P, b=NB, t=L // P)
    sp.dma_start(s.yt[t].rearrange("p a (k n) -> p (a k) n", n=P), y_v[b, t]).then_inc(s.d_y[t], 16)


def load_tail_x(nc, s, sp, x, b, t):
    x_v = x.rearrange("b (t p) d -> b t p d", p=P)
    sp.dma_start(s.xt[t], x_v[b, t]).then_inc(s.d_x[t], 16)


def tail_part(nc, s, x, b_ffn, out):
    with ExitStack() as ctx:
        def sb(name, shape, dt=F32):
            return ctx.enter_context(nc.sbuf_tensor("t_" + name, shape, dt))

        def sem(name):
            return ctx.enter_context(nc.semaphore("t_" + name))

        KI, TT = DI // P, L // P
        half, eps = sb("half", [P, 1]), sb("eps", [P, 1])
        bias = sb("bias", [P, D])
        ga, gb = sb("ga", [P, NB, D]), sb("gb", [P, NB, D])
        gsc, gbias = sb("gsc", [P, NB, D]), sb("gbias", [P, NB, D])
        y_hi, y_lo = sb("y_hi", [P, 2, KI, P], F32R), sb("y_lo", [P, 2, KI, P], F32R)
        x2 = sb("x2", [P, TT, D])
        att, xn = sb("att", [P, 2, D]), sb("xn", [P, 2, D])
        st_, mv, rstd = sb("st", [P, 2, 6]), sb("mv", [P, 2, 2]), sb("rstd", [P, 2, 2])
        hf = sb("hf", [P, 2, KC, P])
        h_hi, h_lo = sb("h_hi", [P, 2, KC, P], F32R), sb("h_lo", [P, 2, KC, P], F32R)
        f1, o = sb("f1", [P, 2, D]), sb("o", [P, 2, D])
        OB, TB, FB = s.bank[0:2], s.bank[2:4], s.bank[4:6]

        d_out = [sem(f"d_out{i}") for i in range(2)]
        d_g, konst = sem("d_g"), sem("konst")
        g_done = sem("g_done")
        yhi_done, ylo_done, op_done = sem("yhi_done"), sem("ylo_done"), sem("op_done")
        gated, x2_done, bn_done, st_done, eps_done, rs_done, xn_done = (
            sem(n) for n in ("gated", "x2_done", "bn_done", "st_done", "eps_done", "rs_done", "xn_done"))
        tr_done, hf_done, hhi_done, hlo_done, ffn_done, f1_done, res_done, o_done = (
            sem(n) for n in ("tr_done", "hf_done", "hhi_done", "hlo_done", "ffn_done", "f1_done", "res_done", "o_done"))
        block = ctx.enter_context(nc.Block())

        def run(eng, step):
            for t in range(TT):
                step(Step(0, t))
            with eng.Fori(1, NB - 1) as b:
                for t in range(TT):
                    step(Step(b, t))
            for t in range(TT):
                step(Step(NB - 1, t))

        def is_last(st):
            return isinstance(st.gp, int) and st.gp == NB - 1 and st.b == TT - 1

        def yt_v(t):
            return s.yt[t].rearrange("p a (k n) -> p (a k) n", n=P)

        def gates_of(st):
            return 2 if isinstance(st.gp, int) and st.gp == 0 else 2 * NB

        def two_more(st):
            return not (isinstance(st.gp, int) and st.gp == NB - 1 and st.b >= TT - 2)

        def two_back(st):
            return not (isinstance(st.gp, int) and st.gp == 0 and st.b < 2)

        def is_first(st):
            return isinstance(st.gp, int) and st.gp == 0 and st.b == 0

        @block.sync
        def _(sp):
            o_v = out.rearrange("b (t p) d -> b t p d", p=P)

            def load(st):
                load_tail_y(nc, s, sp, st.gp, st.b)
                load_tail_x(nc, s, sp, x, st.gp, st.b)

            def store(st):
                sp.wait_ge(o_done, st.n(1, 1))
                sp.dma_start(o_v[st.gp, st.b], o[:, st.b % 2, :]).then_inc(d_out[st.b % 2], 16)

            def step(st):
                if not (isinstance(st.gp, int) and st.gp == NB - 1):
                    sp.wait_ge(ylo_done, st.n(1, 1))
                    sp.wait_ge(x2_done, st.n(1, 1))
                    load(Step(st.gp + 1, st.b))
                if not is_first(st):
                    store(st.prev())

            run(sp, step)
            store(Step(NB - 1, TT - 1))
            for i in range(2):
                sp.wait_ge(d_out[i], 16 * NB * TT // 2)

        @block.scalar
        def _(act):
            for b in range(NB):
                act.dma_start(ga[:, b, :], s.g_d[0, b:b + 1, :].broadcast_to([P, D])).then_inc(d_g, 16)
                act.dma_start(gb[:, b, :], s.g_d[1, b:b + 1, :].broadcast_to([P, D])).then_inc(d_g, 16)
            act.dma_start(bias[:, :], b_ffn.rearrange("(o n) -> o n", o=1).broadcast_to([P, D])).then_inc(d_g, 16)

            def split(st):
                act.wait_ge(s.d_y[st.b], st.gp * 16 + 16)
                wait(act, op_done, st.n(1, -1))
                act.activation(y_hi[:, st.b % 2, :, :], yt_v(st.b), ACT.Copy).then_inc(yhi_done, 1)

            def step(st):
                act.wait_ge(ylo_done, st.n(1, 1))
                if two_more(st):
                    split(st.next().next())
                act.wait_ge(d_g, 16 * 9)
                act.wait_ge(tr_done, st.n(1, 1))
                wait(act, hlo_done, st.n(1, -1))
                for k in range(KC):
                    ins = act.activation(hf[:, st.b % 2, k, :], TB[st.b % 2][:, k * P:(k + 1) * P], ACT.Identity,
                                         scale=s.mod_t[:, 2, k, st.gp].unsqueeze(1), bias=s.mod_t[:, 3, k, st.gp].unsqueeze(1))
                ins.then_inc(hf_done, 1)

            split(Step(0, 0))
            split(Step(0, 1))
            run(act, step)

        @block.gpsimd
        def _(pool):
            pool.memset(half[:, :], -0.5).then_inc(konst, 1)
            pool.memset(eps[:, :], EPS).then_inc(konst, 1)

            def split(st):
                pool.wait_ge(yhi_done, st.n(1, 1))
                pool.tensor_tensor(y_lo[:, st.b % 2, :, :], yt_v(st.b), y_hi[:, st.b % 2, :, :].bitcast(F32),
                                   ALU.subtract).then_inc(ylo_done, 1)

            def scale_gates(b):
                pool.tensor_tensor(gsc[:, b, :], gb[:, b, :], s.alpha, ALU.mult).then_inc(g_done, 1)
                pool.tensor_tensor(gbias[:, b, :], gb[:, b, :], bias[:, :], ALU.mult).then_inc(g_done, 1)

            def step(st):
                pool.wait_ge(st_done, st.n(1, 1))
                pool.tensor_tensor(rstd[:, st.b % 2, 0:1], mv[:, st.b % 2, 1:2], eps[:, :], ALU.add).then_inc(eps_done, 1)
                pool.wait_ge(eps_done, st.n(1, 1))
                pool.tensor_tensor(rstd[:, st.b % 2, 1:2], rstd[:, st.b % 2, 0:1], half[:, :], ALU.pow).then_inc(rs_done, 1)
                if two_more(st):
                    split(st.next().next())
                pool.wait_ge(g_done, gates_of(st))
                pool.wait_ge(x2_done, st.n(1, 1))
                wait(pool, o_done, st.n(1, -1))
                pool.tensor_tensor(f1[:, st.b % 2, :], x2[:, st.b, :], gbias[:, st.gp, :], ALU.add).then_inc(res_done, 1)
                if isinstance(st.gp, int) and st.gp == 0 and st.b < NB - 1:
                    scale_gates(st.b + 1)

            pool.wait_ge(konst, 2)
            split(Step(0, 0))
            split(Step(0, 1))
            pool.wait_ge(d_g, 16 * 9)
            scale_gates(0)
            run(pool, step)

        @block.vector
        def _(dve):
            def residual(st):
                dve.wait_ge(op_done, st.n(1, 1))
                wait(dve, xn_done, st.n(1, -1))
                dve.wait_ge(s.d_x[st.b], st.gp * 16 + 16)
                dve.tensor_tensor(att[:, st.b % 2, :], OB[st.b % 2][:, :], ga[:, st.gp, :], ALU.mult).then_inc(gated, 1)
                dve.wait_ge(gated, st.n(1, 1))
                wait(dve, res_done, st.n(1, -3))
                dve.tensor_tensor(x2[:, st.b, :], att[:, st.b % 2, :], s.xt[st.b], ALU.add).then_inc(x2_done, 1)
                dve.wait_ge(x2_done, st.n(1, 1))
                dve.bn_stats(st_[:, st.b % 2, :], x2[:, st.b, :]).then_inc(bn_done, 1)
                dve.wait_ge(g_done, 2)
                dve.wait_ge(bn_done, st.n(1, 1))
                wait(dve, rs_done, st.n(1, -1))
                dve.bn_aggr(mv[:, st.b % 2, :], st_[:, st.b % 2, :]).then_inc(st_done, 1)

            def normalize(st):
                dve.wait_ge(rs_done, st.n(1, 1))
                wait(dve, tr_done, st.n(1, -1))
                dve.tensor_scalar(xn[:, st.b % 2, :], x2[:, st.b, :], mv[:, st.b % 2, 0:1], rstd[:, st.b % 2, 1:2],
                                  ALU.subtract, ALU.mult).then_inc(xn_done, 1)

            def split(st):
                dve.wait_ge(hf_done, st.n(1, 1))
                wait(dve, ffn_done, st.n(1, -1))
                dve.tensor_copy(h_hi[:, st.b % 2, :, :], hf[:, st.b % 2, :, :]).then_inc(hhi_done, 1)
                dve.wait_ge(hhi_done, st.n(1, 1))
                dve.tensor_tensor(h_lo[:, st.b % 2, :, :], hf[:, st.b % 2, :, :], h_hi[:, st.b % 2, :, :].bitcast(F32),
                                  ALU.subtract).then_inc(hlo_done, 1)

            def finish(st):
                dve.wait_ge(g_done, gates_of(st))
                dve.wait_ge(ffn_done, st.n(1, 1))
                if st.b >= 2:
                    dve.wait_ge(d_out[st.b % 2], st.gp * 32 + 16)
                elif not (isinstance(st.gp, int) and st.gp == 0):
                    dve.wait_ge(d_out[st.b % 2], st.gp * 32)
                dve.tensor_tensor(o[:, st.b % 2, :], FB[st.b % 2][:, :], gsc[:, st.gp, :], ALU.mult).then_inc(f1_done, 1)
                dve.wait_ge(f1_done, st.n(1, 1))
                dve.wait_ge(res_done, st.n(1, 1))
                dve.tensor_tensor(o[:, st.b % 2, :], o[:, st.b % 2, :], f1[:, st.b % 2, :], ALU.add).then_inc(o_done, 1)

            def step(st):
                residual(st)
                if two_back(st):
                    finish(st.prev().prev())
                normalize(st)
                if not is_first(st):
                    split(st.prev())

            dve.wait_ge(d_g, 16 * 9)
            run(dve, step)
            finish(Step(NB - 1, TT - 2))
            split(Step(NB - 1, TT - 1))
            finish(Step(NB - 1, TT - 1))

        @block.tensor
        def _(pe):
            def project(st):
                pe.wait_ge(ylo_done, st.n(1, 1))
                wait(pe, gated, st.n(1, -1))
                i = st.b % 2
                for k in range(KI):
                    for n, (y, w) in enumerate(((y_hi, s.wo_hi), (y_lo, s.wo_hi), (y_hi, s.wo_lo))):
                        ins = pe.matmul(OB[i][:, :], y[:, i, k, :], w[k], start=(k == 0 and n == 0),
                                        stop=(k == KI - 1 and n == 2))
                ins.then_inc(op_done, 1)

            def turn(st):
                i = st.b % 2
                pe.wait_ge(xn_done, st.n(1, 1))
                wait(pe, hf_done, st.n(1, -1))
                for k in range(KC):
                    ins = pe.transpose(TB[i][:, k * P:(k + 1) * P], xn[:, i, k * P:(k + 1) * P], s.ident[:, :])
                ins.then_inc(tr_done, 1)

            def linear(st):
                i = st.b % 2
                pe.wait_ge(hlo_done, st.n(1, 1))
                wait(pe, f1_done, st.n(1, -1))
                for k in range(KC):
                    for n, h in enumerate((h_hi, h_lo)):
                        ins = pe.matmul(FB[i][:, :], h[:, i, k, :], s.sign[:, k, :], start=(k == 0 and n == 0),
                                        stop=(k == KC - 1 and n == 1))
                ins.then_inc(ffn_done, 1)

            def step(st):
                if not is_last(st):
                    project(st.next())
                turn(st)
                if not is_first(st):
                    linear(st.prev())

            project(Step(0, 0))
            run(pe, step)
            linear(Step(NB - 1, TT - 1))


_INS = ['L0_attn_input_', 'L0_attn_in_proj_w', 'L0_attn_conv1d_weight', 'L0_attn_conv1d_bias', 'L0_attn_z_bias',
        'L0_attn_D', 'L0_attn_out_proj_w', 'L0_ffn_weight', 'L0_ffn_bias', 'L0_c', 'L0_wmod']
_OUTS = [((NB, L, D), 'float32')]


def kernel(**inputs):
    import numpy as _np
    import concourse.bacc as _bacc
    from concourse import mybir as _mybir
    from concourse.bass_utils import run_bass_kernel_spmd as _run

    nc = _bacc.Bacc("TRN2", target_bir_lowering=False, num_devices=1)
    arrays, args = {}, {}
    for name in _INS:
        a = _np.ascontiguousarray(inputs[name])
        arrays[f"in_{name}_dram"] = a
        args[name] = nc.dram_tensor(f"in_{name}_dram", a.shape, _mybir.dt.from_np(a.dtype), kind="ExternalInput").ap()
    for i, (shape, dtype) in enumerate(_OUTS):
        dt = _mybir.dt.from_np(_np.dtype(dtype))
        out = nc.dram_tensor(f"out_{i}_dram", shape, dt, kind="ExternalOutput").ap()
    adaln_kernel(nc, args['L0_attn_input_'], args['L0_attn_in_proj_w'], args['L0_attn_conv1d_weight'],
                 args['L0_attn_conv1d_bias'], args['L0_attn_z_bias'], args['L0_attn_D'], args['L0_attn_out_proj_w'],
                 args['L0_ffn_weight'], args['L0_ffn_bias'], args['L0_c'], args['L0_wmod'], out)
    r = _run(nc, [arrays], core_ids=[0])
    got = tuple(r.results[0][f"out_{i}_dram"] for i in range(len(_OUTS)))
    return got[0]
```
